# Optimizing a Trainium2 kernel written in Bass

```python
import numpy as np
import jax
import jax.numpy as jnp

def _softmax(x, axis=-1):
    return jax.nn.softmax(x, axis=axis)

def _gelu(x):
    return jax.nn.gelu(x, approximate=True)

def _silu(x):
    return jax.nn.silu(x)

def _sigmoid(x):
    return jax.nn.sigmoid(x)

def _layernorm(x, axis=-1, eps=1e-05):
    m = jnp.mean(x, axis=axis, keepdims=True)
    v = jnp.var(x, axis=axis, keepdims=True)
    return (x - m) / jnp.sqrt(v + eps)

def _scatter_add(tgt, idx, src, axis=0):
    return tgt.at[idx].add(src)

def _segment_sum(src, seg, n):
    return jax.ops.segment_sum(src, seg, n)
kernel_name = 'mk_seq_preln_d2_jaxref_r8_9f8cfd'

def setup_inputs(seed: int=0):
    np.random.seed(seed)
    _w = jnp.asarray

    def _L0_attn_setup():
        import jax, jax.numpy as jnp
        import numpy as np
        ROPE_BASE = 10000.0
        ROPE_SCALE = 1.0
        ATTN_SCALE = 0.08838834764831845
        WINDOW = 128
        EPS = 1e-06

        def rms_norm(x, scale):
            var = jnp.mean(jnp.square(x), axis=-1, keepdims=True)
            return x * jax.lax.rsqrt(var + EPS) * scale

        def apply_rope(x, positions):
            H = x.shape[-1]
            frac = jnp.arange(0, H, 2, dtype=jnp.float32) / H
            timescale = ROPE_BASE ** frac
            sinusoid = positions[..., None].astype(jnp.float32) / timescale
            sinusoid = sinusoid / ROPE_SCALE
            sin = jnp.sin(sinusoid)[:, :, None, :]
            cos = jnp.cos(sinusoid)[:, :, None, :]
            x1, x2 = jnp.split(x, 2, axis=-1)
            return jnp.concatenate([x1 * cos - x2 * sin, x2 * cos + x1 * sin], axis=-1).astype(x.dtype)
        key = jax.random.key(seed)
        ks = jax.random.split(key, 4)
        B, T, D, N, K, H = (1, 512, 256, 16, 8, 128)
        return {'x': jax.random.normal(ks[0], (B, T, D), jnp.float32), 'q_kernel': jax.random.normal(ks[1], (N, D, H), jnp.float32) * D ** (-0.5), 'kv_kernel': jax.random.normal(ks[2], (2, K, D, H), jnp.float32) * D ** (-0.5), 'out_kernel': jax.random.normal(ks[3], (N, H, D), jnp.float32) * (N * H) ** (-0.5), 'q_norm_scale': jnp.ones((H,), jnp.float32), 'k_norm_scale': jnp.ones((H,), jnp.float32)}
    _L0_attn_in = _L0_attn_setup()

    def _L0_ffn_setup():
        import jax, jax.numpy as jnp
        import numpy as np
        H, I, E, TOP_K = (256, 176, 16, 6)
        IS = 352
        NORM_TOPK_PROB = False

        def _silu_and_mul(gate_up):
            d = gate_up.shape[-1] // 2
            g, u = (gate_up[..., :d], gate_up[..., d:])
            return jax.nn.silu(g) * u
        key = jax.random.key(seed)
        ks = jax.random.split(key, 6)
        s = 0.02
        return {'x': jax.random.normal(ks[0], (1, 256, H), jnp.float32), 'gate_w': jax.random.normal(ks[1], (E, H), jnp.float32) * s, 'w1': jax.random.normal(ks[2], (E, 2 * I, H), jnp.float32) * s, 'w2': jax.random.normal(ks[3], (E, H, I), jnp.float32) * s, 'shared_w1': jax.random.normal(ks[4], (2 * IS, H), jnp.float32) * s, 'shared_w2': jax.random.normal(ks[5], (H, IS), jnp.float32) * s}
    _L0_ffn_in = _L0_ffn_setup()

    def _L1_attn_setup():
        import jax, jax.numpy as jnp
        import numpy as np
        EMBED_DIM = 256
        NUM_HEADS = 16
        HEAD_DIM = EMBED_DIM // NUM_HEADS
        SCALE = 1.0 / float(np.sqrt(HEAD_DIM))
        B, S = (2, 256)
        key = jax.random.key(seed)
        ks = jax.random.split(key, 6)
        w = 0.02
        x = jax.random.normal(ks[0], (B, S, EMBED_DIM), dtype=jnp.float32)
        Wq = jax.random.normal(ks[1], (EMBED_DIM, EMBED_DIM), dtype=jnp.float32) * w
        Wk = jax.random.normal(ks[2], (EMBED_DIM, EMBED_DIM), dtype=jnp.float32) * w
        Wv = jax.random.normal(ks[3], (EMBED_DIM, EMBED_DIM), dtype=jnp.float32) * w
        Wo = jax.random.normal(ks[4], (EMBED_DIM, EMBED_DIM), dtype=jnp.float32) * w
        bo = jax.random.normal(ks[5], (EMBED_DIM,), dtype=jnp.float32) * w
        return {'x': x, 'Wq': Wq, 'Wk': Wk, 'Wv': Wv, 'Wo': Wo, 'bo': bo}
    _L1_attn_in = _L1_attn_setup()

    def _L1_ffn_setup():
        import jax, jax.numpy as jnp
        import numpy as np
        EPS = 1e-08

        def _bit_quant(w):
            scale = jnp.maximum(jnp.mean(jnp.abs(w)), EPS)
            w_ternary = jnp.clip(jnp.round(w / scale), -1.0, 1.0)
            return w + jax.lax.stop_gradient(w_ternary - w)
        key = jax.random.key(seed)
        k = jax.random.split(key, 5)
        emb, dff = (256, 1024)
        B, S = (4, 256)
        x = jax.random.normal(k[0], (B, S, emb), dtype=jnp.float32)
        w1 = jax.random.normal(k[1], (dff, emb), dtype=jnp.float32) * 0.02
        b1 = jax.random.normal(k[2], (dff,), dtype=jnp.float32) * 0.02
        w2 = jax.random.normal(k[3], (emb, dff), dtype=jnp.float32) * 0.02
        b2 = jax.random.normal(k[4], (emb,), dtype=jnp.float32) * 0.02
        return {'x': x, 'w1': w1, 'b1': b1, 'w2': w2, 'b2': b2}
    _L1_ffn_in = _L1_ffn_setup()
    _d = {'L0_attn_x': _L0_attn_in['x'], 'L0_attn_q_kernel': _L0_attn_in['q_kernel'], 'L0_attn_kv_kernel': _L0_attn_in['kv_kernel'], 'L0_attn_out_kernel': _L0_attn_in['out_kernel'], 'L0_attn_q_norm_scale': _L0_attn_in['q_norm_scale'], 'L0_attn_k_norm_scale': _L0_attn_in['k_norm_scale'], 'L0_ffn_gate_w': _L0_ffn_in['gate_w'], 'L0_ffn_w1': _L0_ffn_in['w1'], 'L0_ffn_w2': _L0_ffn_in['w2'], 'L0_ffn_shared_w1': _L0_ffn_in['shared_w1'], 'L0_ffn_shared_w2': _L0_ffn_in['shared_w2'], 'L1_attn_Wq': _L1_attn_in['Wq'], 'L1_attn_Wk': _L1_attn_in['Wk'], 'L1_attn_Wv': _L1_attn_in['Wv'], 'L1_attn_Wo': _L1_attn_in['Wo'], 'L1_attn_bo': _L1_attn_in['bo'], 'L1_ffn_w1': _L1_ffn_in['w1'], 'L1_ffn_b1': _L1_ffn_in['b1'], 'L1_ffn_w2': _L1_ffn_in['w2'], 'L1_ffn_b2': _L1_ffn_in['b2']}
    _x0 = _d['L0_attn_x']
    _d['L0_attn_x'] = jax.random.normal(jax.random.fold_in(jax.random.key(seed), 1), (4, 512, 256), dtype=_x0.dtype)
    del _x0
    return _d

def reference(L0_attn_x, L0_attn_q_kernel, L0_attn_kv_kernel, L0_attn_out_kernel, L0_attn_q_norm_scale, L0_attn_k_norm_scale, L0_ffn_gate_w, L0_ffn_w1, L0_ffn_w2, L0_ffn_shared_w1, L0_ffn_shared_w2, L1_attn_Wq, L1_attn_Wk, L1_attn_Wv, L1_attn_Wo, L1_attn_bo, L1_ffn_w1, L1_ffn_b1, L1_ffn_w2, L1_ffn_b2):

    def _L0_attn_ref(x, q_kernel, kv_kernel, out_kernel, q_norm_scale, k_norm_scale):
        import jax, jax.numpy as jnp
        import numpy as np
        ROPE_BASE = 10000.0
        ROPE_SCALE = 1.0
        ATTN_SCALE = 0.08838834764831845
        WINDOW = 128
        EPS = 1e-06

        def rms_norm(x, scale):
            var = jnp.mean(jnp.square(x), axis=-1, keepdims=True)
            return x * jax.lax.rsqrt(var + EPS) * scale

        def apply_rope(x, positions):
            H = x.shape[-1]
            frac = jnp.arange(0, H, 2, dtype=jnp.float32) / H
            timescale = ROPE_BASE ** frac
            sinusoid = positions[..., None].astype(jnp.float32) / timescale
            sinusoid = sinusoid / ROPE_SCALE
            sin = jnp.sin(sinusoid)[:, :, None, :]
            cos = jnp.cos(sinusoid)[:, :, None, :]
            x1, x2 = jnp.split(x, 2, axis=-1)
            return jnp.concatenate([x1 * cos - x2 * sin, x2 * cos + x1 * sin], axis=-1).astype(x.dtype)
        B, T, D = x.shape
        N, _, H = q_kernel.shape
        K = kv_kernel.shape[1]
        G = N // K
        q = jnp.einsum('btd,ndh->btnh', x, q_kernel)
        kv = jnp.einsum('bsd,ckdh->cbskh', x, kv_kernel)
        k, v = (kv[0], kv[1])
        q = rms_norm(q, q_norm_scale)
        k = rms_norm(k, k_norm_scale)
        positions = jnp.broadcast_to(jnp.arange(T)[None, :], (B, T))
        q = apply_rope(q, positions)
        k = apply_rope(k, positions)
        i = jnp.arange(T)[:, None]
        j = jnp.arange(T)[None, :]
        mask = (j <= i) & (i - j < WINDOW)
        qg = q.reshape(B, T, K, G, H)
        logits = jnp.einsum('btkgh,bskh->bkgts', qg * ATTN_SCALE, k)
        logits = jnp.where(mask[None, None, None], logits, jnp.finfo(logits.dtype).min)
        probs = jax.nn.softmax(logits, axis=-1)
        enc = jnp.einsum('bkgts,bskh->btkgh', probs, v).reshape(B, T, N, H)
        return jnp.einsum('btnh,nhd->btd', enc, out_kernel)

    def _L0_ffn_ref(x, gate_w, w1, w2, shared_w1, shared_w2):
        import jax, jax.numpy as jnp
        import numpy as np
        H, I, E, TOP_K = (256, 176, 16, 6)
        IS = 352
        NORM_TOPK_PROB = False

        def _silu_and_mul(gate_up):
            d = gate_up.shape[-1] // 2
            g, u = (gate_up[..., :d], gate_up[..., d:])
            return jax.nn.silu(g) * u
        B, S, Hd = x.shape
        xf = x.reshape(-1, Hd)
        T = xf.shape[0]
        shared_out = _silu_and_mul(xf @ shared_w1.T) @ shared_w2.T
        logits = xf @ gate_w.T
        probs = jax.nn.softmax(logits.astype(jnp.float32), axis=-1)
        routing_weights, selected = jax.lax.top_k(probs, TOP_K)
        if NORM_TOPK_PROB:
            routing_weights = routing_weights / routing_weights.sum(-1, keepdims=True)
        combine = jnp.zeros((T, E), jnp.float32).at[jnp.arange(T)[:, None], selected].add(routing_weights).astype(x.dtype)
        gate_up = jnp.einsum('th,eoh->teo', xf, w1)
        act = _silu_and_mul(gate_up)
        moe_out = jnp.einsum('te,tei,ehi->th', combine, act, w2)
        return (moe_out + shared_out).reshape(B, S, Hd)

    def _L1_attn_ref(x, Wq, Wk, Wv, Wo, bo):
        import jax, jax.numpy as jnp
        import numpy as np
        EMBED_DIM = 256
        NUM_HEADS = 16
        HEAD_DIM = EMBED_DIM // NUM_HEADS
        SCALE = 1.0 / float(np.sqrt(HEAD_DIM))
        B, S = (2, 256)
        b, s, e = x.shape
        q = (x @ Wq).reshape(b, s, NUM_HEADS, HEAD_DIM)
        k = (x @ Wk).reshape(b, s, NUM_HEADS, HEAD_DIM)
        v = (x @ Wv).reshape(b, s, NUM_HEADS, HEAD_DIM)
        scores = jnp.einsum('bqhd,bkhd->bhqk', q, k) * SCALE
        p = jax.nn.softmax(scores, axis=-1)
        o = jnp.einsum('bhqk,bkhd->bqhd', p, v).reshape(b, s, e)
        return o @ Wo + bo

    def _L1_ffn_ref(x, w1, b1, w2, b2):
        import jax, jax.numpy as jnp
        import numpy as np
        EPS = 1e-08

        def _bit_quant(w):
            scale = jnp.maximum(jnp.mean(jnp.abs(w)), EPS)
            w_ternary = jnp.clip(jnp.round(w / scale), -1.0, 1.0)
            return w + jax.lax.stop_gradient(w_ternary - w)
        w1q = _bit_quant(w1)
        w2q = _bit_quant(w2)
        h = jnp.einsum('bsd,fd->bsf', x, w1q) + b1
        h = jax.nn.gelu(h, approximate=False)
        return jnp.einsum('bsf,df->bsd', h, w2q) + b2
    x = L0_attn_x
    x = x + _L0_attn_ref(_layernorm(x, axis=-1), L0_attn_q_kernel, L0_attn_kv_kernel, L0_attn_out_kernel, L0_attn_q_norm_scale, L0_attn_k_norm_scale)
    x = x + _L0_ffn_ref(_layernorm(x, axis=-1), L0_ffn_gate_w, L0_ffn_w1, L0_ffn_w2, L0_ffn_shared_w1, L0_ffn_shared_w2)
    x = x + _L1_attn_ref(_layernorm(x, axis=-1), L1_attn_Wq, L1_attn_Wk, L1_attn_Wv, L1_attn_Wo, L1_attn_bo)
    x = x + _L1_ffn_ref(_layernorm(x, axis=-1), L1_ffn_w1, L1_ffn_b1, L1_ffn_w2, L1_ffn_b2)
    return x

_drawn_inputs = setup_inputs


def setup_inputs(seed=0):
    import zlib

    import numpy as np

    out = dict(_drawn_inputs(seed))
    spreads = {'L0_attn_q_norm_scale': (1.0, 0.553), 'L0_attn_k_norm_scale': (1.0, 0.2)}
    factors = {'L0_ffn_gate_w': 8.0,
     'L0_ffn_w1': 8.0,
     'L0_ffn_w2': 8.0,
     'L0_ffn_shared_w1': 3.153,
     'L0_ffn_shared_w2': 3.154,
     'L1_attn_Wq': 8.0,
     'L1_attn_Wk': 8.0,
     'L1_attn_Wv': 8.0,
     'L1_attn_Wo': 8.0,
     'L1_attn_bo': 19.442,
     'L1_ffn_b1': 37.437,
     'L1_ffn_b2': 64.0}
    for name, (base, spread) in spreads.items():
        noise = np.random.default_rng([zlib.crc32(name.encode()), seed]).standard_normal(out[name].shape)
        drawn = base * np.exp(spread * noise) if base else spread * noise
        out[name] = jnp.asarray(drawn.astype(out[name].dtype))
    for name, factor in factors.items():
        out[name] = (out[name] * factor).astype(out[name].dtype)
    return out
```

```python
from contextlib import ExitStack

import concourse.bass as bass
from concourse import mybir

F32 = mybir.dt.float32
F32R = mybir.dt.float32r
BF16 = mybir.dt.bfloat16
ALU = mybir.AluOpType
ACT = mybir.ActivationFunctionType
AX = mybir.AxisListType

P = 128
BATCHES, SEQ, D = 4, 512, 256
TT = SEQ // P
KT = D // P
NTILES = BATCHES * TT
LN_EPS = 1e-5

HEADS0, KV0, HD0 = 16, 8, 128
RMS_EPS = 1e-6
ATTN_SCALE0 = 0.08838834764831845
GROUPS = KV0
STEPS = GROUPS * TT
RAW_RING, QK_RING = 10, 4
LAST_LAG = 8

EXPERTS, INTER, TOP_K, SHARED = 16, 176, 6, 352
FEATS = EXPERTS * INTER + SHARED
FT = -(-FEATS // P)
W1_PIECE = 5
PIECE = 32

HEADS1, HD1 = 16, 16
PAIRS = HEADS1 // 2
VW = 32
MAX_ROW = 48
SCALE1 = 0.25

DFF = 1024
HT = DFF // P
ROUTE = 22
NORMED = PAIRS // 2 + TT
QUANT_EPS = 1e-8


def build(nc, dram, out):
    with ExitStack() as ctx:
        def sem(name):
            return ctx.enter_context(nc.semaphore(name))

        def sb(name, shape, dt=F32, where=None):
            return (where or ctx).enter_context(nc.sbuf_tensor(name, shape, dt))

        ps = ctx.enter_context(nc.psum_tensor("ps", [P, 8, 512], F32))

        x_res = sb("x_res", [P, NTILES, D])
        xn = sb("xn", [P, TT, D])
        xnT = sb("xnT", [P, KT, SEQ])
        yT = sb("yT", [P, KT, SEQ])
        ident = sb("ident", [P, P])
        bn_st = sb("bn_st", [P, TT, 6])
        bn_mv = sb("bn_mv", [P, TT, 2])
        ln_ve = sb("ln_ve", [P, TT])
        ln_rs = sb("ln_rs", [P, TT])
        minus_half = sb("minus_half", [P, 16])
        eps_sum = sb("eps_sum", [P, 3])
        spare = sb("spare", [P, 2])
        w2moe = sb("w2moe", [P, FT, D])
        gate = sb("gate", [P, KT, EXPERTS])

        part_a = ExitStack()
        wqkv = sb("wqkv", [P, KT, GROUPS, 4 * P], where=part_a)
        wo0 = sb("wo0", [P, HEADS0, D], where=part_a)
        ident_b = sb("ident_b", [P, P], BF16, part_a)
        window = sb("window", [P, 2, 2, P], BF16, part_a)
        qks = sb("qks", [P, 3, P], where=part_a)
        cos_in = sb("cos_in", [P, TT, P], where=part_a)
        sin_in = sb("sin_in", [P, TT, P], where=part_a)
        cos3 = sb("cos3", [P, TT, 3, P], where=part_a)
        sin3 = sb("sin3", [P, TT, 3, P], where=part_a)
        raw = sb("raw", [P, RAW_RING, 4 * P], where=part_a)
        sq = sb("sq", [P, 2, 3 * P], where=part_a)
        ssum = sb("ssum", [P, 2, 3], where=part_a)
        msq = sb("msq", [P, 2, 3], where=part_a)
        rms = sb("rms", [P, 2, 3], where=part_a)
        rope1 = sb("rope1", [P, 2, 3 * P], where=part_a)
        rope2 = sb("rope2", [P, 2, 3 * P], where=part_a)
        rot = sb("rot", [P, 2, 3 * P], where=part_a)
        qkn = sb("qkn", [P, 2, 3 * P], where=part_a)
        qkT = sb("qkT", [P, QK_RING, 3, P], where=part_a)
        nmax = sb("nmax", [P, 2, 2], where=part_a)
        psums = sb("psums", [P, 2, 2], where=part_a)
        rsums = sb("rsums", [P, 2, 2], where=part_a)
        prob = sb("prob", [P, 2, 2, 2 * P], where=part_a)
        probn = sb("probn", [P, 2, 2, 2 * P], where=part_a)
        probT = sb("probT", [P, 2, 4, P], where=part_a)
        encT = sb("encT", [P, HEADS0, SEQ], where=part_a)
        part_a.close()

        part_b = ExitStack()
        w1moe = sb("w1moe", [P, FT, KT, 2, P], where=part_b)
        sel = sb("sel", [3 * PIECE, FT, P], BF16, part_b)
        lg = sb("lg", [P, TT, EXPERTS], where=part_b)
        gmax = sb("gmax", [P, TT], where=part_b)
        gexp = sb("gexp", [P, TT, EXPERTS], where=part_b)
        gsum = sb("gsum", [P, TT], where=part_b)
        ginv = sb("ginv", [P, TT], where=part_b)
        gprob = sb("gprob", [P, TT, EXPERTS + 2], where=part_b)
        gtop = sb("gtop", [P, TT, 8], where=part_b)
        gmark = sb("gmark", [P, TT, EXPERTS + 2], where=part_b)
        gmask = sb("gmask", [P, TT, EXPERTS], where=part_b)
        comb = sb("comb", [P, TT, P], where=part_b)
        cT = sb("cT", [PIECE, SEQ], where=part_b)
        cTr = sb("cTr", [PIECE, 2, SEQ], where=part_b)
        cpieces = sb("cpieces", [3 * PIECE, SEQ], BF16, part_b)
        sg = sb("sg", [P, 2, SEQ], where=part_b)
        gated = sb("gated", [P, 2, SEQ], where=part_b)
        moe_act = sb("moe_act", [P, 3, SEQ], where=part_b)
        part_b.close()

        part_c = ExitStack()
        wq1 = sb("wq1", [P, KT, PAIRS, P], where=part_c)
        wk1 = sb("wk1", [P, KT, PAIRS, P], where=part_c)
        wv1 = sb("wv1", [P, KT, HEADS1 * VW], where=part_c)
        wo1 = sb("wo1", [P, KT, D], where=part_c)
        bo1 = sb("bo1", [P, D], where=part_c)
        vones = sb("vones", [P, HEADS1 * VW], where=part_c)
        stack = sb("stack", [P, 4], where=part_c)
        v1 = sb("v1", [P, TT, HEADS1 * VW], where=part_c)
        qhi = sb("qhi", [P, 2, SEQ], F32R, part_c)
        khi = sb("khi", [P, 2, SEQ], F32R, part_c)
        qst = sb("qst", [P, 2, SEQ], F32R, part_c)
        kst = sb("kst", [P, 3, SEQ], F32R, part_c)
        qsm = sb("qsm", [P, 2, SEQ], F32R, part_c)
        nm1 = sb("nm1", [P, 2, TT, P], where=part_c)
        pT1 = sb("pT1", [P, 2, 4, TT, SEQ], where=part_c)
        oT1 = sb("oT1", [P, 2, SEQ], where=part_c)
        oinv = sb("oinv", [P, 2, TT, 4], where=part_c)
        otok = sb("otok", [P, TT, D], where=part_c)
        oTn = sb("oTn", [P, KT, SEQ], where=part_c)
        part_c.close()
        part_d = ExitStack()
        wm1 = sb("wm1", [P, KT, DFF], where=part_d)
        wm2 = sb("wm2", [P, HT, D], where=part_d)
        wneg = sb("wneg", [P, 2, KT * DFF], where=part_d)
        wt1 = sb("wt1", [P, KT, DFF], where=part_d)
        wt2 = sb("wt2", [P, HT, D], where=part_d)
        ones = sb("ones", [P, P], where=part_d)
        wabs = sb("wabs", [P, 2], where=part_d)
        wscl = sb("wscl", [P, 2], where=part_d)
        whalf = sb("whalf", [P, 2], where=part_d)
        wmhalf = sb("wmhalf", [P, 2], where=part_d)
        b1m = sb("b1m", [P, HT], where=part_d)
        b2m = sb("b2m", [P, KT], where=part_d)
        hact = sb("hact", [P, 3, SEQ], where=part_d)
        part_d.close()

        x_loaded = sem("x_loaded")
        consts_loaded = sem("consts_loaded")
        tables_loaded = sem("tables_loaded")
        wqkv_loaded = [sem(f"wqkv_loaded{i}") for i in range(GROUPS // 2)]
        wo0_loaded = sem("wo0_loaded")
        wb_loaded = sem("wb_loaded")
        sel_loaded = sem("sel_loaded")
        w1_loaded = [sem(f"w1_loaded{i}") for i in range(FT // W1_PIECE)]
        wc_loaded = sem("wc_loaded")
        wd_loaded = sem("wd_loaded")
        masks_loaded = sem("masks_loaded")
        out_stored = sem("out_stored")
        half_set = sem("half_set")
        ln_stats, ln_aggr, ln_var = sem("ln_stats"), sem("ln_aggr"), sem("ln_var")
        ln_rstd, xn_ready = sem("ln_rstd"), sem("xn_ready")
        xn_turned, xnT_ready = sem("xn_turned"), sem("xnT_ready")
        tables_scaled = sem("tables_scaled")
        projected, raw_kept, squared = sem("projected"), sem("raw_kept"), sem("squared")
        summed, meaned, rms_ready = sem("summed"), sem("meaned"), sem("rms_ready")
        roped, rotated, qk_normed = sem("roped"), sem("rotated"), sem("qk_normed")
        qk_turned, qkT_ready = sem("qk_turned"), sem("qkT_ready")
        scored, max_ready, prob_ready = sem("scored"), sem("max_ready"), sem("prob_ready")
        inv_ready, probn_ready = sem("inv_ready"), sem("probn_ready")
        prob_turned, probT_ready = sem("prob_turned"), sem("probT_ready")
        attended, enc_ready = sem("attended"), sem("enc_ready")
        out0_ready, out0_added = sem("out0_ready"), sem("out0_added")
        logits_ready, route_step = sem("logits_ready"), sem("route_step")
        comb_turned, comb_step = sem("comb_turned"), sem("comb_step")
        gate_exp = sem("gate_exp")
        gu_ready, silu_ready, gated_ready = sem("gu_ready"), sem("silu_ready"), sem("gated_ready")
        c_ready, act_ready, y_used = sem("c_ready"), sem("act_ready"), sem("y_used")
        yT_ready, y_turned, y_added = sem("yT_ready"), sem("y_turned"), sem("y_added")
        c_consts_ready = sem("c_consts_ready")
        v_ready, v_kept = sem("v_ready"), sem("v_kept")
        qk1_ready, qk1_hi, qk1_stacked = sem("qk1_ready"), sem("qk1_hi"), sem("qk1_stacked")
        s1_ready, s1_max = sem("s1_ready"), sem("s1_max")
        m_turned, qsm_ready = sem("m_turned"), sem("qsm_ready")
        st_ready, p1_ready = sem("st_ready"), sem("p1_ready")
        o1_ready, oT1_kept, o1_turned = sem("o1_ready"), sem("oT1_kept"), sem("o1_turned")
        o1_inv, o1_normed = sem("o1_inv"), sem("o1_normed")
        on_turned, oTn_ready, out1_ready, out1_added = (
            sem("on_turned"), sem("oTn_ready"), sem("out1_ready"), sem("out1_added"))
        quant_step, wabs_summed, quantized = sem("quant_step"), sem("wabs_summed"), sem("quantized")
        h_ready, h_act, h_used = sem("h_ready"), sem("h_act"), sem("h_used")

        block = ctx.enter_context(nc.Block())

        def wait(eng, s, value):
            if not (isinstance(value, int) and value <= 0):
                eng.wait_ge(s, value)

        @block.sync
        def _(sp):
            sp.dma_start(ident[:], dram["c_ident"]).then_inc(consts_loaded, 16)
            sp.dma_start(x_res[:], dram["x"].rearrange("b (t p) d -> p (b t) d", p=P)).then_inc(x_loaded, 16)
            for i in range(GROUPS // 2):
                sp.dma_start(wqkv[:, :, 2 * i:2 * i + 2, :], dram["wqkv"][:, :, 2 * i:2 * i + 2, :]
                             ).then_inc(wqkv_loaded[i], 16)
                if i == 0:
                    sp.dma_start(qks[:, 0:2, :], dram["qs"].unsqueeze(0).unsqueeze(0).to_broadcast((P, 2, P))
                                 ).then_inc(tables_loaded, 16)
                    sp.dma_start(qks[:, 2, :], dram["ks"].unsqueeze(0).to_broadcast((P, P))
                                 ).then_inc(tables_loaded, 16)
                    sp.dma_start(cos_in[:], dram["c_cos"]).then_inc(tables_loaded, 16)
                    sp.dma_start(sin_in[:], dram["c_sin"]).then_inc(tables_loaded, 16)
            sp.dma_start(wo0[:], dram["wo0"]).then_inc(wo0_loaded, 16)
            sp.dma_start(gate[:], dram["gate"]).then_inc(wb_loaded, 16)
            sp.dma_start(w2moe[:], dram["w2moe"]).then_inc(wb_loaded, 16)
            wait(sp, out0_added, BATCHES * TT)
            for j in range(0, FT, W1_PIECE):
                sp.dma_start(w1moe[:, j:j + W1_PIECE], dram["w1moe"][:, j:j + W1_PIECE]).then_inc(w1_loaded[j // W1_PIECE], 16)
            wait(sp, y_added, BATCHES * TT)
            for name, dst in (("wq1", wq1), ("wk1", wk1), ("wv1", wv1), ("wo1", wo1),
                              ("c_vones", vones), ("c_stack", stack)):
                sp.dma_start(dst[:], dram[name]).then_inc(wc_loaded, 16)
            sp.dma_start(bo1[:], dram["bo1"].unsqueeze(0).to_broadcast((P, D))).then_inc(wc_loaded, 16)
            wait(sp, out1_added, BATCHES * TT)
            for name, dst in (("wm1", wm1), ("wm2", wm2), ("b1m", b1m), ("b2m", b2m)):
                sp.dma_start(dst[:], dram[name]).then_inc(wd_loaded, 16)
            for b in range(BATCHES):
                sp.wait_ge(y_added, (BATCHES + b + 1) * TT)
                sp.dma_start(out[b].rearrange("(t p) d -> p t d", p=P),
                             x_res[:, b * TT:(b + 1) * TT, :]).then_inc(out_stored, 16)
            sp.wait_ge(out_stored, 16 * BATCHES)

        @block.gpsimd
        def _(pool):
            nc.gpsimd.memset(minus_half[:], -0.5).then_inc(half_set, 1)
            nc.gpsimd.memset(eps_sum[:], HD0 * RMS_EPS).then_inc(half_set, 1)
            pool.dma_start(ident_b[:], dram["c_ident"]).then_inc(masks_loaded, 16)
            pool.dma_start(window[:], dram["c_window"]).then_inc(masks_loaded, 16)
            pool.wait_ge(half_set, 2)

            def rstd(i):
                pool.wait_ge(ln_var, i + 1)
                nc.gpsimd.tensor_tensor(ln_rs[:], ln_ve[:], minus_half[:, 0:TT], ALU.pow).then_inc(ln_rstd, 1)

            rstd(0)
            with pool.Fori(0, BATCHES) as b:
                for n in range(STEPS):
                    if n == STEPS // 2 + 1:
                        rstd(b + 1)
                    k, s = b * STEPS + n, n % 2
                    pool.wait_ge(summed, k + 1)
                    if n >= 2:
                        pool.wait_ge(qk_normed, k - 1)
                    nc.gpsimd.tensor_tensor(msq[:, s, :], ssum[:, s, :], eps_sum[:], ALU.add).then_inc(meaned, 1)
                    pool.wait_ge(meaned, k + 1)
                    nc.gpsimd.tensor_tensor(rms[:, s, :], msq[:, s, :], minus_half[:, 0:3],
                                            ALU.pow).then_inc(rms_ready, 1)
                    pool.wait_ge(roped, k + 1)
                    nc.gpsimd.tensor_tensor(rot[:, s, :], rope1[:, s, :], rope2[:, s, :],
                                            ALU.add).then_inc(rotated, 1)
            pool.wait_ge(out0_added, BATCHES * TT)
            pool.dma_start(sel[:], dram["c_sel"]).then_inc(sel_loaded, 16)
            for part in range(1, 4):
                with pool.Fori(0, BATCHES) as b:
                    rstd(b + part * BATCHES + 1)

        @block.vector
        def _(dve):
            V = nc.vector

            def x_tile(b, t):
                return x_res[:, bass.ds(b * TT + t, 1), :].rearrange("p a d -> p (a d)")

            def norm_stats(i, b):
                for t in range(TT):
                    V.bn_stats(bn_st[:, t, :], x_tile(b, t)).then_inc(ln_stats, 1)
                dve.wait_ge(ln_stats, i * TT + TT)
                V.memset(spare[:, 0:1], 0.0)
                for t in range(TT):
                    V.bn_aggr(bn_mv[:, t, :], bn_st[:, t, :]).then_inc(ln_aggr, 1)
                dve.wait_ge(ln_aggr, i * TT + TT)
                V.tensor_scalar(ln_ve[:], bn_mv[:, :, 1], LN_EPS, None, ALU.add).then_inc(ln_var, 1)

            def norm_apply(i, b):
                dve.wait_ge(ln_rstd, i + 1)
                dve.wait_ge(xn_turned, i * KT + 1)
                for t in range(TT):
                    V.tensor_scalar(xn[:, t, :], x_tile(b, t), bn_mv[:, t, 0:1], ln_rs[:, t:t + 1],
                                    ALU.subtract, ALU.mult).then_inc(xn_ready, 1)

            V.memset(spare[:, 0:1], 0.0).then_inc(xn_turned, 1)
            dve.wait_ge(tables_loaded, 4 * 16)
            V.tensor_scalar(qks[:, 0:2, :], qks[:, 0:2, :], ATTN_SCALE0 * HD0 ** 0.5, None, ALU.mult
                            ).then_inc(tables_scaled, 1)
            V.tensor_scalar(qks[:, 2, :], qks[:, 2, :], HD0 ** 0.5, None, ALU.mult).then_inc(tables_scaled, 1)
            dve.wait_ge(tables_scaled, 2)
            H2 = HD0 // 2
            for h in range(3):
                sc = qks[:, h:h + 1, :].to_broadcast((P, TT, P))
                lo, hi = sc[:, :, 0:H2], sc[:, :, H2:HD0]
                V.tensor_tensor(cos3[:, :, h, :], cos_in[:], sc, ALU.mult).then_inc(tables_scaled, 1)
                V.tensor_tensor(sin3[:, :, h, 0:H2], sin_in[:, :, 0:H2], hi, ALU.mult).then_inc(tables_scaled, 1)
                V.tensor_tensor(sin3[:, :, h, H2:HD0], sin_in[:, :, H2:HD0], lo, ALU.mult).then_inc(tables_scaled, 1)
            dve.wait_ge(tables_scaled, 11)

            dve.wait_ge(x_loaded, 16)
            norm_stats(0, 0)
            norm_apply(0, 0)
            with dve.Fori(0, BATCHES) as b:
                following = (b + 1) % BATCHES
                for n in range(STEPS + LAST_LAG):
                    k0 = b * STEPS
                    if n == STEPS // 2:
                        norm_stats(b + 1, following)
                    if n == STEPS // 2 + 2:
                        norm_apply(b + 1, following)
                    if 6 <= n < STEPS + 6:
                        m = n - 6
                        k, s, w = k0 + m, m % 2, (P if m % TT == 0 else 2 * P)
                        dve.wait_ge(prob_ready, k + 1)
                        V.reciprocal(rsums[:, s, :], psums[:, s, :]).then_inc(inv_ready, 1)
                        dve.wait_ge(inv_ready, k + 1)
                        if m >= 2:
                            dve.wait_ge(prob_turned, k - 1)
                        for h in range(2):
                            ins = V.tensor_scalar(probn[:, s, h, 0:w], prob[:, s, h, 0:w], rsums[:, s, h:h + 1],
                                                  None, ALU.mult)
                        ins.then_inc(probn_ready, 1)
                    if 4 <= n < STEPS + 4:
                        m = n - 4
                        k, s, w = k0 + m, m % 2, (P if m % TT == 0 else 2 * P)
                        dve.wait_ge(scored, k + 1)
                        V.tensor_reduce(nmax[:, s, :], ps[:, 3 + s, :].rearrange("p (h f) -> p h f", h=2)[:, :, 0:w],
                                        AX.X, ALU.max, negate=True).then_inc(max_ready, 1)
                    if 7 <= n < STEPS + 7:
                        m = n - 7
                        k, s = k0 + m, m % 2
                        dve.wait_ge(prob_turned, k + 1)
                        if m >= 2:
                            dve.wait_ge(attended, k - 1)
                        kt = slice(1, 4, 2) if m % TT == 0 else slice(0, 4)
                        V.tensor_copy(probT[:, s, kt, :], ps[:, 5, :].rearrange("p (a f) -> p a f", a=4)[:, kt, :]
                                      ).then_inc(probT_ready, 1)
                    if 1 <= n <= STEPS:
                        m = n - 1
                        k, s = k0 + m, m % 2
                        dve.wait_ge(rotated, k + 1)
                        dve.wait_ge(rms_ready, k + 1)
                        if m >= 2:
                            dve.wait_ge(qk_turned, k - 1)
                        V.tensor_tensor(qkn[:, s, :].rearrange("p (h f) -> p h f", h=3),
                                        rot[:, s, :].rearrange("p (h f) -> p h f", h=3),
                                        rms[:, s, :].unsqueeze(2).to_broadcast((P, 3, P)), ALU.mult
                                        ).then_inc(qk_normed, 1)
                    if n < STEPS:
                        k, s, t = k0 + n, n % 2, n % TT
                        dve.wait_ge(squared, k + 1)
                        if n >= 2:
                            dve.wait_ge(rotated, k - 1)
                        V.reduce_sum(ssum[:, s, :], sq[:, s, :].rearrange("p (h f) -> p h f", h=3), AX.X
                                     ).then_inc(summed, 1)
                        r3 = raw[:, n % RAW_RING, 0:3 * P]
                        V.tensor_tensor(rope1[:, s, :], r3, cos3[:, t, :, :].rearrange("p h f -> p (h f)"), ALU.mult)
                        rh = r3.rearrange("p (h f) -> p h f", h=3)
                        o2 = rope2[:, s, :].rearrange("p (h f) -> p h f", h=3)
                        V.tensor_tensor(o2[:, :, 0:H2], rh[:, :, H2:HD0], sin3[:, t, :, 0:H2], ALU.mult)
                        V.tensor_tensor(o2[:, :, H2:HD0], rh[:, :, 0:H2], sin3[:, t, :, H2:HD0], ALU.mult
                                        ).then_inc(roped, 1)
                for t in range(TT):
                    dve.wait_ge(out0_ready, b * TT + t + 1)
                    V.tensor_tensor(x_tile(b, t), ps[:, 5 + t % 2 * 2, 0:D], x_tile(b, t), ALU.add
                                    ).then_inc(out0_added, 1)
                dve.wait_ge(out0_added, b * TT + TT)

            def add_turned(i, b):
                for t in range(TT):
                    if t % 2 == 0:
                        dve.wait_ge(y_turned, i * 2 + t // 2 + 1)
                    V.tensor_tensor(x_tile(b, t), ps[:, 4 + t // 2, (t % 2) * D:(t % 2 + 1) * D], x_tile(b, t),
                                    ALU.add).then_inc(y_added, 1)
                dve.wait_ge(y_added, i * TT + TT)

            V.memset(cpieces[:], 0.0).then_inc(route_step, 1)
            V.memset(comb[:], 0.0).then_inc(route_step, 1)
            V.memset(gprob[:], -1.0).then_inc(route_step, 1)
            dve.wait_ge(route_step, 3)
            V.memset(comb[:, :, EXPERTS:EXPERTS + 1], 1.0).then_inc(route_step, 1)
            dve.wait_ge(route_step, 4)
            with dve.Fori(0, BATCHES) as b:
                following = (b + 1) % BATCHES
                links = [0]

                def link(ins, wait_now=True):
                    links[0] += 1
                    ins.then_inc(route_step, 1)
                    if wait_now:
                        dve.wait_ge(route_step, b * ROUTE + (4 + links[0]))

                dve.wait_ge(logits_ready, b + 1)
                lps = ps[:, 7, 0:TT * EXPERTS].rearrange("p (t e) -> p t e", t=TT)
                link(V.reduce_max(gmax[:], lps, AX.X))
                link(V.tensor_tensor(lg[:], lps, gmax[:].unsqueeze(2).to_broadcast((P, TT, EXPERTS)), ALU.subtract))
                dve.wait_ge(gate_exp, b + 1)
                link(V.reduce_sum(gsum[:], gexp[:], AX.X))
                link(V.reciprocal(ginv[:], gsum[:]))
                link(V.tensor_tensor(gprob[:, :, 0:EXPERTS], gexp[:],
                                     ginv[:].unsqueeze(2).to_broadcast((P, TT, EXPERTS)), ALU.mult))
                V.memset(spare[:, 1:2], 0.0)
                for t in range(TT):
                    link(V.max(gtop[:, t, :], gprob[:, t, 0:EXPERTS]), t == TT - 1)
                link(V.memset(gtop[:, :, TOP_K:8], -1.0))
                V.memset(spare[:, 1:2], 0.0)
                for t in range(TT):
                    link(V.match_replace(gmark[:, t, :], gtop[:, t, :], gprob[:, t, :], -2.0), t == TT - 1)
                link(V.tensor_scalar(gmask[:], gmark[:, :, 0:EXPERTS], -2.0, None, ALU.is_equal))
                link(V.tensor_tensor(comb[:, :, 0:EXPERTS], gmask[:], gprob[:, :, 0:EXPERTS], ALU.mult))
                dve.wait_ge(comb_turned, b + 1)
                link(V.tensor_copy(cT[:], ps[0:PIECE, 6, :]))
                link(V.tensor_copy(cpieces[0:PIECE, :], cT[:]))
                link(V.tensor_tensor(cTr[:, 0, :], cT[:], cpieces[0:PIECE, :], ALU.subtract))
                link(V.tensor_copy(cpieces[PIECE:2 * PIECE, :], cTr[:, 0, :]))
                link(V.tensor_tensor(cTr[:, 1, :], cTr[:, 0, :], cpieces[PIECE:2 * PIECE, :], ALU.subtract))
                link(V.tensor_copy(cpieces[2 * PIECE:3 * PIECE, :], cTr[:, 1, :]))
                assert links[0] == ROUTE, links
                for j in range(FT):
                    k = b * FT + j
                    if j == FT // 2:
                        norm_stats(b + BATCHES + 1, following)
                    if j == FT // 2 + 2:
                        norm_apply(b + BATCHES + 1, following)
                    dve.wait_ge(silu_ready, k + 1)
                    V.tensor_tensor(gated[:, j % 2, :], ps[:, 2 + j % 2, :], sg[:, j % 2, :], ALU.mult
                                    ).then_inc(gated_ready, 1)
                    dve.wait_ge(gated_ready, k + 1)
                    dve.wait_ge(c_ready, k + 1)
                    if j >= 3:
                        dve.wait_ge(y_used, k - 2)
                    V.tensor_tensor(moe_act[:, j % 3, :], ps[:, 6, :], gated[:, j % 2, :], ALU.mult
                                    ).then_inc(act_ready, 1)
                add_turned(b, b)

            V.memset(nm1[:], 0.0).then_inc(c_consts_ready, 1)
            dve.wait_ge(c_consts_ready, 1)
            dve.wait_ge(wc_loaded, 7 * 16)
            with dve.Fori(0, BATCHES) as b:
                following = (b + 1) % BATCHES
                for t in range(TT):
                    dve.wait_ge(v_ready, b * TT + t + 1)
                    V.tensor_tensor(v1[:, t, :], ps[:, t % 2, :], vones[:], ALU.add).then_inc(v_kept, 1)
                for n in range(PAIRS + 4):
                    kb, kq = b * PAIRS, b * (PAIRS // 2)
                    if n == 5:
                        norm_stats(b + 2 * BATCHES + 1, following)
                    if n == 6:
                        norm_apply(b + 2 * BATCHES + 1, following)
                    for i in range(2 * TT):
                        if 1 <= n <= PAIRS:
                            m = n - 1
                            h, t = i // TT, i % TT
                            dve.wait_ge(s1_ready, (kb + m) * 2 * TT + i + 1)
                            col = 64 * h + MAX_ROW
                            V.tensor_reduce(nm1[:, m % 2, t, col:col + 1], ps[:, 2 + i % 2, :], AX.X, ALU.max,
                                            negate=True).then_inc(s1_max, 1)
                        if i == 0 and 2 <= n <= PAIRS + 1:
                            m = n - 2
                            k = kb + m
                            dve.wait_ge(m_turned, k + 1)
                            if m >= 2:
                                dve.wait_ge(st_ready, (k - 1) * 2 * TT)
                            V.tensor_tensor(qsm[:, m % 2, :], ps[:, 7, :], qst[:, m % 2, :], ALU.add
                                            ).then_inc(qsm_ready, 1)
                        if i == 5 and n < PAIRS:
                            k = kb + n
                            dve.wait_ge(qk1_hi, 2 * (k + 1))
                            if n >= 2:
                                dve.wait_ge(qsm_ready, k - 1)
                            V.scalar_tensor_tensor(qst[:, n % 2, :], qhi[:, n % 2, :], stack[:, 0:1], ps[:, 0, :],
                                                   ALU.mult, ALU.add).then_inc(qk1_stacked, 1)
                            if n >= 3:
                                dve.wait_ge(st_ready, (k - 2) * 2 * TT)
                            V.scalar_tensor_tensor(kst[:, n % 3, :], khi[:, n % 2, :], stack[:, 1:2], ps[:, 1, :],
                                                   ALU.mult, ALU.add).then_inc(qk1_stacked, 1)
                        if i == 5 and n >= 5 and n % 2 == 1:
                            u = (n - 5) // 2
                            dve.wait_ge(o1_turned, kq + u + 1)
                            o4 = ps[:, 6, :].rearrange("p (t h c) -> p t h c", t=TT, h=4)
                            V.reciprocal(oinv[:, u % 2, :, :], o4[:, :, :, HD1]).then_inc(o1_inv, 1)
                            dve.wait_ge(o1_inv, kq + u + 1)
                            V.tensor_tensor(
                                otok[:, :, u * 4 * HD1:(u + 1) * 4 * HD1].rearrange("p t (h c) -> p t h c", h=4),
                                o4[:, :, :, 0:HD1], oinv[:, u % 2, :, :].unsqueeze(3).to_broadcast((P, TT, 4, HD1)),
                                ALU.mult).then_inc(o1_normed, 1)
                for t in range(TT):
                    dve.wait_ge(out1_ready, b * TT + t + 1)
                    V.tensor_tensor(x_tile(b, t), ps[:, 2 + t, 0:D], x_tile(b, t),
                                    ALU.add).then_inc(o1_normed, 1)
                    dve.wait_ge(o1_normed, b * NORMED + PAIRS // 2 + t + 1)
                    V.tensor_tensor(x_tile(b, t), x_tile(b, t), bo1[:], ALU.add).then_inc(out1_added, 1)
                dve.wait_ge(out1_added, b * TT + TT)

            V.memset(ones[:], 1.0).then_inc(quant_step, 1)
            dve.wait_ge(wd_loaded, 4 * 16)
            flat = [wm1[:].rearrange("p a f -> p (a f)"), wm2[:].rearrange("p a f -> p (a f)")]
            tern = [wt1[:].rearrange("p a f -> p (a f)"), wt2[:].rearrange("p a f -> p (a f)")]
            for i in range(2):
                V.tensor_reduce(wabs[:, i:i + 1], flat[i], AX.X, ALU.add, apply_absolute_value=True
                                ).then_inc(quant_step, 1)
            dve.wait_ge(wabs_summed, 1)
            V.tensor_scalar(wscl[:], ps[:, 6, 0:2], 1.0 / (DFF * D), QUANT_EPS, ALU.mult, ALU.max
                            ).then_inc(quant_step, 1)
            dve.wait_ge(quant_step, 4)
            V.tensor_scalar(whalf[:], wscl[:], 0.5, None, ALU.mult).then_inc(quant_step, 1)
            V.tensor_scalar(wmhalf[:], wscl[:], -0.5, None, ALU.mult).then_inc(quant_step, 1)
            dve.wait_ge(quant_step, 6)
            for i in range(2):
                V.tensor_scalar(wneg[:, i, :], flat[i], wmhalf[:, i:i + 1], None, ALU.is_lt).then_inc(quant_step, 1)
                dve.wait_ge(quant_step, 7 + i)
                V.scalar_tensor_tensor(tern[i], flat[i], whalf[:, i:i + 1], wneg[:, i, :], ALU.is_gt, ALU.subtract
                                       ).then_inc(quantized, 1)
            with dve.Fori(0, BATCHES) as b:
                with_next = (b + 1) % BATCHES
                norm_stats(b + 3 * BATCHES + 1, with_next)
                norm_apply(b + 3 * BATCHES + 1, with_next)
                add_turned(b + BATCHES, b)

        @block.scalar
        def _(act):
            A = nc.scalar.activation

            def keep_xnT(i):
                for c in range(KT):
                    act.wait_ge(xn_turned, i * KT + c + 2)
                    A(xnT[:, c, :], ps[:, c, :], ACT.Copy).then_inc(xnT_ready, 1)

            keep_xnT(0)
            with act.Fori(0, BATCHES) as b:
                k0 = b * STEPS
                for n in range(STEPS + LAST_LAG):
                    if n < STEPS:
                        k, s = k0 + n, n % 2
                        act.wait_ge(projected, k + 1)
                        A(raw[:, n % RAW_RING, :], ps[:, s, :], ACT.Copy).then_inc(raw_kept, 1)
                        if n >= 2:
                            act.wait_ge(summed, k - 1)
                        A(sq[:, s, :], ps[:, s, 0:3 * P], ACT.Square).then_inc(squared, 1)
                    if n == STEPS + 2:
                        keep_xnT(b + 1)
                    if n >= 8:
                        m = n - 8
                        g, t = m // TT, m % TT
                        act.wait_ge(attended, k0 + m + 1)
                        A(encT[:, 2 * g:2 * g + 2, t * P:(t + 1) * P],
                          ps[:, 6, 0:2 * P].rearrange("p (h f) -> p h f", h=2), ACT.Copy).then_inc(enc_ready, 1)
                    if 4 <= n < STEPS + 4:
                        m = n - 4
                        k, s, w = k0 + m, m % 2, (P if m % TT == 0 else 2 * P)
                        act.wait_ge(max_ready, k + 1)
                        if m >= 2:
                            act.wait_ge(probn_ready, k - 1)
                        for h in range(2):
                            ins = A(prob[:, s, h, 0:w], ps[:, 3 + s, h * 2 * P:h * 2 * P + w], ACT.Exp,
                                    bias=nmax[:, s, h:h + 1], accum_out=psums[:, s, h:h + 1])
                        ins.then_inc(prob_ready, 1)
                    if 2 <= n < STEPS + 2:
                        m = n - 2
                        act.wait_ge(qk_turned, k0 + m + 1)
                        A(qkT[:, m % QK_RING, :, :], ps[:, 2, 0:3 * P].rearrange("p (h f) -> p h f", h=3), ACT.Copy
                          ).then_inc(qkT_ready, 1)

            with act.Fori(0, BATCHES) as b:
                act.wait_ge(route_step, b * ROUTE + 4 + 2)
                A(gexp[:], lg[:], ACT.Exp).then_inc(gate_exp, 1)
                for j in range(FT):
                    k = b * FT + j
                    act.wait_ge(gu_ready, k + 1)
                    if j >= 2:
                        act.wait_ge(gated_ready, k - 1)
                    A(sg[:, j % 2, :], ps[:, j % 2, :], ACT.Silu).then_inc(silu_ready, 1)
                keep_xnT(b + BATCHES + 1)
                act.wait_ge(y_used, b * FT + FT)
                for c in range(KT):
                    A(yT[:, c, :], ps[:, 4 + c, :], ACT.Copy).then_inc(yT_ready, 1)

            act.wait_ge(wc_loaded, 7 * 16)
            with act.Fori(0, BATCHES) as b:
                for n in range(PAIRS + 3):
                    kb, kq = b * PAIRS, b * (PAIRS // 2)
                    for i in range(2 * TT):
                        if 2 <= n <= PAIRS + 1:
                            m = n - 2
                            h, c, u = i // TT, i % TT, m // 2
                            if m >= 4 and i == 0:
                                act.wait_ge(o1_ready, kq + u - 1)
                            act.wait_ge(st_ready, (kb + m) * 2 * TT + i + 1)
                            A(pT1[:, u % 2, 2 * (m % 2) + h, c, :], ps[:, 4 + i % 2, :], ACT.Exp, scale=SCALE1
                              ).then_inc(p1_ready, 1)
                        if n < PAIRS and i == 3:
                            k = kb + n
                            act.wait_ge(qk1_ready, k + 1)
                            if n >= 2:
                                act.wait_ge(qk1_stacked, 2 * (k - 1))
                            A(qhi[:, n % 2, :], ps[:, 0, :], ACT.Copy).then_inc(qk1_hi, 1)
                            A(khi[:, n % 2, :], ps[:, 1, :], ACT.Identity, bias=stack[:, 2:3]).then_inc(qk1_hi, 1)
                    if n >= 4 and n % 2 == 0:
                        u = (n - 4) // 2
                        act.wait_ge(o1_ready, kq + u + 1)
                        if u >= 2:
                            act.wait_ge(o1_turned, kq + u - 1)
                        A(oT1[:, u % 2, :], ps[:, 6, :], ACT.Copy).then_inc(oT1_kept, 1)
                    if n == PAIRS + 1:
                        keep_xnT(b + 2 * BATCHES + 1)
                act.wait_ge(on_turned, b + 1)
                for c in range(KT):
                    A(oTn[:, c, :], ps[:, c, :], ACT.Copy).then_inc(oTn_ready, 1)

            act.wait_ge(wd_loaded, 4 * 16)
            with act.Fori(0, BATCHES) as b:
                for f in range(HT):
                    k = b * HT + f
                    act.wait_ge(h_ready, k + 1)
                    if f >= 3:
                        act.wait_ge(h_used, k - 2)
                    A(hact[:, f % 3, :], ps[:, 2 + f % 2, :], ACT.Gelu, bias=b1m[:, f:f + 1]).then_inc(h_act, 1)
                keep_xnT(b + 3 * BATCHES + 1)
                act.wait_ge(h_used, b * HT + HT)
                for c in range(KT):
                    A(yT[:, c, :], ps[:, 6 + c, :], ACT.Identity, bias=b2m[:, c:c + 1]).then_inc(yT_ready, 1)

        @block.tensor
        def _(pe):
            MM, T = nc.tensor.matmul, nc.tensor.transpose

            def turn_xn(i):
                pe.wait_ge(xn_ready, i * TT + TT)
                for c in range(KT):
                    for t in range(TT):
                        ins = T(ps[:, c, t * P:(t + 1) * P], xn[:, t, c * P:(c + 1) * P], ident[:])
                    ins.then_inc(xn_turned, 1)

            def turn_y(i):
                pe.wait_ge(yT_ready, i * KT + KT)
                for t in range(TT):
                    for c in range(KT):
                        ins = T(ps[:, 4 + t // 2, (t % 2) * D + c * P:(t % 2) * D + (c + 1) * P],
                                yT[:, c, t * P:(t + 1) * P], ident[:])
                    if t % 2 == 1:
                        ins.then_inc(y_turned, 1)

            pe.wait_ge(consts_loaded, 16)
            pe.wait_ge(masks_loaded, 32)
            turn_xn(0)
            with pe.Fori(0, BATCHES) as b:
                pe.wait_ge(xnT_ready, b * KT + KT)
                k0 = b * STEPS
                for n in range(STEPS + LAST_LAG):
                    if n >= 8:
                        m = n - 8
                        k, s, t = k0 + m, m % 2, m % TT
                        pe.wait_ge(probT_ready, k + 1)
                        if m >= 1:
                            pe.wait_ge(enc_ready, k)
                        parts = (1,) if t == 0 else (0, 1)
                        for part in parts:
                            ins = MM(ps[:, 6, 0:2 * P], raw[:, (m - 1 + part) % RAW_RING, 3 * P:4 * P],
                                     probT[:, s, part::2, :], start=part == parts[0], stop=part == 1)
                        ins.then_inc(attended, 1)
                    if n < STEPS:
                        k, g, t = k0 + n, n // TT, n % TT
                        if n % (2 * TT) == 0:
                            pe.wait_ge(wqkv_loaded[n // (2 * TT)], 16)
                        if n >= 2:
                            pe.wait_ge(squared, k - 1)
                        for c in range(KT):
                            ins = MM(ps[:, n % 2, :], xnT[:, c, t * P:(t + 1) * P], wqkv[:, c, g, :],
                                     start=c == 0, stop=c == KT - 1)
                        ins.then_inc(projected, 1)
                    if n == STEPS:
                        pe.wait_ge(squared, k0 + STEPS)
                        turn_xn(b + 1)
                    if 2 <= n < STEPS + 2:
                        m = n - 2
                        k = k0 + m
                        pe.wait_ge(qk_normed, k + 1)
                        if m >= 1:
                            pe.wait_ge(qkT_ready, k)
                        for h in range(3):
                            ins = T(ps[:, 2, h * P:(h + 1) * P], qkn[:, m % 2, h * P:(h + 1) * P], ident[:])
                        ins.then_inc(qk_turned, 1)
                    if 3 <= n < STEPS + 3:
                        m = n - 3
                        k, s, t = k0 + m, m % 2, m % TT
                        pe.wait_ge(qkT_ready, k + 1)
                        if m >= 2:
                            pe.wait_ge(prob_ready, k - 1)
                        bank = ps[:, 3 + s, :].rearrange("p (h f) -> p h f", h=2)
                        if t == 0:
                            MM(bank[:, :, 0:P], ident_b[:], window[:, :, 1, :], start=True, stop=False,
                               skip_group_check=True)
                        else:
                            MM(ps[:, 3 + s, :], ident_b[:], window[:].rearrange("p h a f -> p (h a f)"),
                               start=True, stop=False, skip_group_check=True)
                        for h in range(2):
                            for part in ((1,) if t == 0 else (0, 1)):
                                at = 0 if t == 0 else part * P
                                ins = MM(bank[:, h, at:at + P], qkT[:, m % QK_RING, h, :],
                                         qkT[:, (m - 1 + part) % QK_RING, 2, :], start=False,
                                         stop=h == 1 and part == 1, skip_group_check=True)
                        ins.then_inc(scored, 1)
                    if 6 <= n < STEPS + 6:
                        m = n - 6
                        k, s, t = k0 + m, m % 2, m % TT
                        pe.wait_ge(probn_ready, k + 1)
                        if m >= 1:
                            pe.wait_ge(probT_ready, k)
                        for h in range(2):
                            for part in ((1,) if t == 0 else (0, 1)):
                                at = 0 if t == 0 else part * P
                                ins = T(ps[:, 5, (2 * h + part) * P:(2 * h + part + 1) * P],
                                        probn[:, s, h, at:at + P], ident[:])
                        ins.then_inc(prob_turned, 1)
                pe.wait_ge(wo0_loaded, 16)
                pe.wait_ge(enc_ready, k0 + STEPS)
                for t in range(TT):
                    if t >= 2:
                        pe.wait_ge(out0_added, b * TT + t - 1)
                    for h in range(HEADS0):
                        ins = MM(ps[:, 5 + t % 2 * 2, 0:D], encT[:, h, t * P:(t + 1) * P], wo0[:, h, :],
                                 start=h == 0, stop=h == HEADS0 - 1)
                    ins.then_inc(out0_ready, 1)
                pe.wait_ge(out0_added, b * TT + TT)

            pe.wait_ge(wb_loaded, 2 * 16)
            with pe.Fori(0, BATCHES) as b:
                pe.wait_ge(xnT_ready, (b + BATCHES) * KT + KT)
                for t in range(TT):
                    for c in range(KT):
                        ins = MM(ps[:, 7, t * EXPERTS:(t + 1) * EXPERTS], xnT[:, c, t * P:(t + 1) * P], gate[:, c, :],
                                 start=c == 0, stop=c == KT - 1)
                ins.then_inc(logits_ready, 1)
                for j in range(FT + 2):
                    k = b * FT + j
                    if j < FT:
                        if j % W1_PIECE == 0:
                            pe.wait_ge(w1_loaded[j // W1_PIECE], 16)
                        if j >= 2:
                            pe.wait_ge(gated_ready, k - 1)
                        for half in range(2):
                            for c in range(KT):
                                ins = MM(ps[:, 2 * half + j % 2, :], w1moe[:, j, c, half, :], xnT[:, c, :],
                                         start=c == 0, stop=c == KT - 1)
                        ins.then_inc(gu_ready, 1)
                    if j == FT:
                        pe.wait_ge(gated_ready, b * FT + FT)
                        turn_xn(b + BATCHES + 1)
                    if j == 1:
                        pe.wait_ge(route_step, b * ROUTE + 4 + 16)
                        for t in range(TT):
                            ins = T(ps[:, 6, t * P:(t + 1) * P], comb[:, t, :], ident[:])
                        ins.then_inc(comb_turned, 1)
                        pe.wait_ge(route_step, b * ROUTE + 4 + ROUTE)
                        pe.wait_ge(sel_loaded, 16)
                    if 1 <= j <= FT:
                        if j >= 2:
                            pe.wait_ge(act_ready, k - 1)
                        MM(ps[:, 6, :], sel[:, j - 1, :], cpieces[:], start=True, stop=True).then_inc(c_ready, 1)
                    if j >= 2:
                        m = j - 2
                        pe.wait_ge(act_ready, k - 1)
                        for c in range(KT):
                            ins = MM(ps[:, 4 + c, :], w2moe[:, m, c * P:(c + 1) * P], moe_act[:, m % 3, :],
                                     start=m == 0, stop=m == FT - 1)
                        ins.then_inc(y_used, 1)
                turn_y(b)
                pe.wait_ge(y_added, b * TT + TT)

            pe.wait_ge(wc_loaded, 7 * 16)
            pe.wait_ge(c_consts_ready, 1)
            with pe.Fori(0, BATCHES) as b:
                pe.wait_ge(xnT_ready, (b + 2 * BATCHES) * KT + KT)
                for t in range(TT):
                    if t >= 2:
                        pe.wait_ge(v_kept, b * TT + t - 1)
                    for c in range(KT):
                        ins = MM(ps[:, t % 2, :], xnT[:, c, t * P:(t + 1) * P], wv1[:, c, :],
                                 start=c == 0, stop=c == KT - 1)
                    ins.then_inc(v_ready, 1)
                pe.wait_ge(v_kept, b * TT + TT)
                for n in range(PAIRS + 4):
                    kb, kq = b * PAIRS, b * (PAIRS // 2)
                    for i in range(2 * TT + 2):
                        if n == PAIRS + 1 and i == 0:
                            pe.wait_ge(qk1_stacked, 2 * (kb + PAIRS))
                            turn_xn(b + 2 * BATCHES + 1)
                        if 1 <= n <= PAIRS and i < 2 * TT:
                            m = n - 1
                            k = kb + m
                            h, t = i // TT, i % TT
                            rows = slice(64 * h, 64 * h + 64)
                            if i == 0:
                                pe.wait_ge(qk1_stacked, 2 * (k + 1))
                            if m >= 1 or i >= 2:
                                pe.wait_ge(s1_max, k * 2 * TT + i - 1)
                            MM(ps[:, 2 + i % 2, :], qst[rows, m % 2, t * P:(t + 1) * P], kst[rows, m % 3, :],
                               start=True, stop=True).then_inc(s1_ready, 1)
                        if i == 0 and 2 <= n <= PAIRS + 1:
                            m = n - 2
                            k = kb + m
                            pe.wait_ge(s1_max, (k + 1) * 2 * TT)
                            if m >= 1:
                                pe.wait_ge(qsm_ready, k)
                            for t in range(TT):
                                ins = T(ps[:, 7, t * P:(t + 1) * P], nm1[:, m % 2, t, :], ident[:])
                            ins.then_inc(m_turned, 1)
                        if n < PAIRS and i < 2 * KT:
                            k = kb + n
                            if n >= 1 and i == 0:
                                pe.wait_ge(qk1_stacked, 2 * k)
                            bank, c = i // KT, i % KT
                            ins = MM(ps[:, bank, :], (wq1, wk1)[bank][:, c, n, :], xnT[:, c, :],
                                     start=c == 0, stop=c == KT - 1)
                            if i == 2 * KT - 1:
                                ins.then_inc(qk1_ready, 1)
                        if 2 <= n <= PAIRS + 1 and i >= 2:
                            m, e = n - 2, i - 2
                            k = kb + m
                            h, t = e // TT, e % TT
                            rows = slice(64 * h, 64 * h + 64)
                            if e == 0:
                                pe.wait_ge(qsm_ready, k + 1)
                            if m >= 1 or e >= 2:
                                pe.wait_ge(p1_ready, k * 2 * TT + e - 1)
                            MM(ps[:, 4 + e % 2, :], kst[rows, m % 3, t * P:(t + 1) * P], qsm[rows, m % 2, :],
                               start=True, stop=True).then_inc(st_ready, 1)
                        if n >= 4 and n % 2 == 0 and 4 <= i < 4 + TT:
                            u, c = (n - 4) // 2, i - 4
                            if c == 0:
                                pe.wait_ge(p1_ready, (kb + 2 * u + 2) * 2 * TT)
                                if u >= 1:
                                    pe.wait_ge(o1_normed, b * NORMED + u)
                            for h in range(4):
                                col = (4 * u + h) * VW
                                ins = MM(ps[VW * h:VW * (h + 1), 6, :], v1[:, c, col:col + VW],
                                         pT1[:, u % 2, h, c, :], start=c == 0, stop=c == TT - 1,
                                         tile_position=(0, VW * h), skip_group_check=True)
                            if c == TT - 1:
                                ins.then_inc(o1_ready, 1)
                        if n >= 5 and n % 2 == 1 and i == 3:
                            u = (n - 5) // 2
                            pe.wait_ge(oT1_kept, kq + u + 1)
                            for t in range(TT):
                                ins = T(ps[:, 6, t * P:(t + 1) * P], oT1[:, u % 2, t * P:(t + 1) * P], ident[:])
                            ins.then_inc(o1_turned, 1)
                pe.wait_ge(o1_normed, b * NORMED + PAIRS // 2)
                pe.wait_ge(xnT_ready, (b + 2 * BATCHES + 2) * KT)
                for c in range(KT):
                    for t in range(TT):
                        ins = T(ps[:, c, t * P:(t + 1) * P], otok[:, t, c * P:(c + 1) * P], ident[:])
                ins.then_inc(on_turned, 1)
                pe.wait_ge(oTn_ready, b * KT + KT)
                for t in range(TT):
                    for c in range(KT):
                        ins = MM(ps[:, 2 + t, 0:D], oTn[:, c, t * P:(t + 1) * P],
                                 wo1[:, c, :], start=c == 0, stop=c == KT - 1)
                    ins.then_inc(out1_ready, 1)
                pe.wait_ge(out1_added, b * TT + TT)

            pe.wait_ge(quant_step, 3)
            MM(ps[:, 6, 0:2], ones[:], wabs[:], start=True, stop=True).then_inc(wabs_summed, 1)
            pe.wait_ge(quantized, 2)
            with pe.Fori(0, BATCHES) as b:
                pe.wait_ge(xnT_ready, (b + 3 * BATCHES) * KT + KT)
                for f in range(HT + 1):
                    k = b * HT + f
                    if f < HT:
                        if f >= 2:
                            pe.wait_ge(h_act, k - 1)
                        for c in range(KT):
                            ins = MM(ps[:, 2 + f % 2, :], wt1[:, c, f * P:(f + 1) * P], xnT[:, c, :],
                                     start=c == 0, stop=c == KT - 1)
                        ins.then_inc(h_ready, 1)
                    if f == HT:
                        turn_xn(b + 3 * BATCHES + 1)
                    if f >= 1:
                        m = f - 1
                        pe.wait_ge(h_act, k)
                        for c in range(KT):
                            ins = MM(ps[:, 6 + c, :], wt2[:, m, c * P:(c + 1) * P], hact[:, m % 3, :],
                                     start=m == 0, stop=m == HT - 1)
                        ins.then_inc(h_used, 1)
                turn_y(b + BATCHES)
                pe.wait_ge(y_added, (b + BATCHES) * TT + TT)


def kernel(**inputs):
    import numpy as np
    import concourse.bacc as bacc
    from concourse.bass_utils import run_bass_kernel_spmd as run

    def tiles(a, k):
        return np.ascontiguousarray(a.reshape(k, P, -1).transpose(1, 0, 2))

    g = {k: np.asarray(v) for k, v in inputs.items()}
    arrays = {"x": g["L0_attn_x"], "qs": g["L0_attn_q_norm_scale"], "ks": g["L0_attn_k_norm_scale"]}

    q, kv = g["L0_attn_q_kernel"], g["L0_attn_kv_kernel"]
    w = np.zeros((P, KT, GROUPS, 4, P), np.float32)
    for grp in range(GROUPS):
        for i, head in enumerate((q[2 * grp], q[2 * grp + 1], kv[0, grp], kv[1, grp])):
            w[:, :, grp, i, :] = tiles(head, KT)
    arrays["wqkv"] = w.reshape(P, KT, GROUPS, 4 * P)
    arrays["wo0"] = np.ascontiguousarray(g["L0_attn_out_kernel"].transpose(1, 0, 2))

    w1, w2 = g["L0_ffn_w1"], g["L0_ffn_w2"]
    s1, s2 = g["L0_ffn_shared_w1"], g["L0_ffn_shared_w2"]
    up = np.zeros((2, FT * P, D), np.float32)
    down = np.zeros((FT * P, D), np.float32)
    for half in range(2):
        up[half, 0:EXPERTS * INTER] = w1[:, half * INTER:(half + 1) * INTER, :].reshape(-1, D)
        up[half, EXPERTS * INTER:FEATS] = s1[half * SHARED:(half + 1) * SHARED]
    down[0:EXPERTS * INTER] = w2.transpose(0, 2, 1).reshape(-1, D)
    down[EXPERTS * INTER:FEATS] = s2.T
    arrays["w1moe"] = np.ascontiguousarray(up.reshape(2, FT, P, KT, P).transpose(4, 1, 3, 0, 2))
    arrays["w2moe"] = tiles(down, FT)
    arrays["gate"] = tiles(g["L0_ffn_gate_w"].T, KT)

    for name, src in (("wq1", g["L1_attn_Wq"]), ("wk1", g["L1_attn_Wk"])):
        w = np.zeros((D, HEADS1, 4, HD1), np.float32)
        w[:, :, 0:3, :] = src.reshape(D, HEADS1, 1, HD1)
        arrays[name] = tiles(w.reshape(D, -1), KT).reshape(P, KT, PAIRS, P)
    w = np.zeros((D, HEADS1, VW), np.float32)
    w[:, :, 0:HD1] = g["L1_attn_Wv"].reshape(D, HEADS1, HD1)
    arrays["wv1"] = tiles(w.reshape(D, -1), KT)
    arrays["wo1"] = tiles(g["L1_attn_Wo"], KT)
    arrays["bo1"] = g["L1_attn_bo"]
    arrays["wm1"] = tiles(g["L1_ffn_w1"].T, KT)
    arrays["wm2"] = tiles(g["L1_ffn_w2"].T, HT)
    arrays["b1m"] = np.ascontiguousarray(g["L1_ffn_b1"].reshape(HT, P).T)
    arrays["b2m"] = np.ascontiguousarray(g["L1_ffn_b2"].reshape(KT, P).T)

    arrays["c_ident"] = np.eye(P, dtype=np.float32)
    frac = np.arange(0, HD0, 2, dtype=np.float32) / np.float32(HD0)
    angle = np.arange(SEQ, dtype=np.float32)[:, None] / np.float32(10000.0) ** frac
    cos, sin = np.cos(angle), np.sin(angle)
    arrays["c_cos"] = tiles(np.concatenate([cos, cos], 1), TT)
    arrays["c_sin"] = tiles(np.concatenate([-sin, sin], 1), TT)
    qi, kj = np.arange(P)[:, None], np.arange(P)[None, :]
    masks = np.where(np.stack([kj > qi, kj <= qi], 1), np.float32(0), np.float32(-1e30))
    arrays["c_window"] = np.ascontiguousarray(np.broadcast_to(masks[:, None], (P, 2, 2, P)))
    feat = np.arange(FT * P)
    owner = np.where(feat < EXPERTS * INTER, feat // INTER, EXPERTS)
    sel = np.zeros((3, PIECE, FT * P), np.float32)
    sel[:, owner[feat < FEATS], feat[feat < FEATS]] = 1.0
    arrays["c_sel"] = sel.reshape(3 * PIECE, FT, P)
    vones = np.zeros((P, HEADS1, VW), np.float32)
    vones[:, :, HD1] = 1.0
    arrays["c_vones"] = vones.reshape(P, -1)
    stack = np.zeros((2, 64, 4), np.float32)
    stack[:, 2 * HD1:3 * HD1, 0] = -1.0
    stack[:, HD1:2 * HD1, 1] = -1.0
    stack[:, MAX_ROW, 1:3] = 1.0
    arrays["c_stack"] = stack.reshape(P, 4)

    nc = bacc.Bacc("TRN2", target_bir_lowering=False, num_devices=1)
    feeds, dram = {}, {}
    for name, a in arrays.items():
        a = np.ascontiguousarray(a)
        feeds[f"in_{name}"] = a
        dram[name] = nc.dram_tensor(f"in_{name}", a.shape, mybir.dt.from_np(a.dtype), kind="ExternalInput").ap()
    out = nc.dram_tensor("out_x", (BATCHES, SEQ, D), F32, kind="ExternalOutput").ap()
    build(nc, dram, out)
    result = run(nc, [feeds], core_ids=[0])
    return result.results[0]["out_x"]
```

```python
from contextlib import ExitStack

import concourse.bass as bass
from concourse import mybir

F32 = mybir.dt.float32
F32R = mybir.dt.float32r
BF16 = mybir.dt.bfloat16
ALU = mybir.AluOpType
ACT = mybir.ActivationFunctionType
AX = mybir.AxisListType

P = 128
BATCHES, SEQ, D = 4, 512, 256
TT = SEQ // P
KT = D // P
NTILES = BATCHES * TT
LN_EPS = 1e-5

HEADS0, KV0, HD0 = 16, 8, 128
RMS_EPS = 1e-6
ATTN_SCALE0 = 0.08838834764831845
GROUPS = KV0
STEPS = GROUPS * TT
RAW_RING, QK_RING = 9, 4
LAST_LAG = 8

EXPERTS, INTER, TOP_K, SHARED = 16, 176, 6, 352
FEATS = EXPERTS * INTER + SHARED
FT = -(-FEATS // P)
PIECE = 32

HEADS1, HD1 = 16, 16
PAIRS = HEADS1 // 2
VW = 32
MAX_ROW = 48
SCALE1 = 0.25

DFF = 1024
HT = DFF // P
ROUTE = 22
QUANT_EPS = 1e-8


def build(nc, dram, out):
    with ExitStack() as ctx:
        def sem(name):
            return ctx.enter_context(nc.semaphore(name))

        def sb(name, shape, dt=F32, where=None):
            return (where or ctx).enter_context(nc.sbuf_tensor(name, shape, dt))

        ps = ctx.enter_context(nc.psum_tensor("ps", [P, 8, 512], F32))

        x_res = sb("x_res", [P, NTILES, D])
        xn = sb("xn", [P, TT, D])
        xnT = [sb(f"xnT_{part}", [P, KT, SEQ], F32R) for part in ("hi", "lo")]
        yT = sb("yT", [P, KT, SEQ])
        ident = sb("ident", [P, P])
        bn_st = sb("bn_st", [P, TT, 6])
        bn_mv = sb("bn_mv", [P, TT, 2])
        ln_ve = sb("ln_ve", [P, TT])
        ln_rs = sb("ln_rs", [P, TT])
        minus_half = sb("minus_half", [P, 16])
        eps_sum = sb("eps_sum", [P, 3])
        spare = sb("spare", [P, 2])

        part_a = ExitStack()
        wqkv = [sb(f"wqkv_{part}", [P, GROUPS, KT, 4 * P], F32R, part_a) for part in ("hi", "lo")]
        wo0 = sb("wo0", [P, HEADS0, D], where=part_a)
        ident_b = sb("ident_b", [P, P], BF16, part_a)
        window = sb("window", [P, 2, 2, P], BF16, part_a)
        qks = sb("qks", [P, 3, P], where=part_a)
        cos3 = sb("cos3", [P, TT, 3, P], where=part_a)
        sin3 = sb("sin3", [P, TT, 3, P], where=part_a)
        raw = sb("raw", [P, RAW_RING, 4 * P], where=part_a)
        ssum = sb("ssum", [P, 2, 3], where=part_a)
        msq = sb("msq", [P, 2, 3], where=part_a)
        rms = sb("rms", [P, 2, 3], where=part_a)
        rope1 = sb("rope1", [P, 2, 3 * P], where=part_a)
        rope2 = sb("rope2", [P, 2, 3 * P], where=part_a)
        qkn = sb("qkn", [P, 2, 3 * P], where=part_a)
        qkT = sb("qkT", [P, QK_RING, 3, P], where=part_a)
        nmax = sb("nmax", [P, 2, 2], where=part_a)
        psums = sb("psums", [P, 2, 2], where=part_a)
        rsums = sb("rsums", [P, 2, 2], where=part_a)
        prob = sb("prob", [P, 2, 2, 2 * P], where=part_a)
        probn = sb("probn", [P, 2, 2, 2 * P], where=part_a)
        probT = sb("probT", [P, 2, 4, P], where=part_a)
        encT = sb("encT", [P, HEADS0, SEQ], where=part_a)
        wqkv_in = encT[:].rearrange("p (g c) f -> p g c f", g=GROUPS)
        cos_in, sin_in = (yT[:, i, :].rearrange("p (t f) -> p t f", t=TT) for i in range(2))
        sq = rope2
        part_a.close()

        part_b = ExitStack()
        w1moe = [sb(f"w1moe_{part}", [P, FT, KT, 2, P], F32R, part_b) for part in ("hi", "lo")]
        w2moe = [sb(f"w2moe_{part}", [P, FT, D], F32R, part_b) for part in ("hi", "lo")]
        gate_in = sb("gate_in", [P, KT, EXPERTS], where=part_b)
        gate = [sb(f"gate_{part}", [P, KT, EXPERTS], F32R, part_b) for part in ("hi", "lo")]
        w2_in = sb("w2_in", [P, 2, D], where=part_b)
        w1_in = yT[:].rearrange("p s (c h f) -> p s c h f", c=KT, h=2)
        sel = sb("sel", [3 * PIECE, FT, P], BF16, part_b)
        lg = sb("lg", [P, TT, EXPERTS], where=part_b)
        gmax = sb("gmax", [P, TT], where=part_b)
        gexp = sb("gexp", [P, TT, EXPERTS], where=part_b)
        gsum = sb("gsum", [P, TT], where=part_b)
        ginv = sb("ginv", [P, TT], where=part_b)
        gprob = sb("gprob", [P, TT, EXPERTS + 2], where=part_b)
        gtop = sb("gtop", [P, TT, 8], where=part_b)
        gmark = sb("gmark", [P, TT, EXPERTS + 2], where=part_b)
        gmask = sb("gmask", [P, TT, EXPERTS], where=part_b)
        comb = sb("comb", [P, TT, PIECE], where=part_b)
        cT, cTr = (xn[0:PIECE, 2 * i:2 * i + 2, :].rearrange("p a d -> p (a d)") for i in range(2))
        cpieces = sb("cpieces", [3 * PIECE, SEQ], BF16, part_b)
        sg = sb("sg", [P, 2, SEQ], where=part_b)
        moe_act = [sb(f"moe_act_{part}", [P, 2, SEQ], F32R, part_b) for part in ("hi", "lo")]
        part_b.close()

        part_c = ExitStack()
        THIRDS = (PAIRS * P, PAIRS * P, HEADS1 * VW)
        WC = KT * sum(THIRDS)
        wc = [sb(f"wc_{part}", [P, WC], F32R, part_c) for part in ("hi", "lo")]
        wq1 = [w[:, 0:KT * THIRDS[0]].rearrange("p (c n f) -> p c n f", c=KT, f=P) for w in wc]
        wk1 = [w[:, KT * THIRDS[0]:2 * KT * THIRDS[0]].rearrange("p (c n f) -> p c n f", c=KT, f=P) for w in wc]
        wv1 = [w[:, 2 * KT * THIRDS[0]:WC].rearrange("p (c f) -> p c f", c=KT) for w in wc]
        wo1 = sb("wo1", [P, KT, D], where=part_c)
        bo1 = sb("bo1", [P, D], where=part_c)
        vones = sb("vones", [P, HEADS1 * VW], where=part_c)
        stack = sb("stack", [P, 4], where=part_c)
        v1 = sb("v1", [P, TT, HEADS1 * VW], where=part_c)
        qhi = sb("qhi", [P, 2, SEQ], F32R, part_c)
        khi = sb("khi", [P, 2, SEQ], F32R, part_c)
        qst = sb("qst", [P, 2, SEQ], F32R, part_c)
        kst = sb("kst", [P, 4, SEQ], F32R, part_c)
        qsm = sb("qsm", [P, 2, SEQ], F32R, part_c)
        nm1 = sb("nm1", [P, 2, TT, P], where=part_c)
        pT1 = sb("pT1", [P, 2, 4, TT, SEQ], where=part_c)
        wc_in = pT1[:].rearrange("p s h c f -> p (s h c f)")[:, 0:WC]
        oT1 = sb("oT1", [P, 2, SEQ], where=part_c)
        oinv = sb("oinv", [P, 2, TT, 4], where=part_c)
        otok = sb("otok", [P, TT, D], where=part_c)
        oTn = sb("oTn", [P, KT, SEQ], where=part_c)
        part_c.close()
        part_d = ExitStack()
        wm1 = sb("wm1", [P, KT, DFF], where=part_d)
        wm2 = sb("wm2", [P, HT, D], where=part_d)
        wneg = sb("wneg", [P, 2, KT * DFF], where=part_d)
        wt1 = sb("wt1", [P, KT, DFF], F32R, part_d)
        wt2 = sb("wt2", [P, HT, D], F32R, part_d)
        ones = sb("ones", [P, P], where=part_d)
        wabs = sb("wabs", [P, 2], where=part_d)
        wscl = sb("wscl", [P, 2], where=part_d)
        whalf = sb("whalf", [P, 2], where=part_d)
        wmhalf = sb("wmhalf", [P, 2], where=part_d)
        b1m = sb("b1m", [P, HT], where=part_d)
        b2m = sb("b2m", [P, KT], where=part_d)
        hact = sb("hact", [P, 2, SEQ], where=part_d)
        hact2 = [sb(f"hact_{part}", [P, 2, SEQ], F32R, part_d) for part in ("hi", "lo")]
        part_d.close()

        x_loaded = sem("x_loaded")
        consts_loaded = sem("consts_loaded")
        tables_loaded = sem("tables_loaded")
        wqkv_loaded = [sem(f"wqkv_loaded{i}") for i in range(GROUPS // 2)]
        wo0_loaded = sem("wo0_loaded")
        wb_loaded = sem("wb_loaded")
        sel_loaded = sem("sel_loaded")
        moe_loaded = [sem(f"moe_loaded{i}") for i in range(2)]
        moe_high, moe_split = sem("moe_high"), sem("moe_split")
        gate_high, gate_split = sem("gate_high"), sem("gate_split")
        wqkv_high, wqkv_split = sem("wqkv_high"), sem("wqkv_split")
        wc_high, wc_split = sem("wc_high"), sem("wc_split")
        wc_loaded = sem("wc_loaded")
        wd_loaded = sem("wd_loaded")
        masks_loaded = sem("masks_loaded")
        out_stored = sem("out_stored")
        half_set = sem("half_set")
        ln_stats, ln_aggr, ln_var = sem("ln_stats"), sem("ln_aggr"), sem("ln_var")
        ln_rstd, xn_ready = sem("ln_rstd"), sem("xn_ready")
        xn_turned, xnT_high, xnT_ready = sem("xn_turned"), sem("xnT_high"), sem("xnT_ready")
        tables_scaled = sem("tables_scaled")
        projected, raw_kept, squared = sem("projected"), sem("raw_kept"), sem("squared")
        summed, meaned, rms_ready = sem("summed"), sem("meaned"), sem("rms_ready")
        roped, rotated, qk_normed = sem("roped"), sem("rotated"), sem("qk_normed")
        qk_turned, qkT_ready = sem("qk_turned"), sem("qkT_ready")
        scored, max_ready, prob_ready = sem("scored"), sem("max_ready"), sem("prob_ready")
        inv_ready, probn_ready = sem("inv_ready"), sem("probn_ready")
        prob_turned, probT_ready = sem("prob_turned"), sem("probT_ready")
        attended, enc_ready = sem("attended"), sem("enc_ready")
        out0_ready, out0_added = sem("out0_ready"), sem("out0_added")
        logits_ready, route_step = sem("logits_ready"), sem("route_step")
        comb_turned, comb_step = sem("comb_turned"), sem("comb_step")
        gate_exp = sem("gate_exp")
        gu_ready, silu_ready, gated_ready = sem("gu_ready"), sem("silu_ready"), sem("gated_ready")
        c_ready, weighted = sem("c_ready"), sem("weighted")
        act_high, act_ready, y_used = sem("act_high"), sem("act_ready"), sem("y_used")
        yT_ready, y_turned, y_added = sem("yT_ready"), sem("y_turned"), sem("y_added")
        c_consts_ready = sem("c_consts_ready")
        v_ready, v_kept = sem("v_ready"), sem("v_kept")
        qk1_ready, qk1_hi, qk1_stacked = sem("qk1_ready"), sem("qk1_hi"), sem("qk1_stacked")
        s1_ready, s1_max = sem("s1_ready"), sem("s1_max")
        m_turned, qsm_ready = sem("m_turned"), sem("qsm_ready")
        st_ready, p1_ready = sem("st_ready"), sem("p1_ready")
        o1_ready, oT1_kept, o1_turned = sem("o1_ready"), sem("oT1_kept"), sem("o1_turned")
        o1_inv, o1_normed = sem("o1_inv"), sem("o1_normed")
        on_turned, oTn_ready, out1_ready = sem("on_turned"), sem("oTn_ready"), sem("out1_ready")
        out1_summed, out1_added = sem("out1_summed"), sem("out1_added")
        quant_step, wabs_summed, quantized = sem("quant_step"), sem("wabs_summed"), sem("quantized")
        h_ready, h_act, h_high, h_split, h_used = (
            sem("h_ready"), sem("h_act"), sem("h_high"), sem("h_split"), sem("h_used"))

        block = ctx.enter_context(nc.Block())

        def wait(eng, s, value):
            if not (isinstance(value, int) and value <= 0):
                eng.wait_ge(s, value)

        @block.sync
        def _(sp):
            sp.dma_start(ident[:], dram["c_ident"]).then_inc(consts_loaded, 16)
            sp.dma_start(x_res[:], dram["x"].rearrange("b (t p) d -> p (b t) d", p=P)).then_inc(x_loaded, 16)
            for i in range(GROUPS // 2):
                sp.dma_start(wqkv_in[:, 2 * i:2 * i + 2], dram["wqkv"][:, 2 * i:2 * i + 2]
                             ).then_inc(wqkv_loaded[i], 16)
                if i == 0:
                    sp.dma_start(qks[:, 0:2, :], dram["qs"].unsqueeze(0).unsqueeze(0).to_broadcast((P, 2, P))
                                 ).then_inc(tables_loaded, 16)
                    sp.dma_start(qks[:, 2, :], dram["ks"].unsqueeze(0).to_broadcast((P, P))
                                 ).then_inc(tables_loaded, 16)
                    sp.dma_start(cos_in, dram["c_cos"]).then_inc(tables_loaded, 16)
                    sp.dma_start(sin_in, dram["c_sin"]).then_inc(tables_loaded, 16)
            sp.dma_start(wo0[:], dram["wo0"]).then_inc(wo0_loaded, 16)
            wait(sp, out0_added, BATCHES * TT)
            sp.dma_start(gate_in[:], dram["gate"]).then_inc(wb_loaded, 16)
            for j in range(FT):
                if j >= 2:
                    sp.wait_ge(moe_split, j - 1)
                sp.dma_start(w1_in[:, j % 2], dram["w1moe"][:, j]).then_inc(moe_loaded[j % 2], 16)
                sp.dma_start(w2_in[:, j % 2, :], dram["w2moe"][:, j]).then_inc(moe_loaded[j % 2], 16)
            wait(sp, y_added, BATCHES * TT)
            sp.dma_start(wc_in, dram["wc"]).then_inc(wc_loaded, 16)
            for name, dst in (("wo1", wo1), ("c_vones", vones), ("c_stack", stack)):
                sp.dma_start(dst[:], dram[name]).then_inc(wc_loaded, 16)
            sp.dma_start(bo1[:], dram["bo1"].unsqueeze(0).to_broadcast((P, D))).then_inc(wc_loaded, 16)
            wait(sp, out1_added, BATCHES * 2)
            for name, dst in (("wm1", wm1), ("wm2", wm2), ("b1m", b1m), ("b2m", b2m)):
                sp.dma_start(dst[:], dram[name]).then_inc(wd_loaded, 16)
            for b in range(BATCHES):
                sp.wait_ge(y_added, (BATCHES + b + 1) * TT)
                sp.dma_start(out[b].rearrange("(t p) d -> p t d", p=P),
                             x_res[:, b * TT:(b + 1) * TT, :]).then_inc(out_stored, 16)
            sp.wait_ge(out_stored, 16 * BATCHES)

        @block.gpsimd
        def _(pool):
            nc.gpsimd.memset(minus_half[:], -0.5).then_inc(half_set, 1)
            nc.gpsimd.memset(eps_sum[:], HD0 * RMS_EPS).then_inc(half_set, 1)
            pool.dma_start(ident_b[:], dram["c_ident"]).then_inc(masks_loaded, 16)
            pool.dma_start(window[:], dram["c_window"]).then_inc(masks_loaded, 16)
            pool.wait_ge(half_set, 2)

            def rstd(i):
                pool.wait_ge(ln_var, i + 1)
                nc.gpsimd.tensor_tensor(ln_rs[:], ln_ve[:], minus_half[:, 0:TT], ALU.pow).then_inc(ln_rstd, 1)

            rstd(0)
            with pool.Fori(0, BATCHES) as b:
                for n in range(STEPS):
                    if n == STEPS // 2 + 1:
                        rstd(b + 1)
                    k, s = b * STEPS + n, n % 2
                    pool.wait_ge(summed, k + 1)
                    if n >= 2:
                        pool.wait_ge(qk_normed, k - 1)
                    nc.gpsimd.tensor_tensor(msq[:, s, :], ssum[:, s, :], eps_sum[:], ALU.add).then_inc(meaned, 1)
                    pool.wait_ge(meaned, k + 1)
                    nc.gpsimd.tensor_tensor(rms[:, s, :], msq[:, s, :], minus_half[:, 0:3],
                                            ALU.pow).then_inc(rms_ready, 1)
                    pool.wait_ge(roped, k + 1)
                    nc.gpsimd.tensor_tensor(rope1[:, s, :], rope1[:, s, :], rope2[:, s, :],
                                            ALU.add).then_inc(rotated, 1)
            pool.wait_ge(out0_added, BATCHES * TT)
            pool.dma_start(sel[:], dram["c_sel"]).then_inc(sel_loaded, 16)
            for part in range(1, 4):
                with pool.Fori(0, BATCHES) as b:
                    rstd(b + part * BATCHES + 1)

        @block.vector
        def _(dve):
            V = nc.vector

            def x_tile(b, t):
                return x_res[:, bass.ds(b * TT + t, 1), :].rearrange("p a d -> p (a d)")

            def norm_stats(i, b):
                for t in range(TT):
                    V.bn_stats(bn_st[:, t, :], x_tile(b, t)).then_inc(ln_stats, 1)
                dve.wait_ge(ln_stats, i * TT + TT)
                V.memset(spare[:, 0:1], 0.0)
                for t in range(TT):
                    V.bn_aggr(bn_mv[:, t, :], bn_st[:, t, :]).then_inc(ln_aggr, 1)
                dve.wait_ge(ln_aggr, i * TT + TT)
                V.tensor_scalar(ln_ve[:], bn_mv[:, :, 1], LN_EPS, None, ALU.add).then_inc(ln_var, 1)

            def norm_apply(i, b):
                dve.wait_ge(ln_rstd, i + 1)
                dve.wait_ge(xn_turned, i * KT + 1)
                for t in range(TT):
                    V.tensor_scalar(xn[:, t, :], x_tile(b, t), bn_mv[:, t, 0:1], ln_rs[:, t:t + 1],
                                    ALU.subtract, ALU.mult).then_inc(xn_ready, 1)

            def split_xnT(i):
                for c in range(KT):
                    dve.wait_ge(xnT_high, i * KT + c + 1)
                    V.tensor_tensor(xnT[1][:, c, :], ps[:, c, :], xnT[0][:, c, :], ALU.subtract
                                    ).then_inc(xnT_ready, 1)

            V.memset(spare[:, 0:1], 0.0).then_inc(xn_turned, 1)
            dve.wait_ge(tables_loaded, 4 * 16)
            V.tensor_scalar(qks[:, 0:2, :], qks[:, 0:2, :], ATTN_SCALE0 * HD0 ** 0.5, None, ALU.mult
                            ).then_inc(tables_scaled, 1)
            V.tensor_scalar(qks[:, 2, :], qks[:, 2, :], HD0 ** 0.5, None, ALU.mult).then_inc(tables_scaled, 1)
            dve.wait_ge(tables_scaled, 2)
            H2 = HD0 // 2
            for h in range(3):
                sc = qks[:, h:h + 1, :].to_broadcast((P, TT, P))
                lo, hi = sc[:, :, 0:H2], sc[:, :, H2:HD0]
                V.tensor_tensor(cos3[:, :, h, :], cos_in, sc, ALU.mult).then_inc(tables_scaled, 1)
                V.tensor_tensor(sin3[:, :, h, 0:H2], sin_in[:, :, 0:H2], hi, ALU.mult).then_inc(tables_scaled, 1)
                V.tensor_tensor(sin3[:, :, h, H2:HD0], sin_in[:, :, H2:HD0], lo, ALU.mult).then_inc(tables_scaled, 1)
            dve.wait_ge(tables_scaled, 11)

            dve.wait_ge(x_loaded, 16)
            norm_stats(0, 0)
            norm_apply(0, 0)
            split_xnT(0)
            for i in range(GROUPS // 2):
                dve.wait_ge(wqkv_high, i + 1)
                V.tensor_tensor(*(w[:, 2 * i:2 * i + 2].rearrange("p g c f -> p (g c f)")
                                  for w in (wqkv[1], wqkv_in, wqkv[0])), ALU.subtract).then_inc(wqkv_split, 1)
            with dve.Fori(0, BATCHES) as b:
                following = (b + 1) % BATCHES
                for n in range(STEPS + LAST_LAG):
                    k0 = b * STEPS
                    if n == STEPS + 3:
                        split_xnT(b + 1)
                    if n == STEPS // 2:
                        norm_stats(b + 1, following)
                    if n == STEPS // 2 + 2:
                        norm_apply(b + 1, following)
                    if 6 <= n < STEPS + 6:
                        m = n - 6
                        k, s, w = k0 + m, m % 2, (P if m % TT == 0 else 2 * P)
                        dve.wait_ge(prob_ready, k + 1)
                        V.reciprocal(rsums[:, s, :], psums[:, s, :]).then_inc(inv_ready, 1)
                        dve.wait_ge(inv_ready, k + 1)
                        if m >= 2:
                            dve.wait_ge(prob_turned, k - 1)
                        for h in range(2):
                            ins = V.tensor_scalar(probn[:, s, h, 0:w], prob[:, s, h, 0:w], rsums[:, s, h:h + 1],
                                                  None, ALU.mult)
                        ins.then_inc(probn_ready, 1)
                    if 4 <= n < STEPS + 4:
                        m = n - 4
                        k, s, w = k0 + m, m % 2, (P if m % TT == 0 else 2 * P)
                        dve.wait_ge(scored, k + 1)
                        V.tensor_reduce(nmax[:, s, :], ps[:, 3 + s, :].rearrange("p (h f) -> p h f", h=2)[:, :, 0:w],
                                        AX.X, ALU.max, negate=True).then_inc(max_ready, 1)
                    if 7 <= n < STEPS + 7:
                        m = n - 7
                        k, s = k0 + m, m % 2
                        dve.wait_ge(prob_turned, k + 1)
                        if m >= 2:
                            dve.wait_ge(attended, k - 1)
                        kt = slice(1, 4, 2) if m % TT == 0 else slice(0, 4)
                        V.tensor_copy(probT[:, s, kt, :], ps[:, 5, :].rearrange("p (a f) -> p a f", a=4)[:, kt, :]
                                      ).then_inc(probT_ready, 1)
                    if 1 <= n <= STEPS:
                        m = n - 1
                        k, s = k0 + m, m % 2
                        dve.wait_ge(rotated, k + 1)
                        dve.wait_ge(rms_ready, k + 1)
                        if m >= 2:
                            dve.wait_ge(qk_turned, k - 1)
                        V.tensor_tensor(qkn[:, s, :].rearrange("p (h f) -> p h f", h=3),
                                        rope1[:, s, :].rearrange("p (h f) -> p h f", h=3),
                                        rms[:, s, :].unsqueeze(2).to_broadcast((P, 3, P)), ALU.mult
                                        ).then_inc(qk_normed, 1)
                    if n < STEPS:
                        k, s, t = k0 + n, n % 2, n % TT
                        dve.wait_ge(squared, k + 1)
                        if n >= 2:
                            dve.wait_ge(rotated, k - 1)
                            dve.wait_ge(qk_normed, k - 1)
                        V.reduce_sum(ssum[:, s, :], sq[:, s, :].rearrange("p (h f) -> p h f", h=3), AX.X
                                     ).then_inc(summed, 1)
                        r3 = raw[:, n % RAW_RING, 0:3 * P]
                        dve.wait_ge(summed, k + 1)
                        V.tensor_tensor(rope1[:, s, :], r3, cos3[:, t, :, :].rearrange("p h f -> p (h f)"), ALU.mult)
                        rh = r3.rearrange("p (h f) -> p h f", h=3)
                        o2 = rope2[:, s, :].rearrange("p (h f) -> p h f", h=3)
                        V.tensor_tensor(o2[:, :, 0:H2], rh[:, :, H2:HD0], sin3[:, t, :, 0:H2], ALU.mult)
                        V.tensor_tensor(o2[:, :, H2:HD0], rh[:, :, 0:H2], sin3[:, t, :, H2:HD0], ALU.mult
                                        ).then_inc(roped, 1)
                for t in range(TT):
                    dve.wait_ge(out0_ready, b * TT + t + 1)
                    V.tensor_tensor(x_tile(b, t), ps[:, 5 + t % 2 * 2, 0:D], x_tile(b, t), ALU.add
                                    ).then_inc(out0_added, 1)
                dve.wait_ge(out0_added, b * TT + TT)

            def add_turned(i, b):
                for t in range(TT):
                    if t % 2 == 0:
                        dve.wait_ge(y_turned, i * 2 + t // 2 + 1)
                    V.tensor_tensor(x_tile(b, t), ps[:, 4 + t // 2, (t % 2) * D:(t % 2 + 1) * D], x_tile(b, t),
                                    ALU.add).then_inc(y_added, 1)
                dve.wait_ge(y_added, i * TT + TT)

            V.memset(cpieces[:], 0.0).then_inc(route_step, 1)
            V.memset(comb[:], 0.0).then_inc(route_step, 1)
            V.memset(gprob[:], -1.0).then_inc(route_step, 1)
            dve.wait_ge(route_step, 3)
            V.memset(comb[:, :, EXPERTS:EXPERTS + 1], 1.0).then_inc(route_step, 1)
            dve.wait_ge(route_step, 4)
            def experts(b):
                following = (b + 1) % BATCHES
                links = [0]

                def link(ins, wait_now=True):
                    links[0] += 1
                    ins.then_inc(route_step, 1)
                    if wait_now:
                        dve.wait_ge(route_step, b * ROUTE + (4 + links[0]))

                dve.wait_ge(logits_ready, b + 1)
                lps = ps[:, 7, 0:TT * EXPERTS].rearrange("p (t e) -> p t e", t=TT)
                link(V.reduce_max(gmax[:], lps, AX.X))
                link(V.tensor_tensor(lg[:], lps, gmax[:].unsqueeze(2).to_broadcast((P, TT, EXPERTS)), ALU.subtract))
                dve.wait_ge(gate_exp, b + 1)
                link(V.reduce_sum(gsum[:], gexp[:], AX.X))
                link(V.reciprocal(ginv[:], gsum[:]))
                link(V.tensor_tensor(gprob[:, :, 0:EXPERTS], gexp[:],
                                     ginv[:].unsqueeze(2).to_broadcast((P, TT, EXPERTS)), ALU.mult))
                V.memset(spare[:, 1:2], 0.0)
                for t in range(TT):
                    link(V.max(gtop[:, t, :], gprob[:, t, 0:EXPERTS]), t == TT - 1)
                link(V.memset(gtop[:, :, TOP_K:8], -1.0))
                V.memset(spare[:, 1:2], 0.0)
                for t in range(TT):
                    link(V.match_replace(gmark[:, t, :], gtop[:, t, :], gprob[:, t, :], -2.0), t == TT - 1)
                link(V.tensor_scalar(gmask[:], gmark[:, :, 0:EXPERTS], -2.0, None, ALU.is_equal))
                link(V.tensor_tensor(comb[:, :, 0:EXPERTS], gmask[:], gprob[:, :, 0:EXPERTS], ALU.mult))
                dve.wait_ge(comb_turned, b + 1)
                link(V.tensor_copy(cT, ps[0:PIECE, 6, :]))
                link(V.tensor_copy(cpieces[0:PIECE, :], cT))
                link(V.tensor_tensor(cTr, cT, cpieces[0:PIECE, :], ALU.subtract))
                link(V.tensor_copy(cpieces[PIECE:2 * PIECE, :], cTr))
                link(V.tensor_tensor(cT, cTr, cpieces[PIECE:2 * PIECE, :], ALU.subtract))
                link(V.tensor_copy(cpieces[2 * PIECE:3 * PIECE, :], cT))
                assert links[0] == ROUTE, links
                for j in range(FT):
                    k = b * FT + j
                    if isinstance(b, int) and j + 2 < FT:
                        split_moe(j + 2)
                    if j == FT // 2:
                        norm_stats(b + BATCHES + 1, following)
                    if j == FT // 2 + 2:
                        norm_apply(b + BATCHES + 1, following)
                    dve.wait_ge(silu_ready, k + 1)
                    V.tensor_tensor(sg[:, j % 2, :], ps[:, 2 + j % 2, :], sg[:, j % 2, :], ALU.mult
                                    ).then_inc(gated_ready, 1)
                    dve.wait_ge(gated_ready, k + 1)
                    dve.wait_ge(c_ready, k + 1)
                    V.tensor_tensor(sg[:, j % 2, :], ps[:, 6, :], sg[:, j % 2, :], ALU.mult
                                    ).then_inc(weighted, 1)
                    dve.wait_ge(act_high, k + 1)
                    V.tensor_tensor(moe_act[1][:, j % 2, :], sg[:, j % 2, :], moe_act[0][:, j % 2, :], ALU.subtract
                                    ).then_inc(act_ready, 1)
                split_xnT(b + BATCHES + 1)
                add_turned(b, b)

            def split_moe(j):
                dve.wait_ge(moe_high, j + 1)
                V.tensor_tensor(w1moe[1][:, j], w1_in[:, j % 2], w1moe[0][:, j], ALU.subtract)
                V.tensor_tensor(w2moe[1][:, j, :], w2_in[:, j % 2, :], w2moe[0][:, j, :], ALU.subtract
                                ).then_inc(moe_split, 1)

            dve.wait_ge(gate_high, 1)
            V.tensor_tensor(gate[1][:], gate_in[:], gate[0][:], ALU.subtract).then_inc(gate_split, 1)
            split_moe(0)
            split_moe(1)
            experts(0)
            with dve.Fori(1, BATCHES) as b:
                experts(b)

            V.memset(nm1[:], 0.0).then_inc(c_consts_ready, 1)
            dve.wait_ge(c_consts_ready, 1)
            dve.wait_ge(wc_loaded, 5 * 16)
            dve.wait_ge(wc_high, 1)
            V.tensor_tensor(wc[1][:], wc_in, wc[0][:], ALU.subtract).then_inc(wc_split, 1)
            def pair_step(b, n, new, old):
                kb, kq, i_next = b * PAIRS, b * (PAIRS // 2), b + 2 * BATCHES + 1
                valid = lambda m: new if m >= 0 else old
                for i in range(2 * TT):
                    if valid(n - 1):
                        m = n - 1
                        h, t = i // TT, i % TT
                        dve.wait_ge(s1_ready, (kb + m) * 2 * TT + i + 1)
                        col = 64 * h + MAX_ROW
                        V.tensor_reduce(nm1[:, m % 2, t, col:col + 1], ps[:, 2 + i % 2, :], AX.X, ALU.max,
                                        negate=True).then_inc(s1_max, 1)
                    if i == 0 and valid(n - 2):
                        m = n - 2
                        k = kb + m
                        dve.wait_ge(m_turned, k + 1)
                        if old or m >= 2:
                            dve.wait_ge(st_ready, (k - 1) * 2 * TT)
                        V.tensor_tensor(qsm[:, m % 2, :], ps[:, 7, :], qst[:, m % 2, :], ALU.add
                                        ).then_inc(qsm_ready, 1)
                    if i == 5 and new:
                        k = kb + n
                        dve.wait_ge(qk1_hi, 2 * (k + 1))
                        if old or n >= 2:
                            dve.wait_ge(qsm_ready, k - 1)
                        V.scalar_tensor_tensor(qst[:, n % 2, :], qhi[:, n % 2, :], stack[:, 0:1], ps[:, 0, :],
                                               ALU.mult, ALU.add).then_inc(qk1_stacked, 1)
                        if old or n >= 4:
                            dve.wait_ge(st_ready, (k - 3) * 2 * TT)
                        V.scalar_tensor_tensor(kst[:, n % 4, :], khi[:, n % 2, :], stack[:, 1:2], ps[:, 1, :],
                                               ALU.mult, ALU.add).then_inc(qk1_stacked, 1)
                    if i == 5 and n % 2 == 1 and valid((n - 5) // 2):
                        u = (n - 5) // 2
                        c0 = (u % (PAIRS // 2)) * 4 * HD1
                        if u == 0 and old:
                            dve.wait_ge(on_turned, KT * b)
                        dve.wait_ge(o1_turned, kq + u + 1)
                        o4 = ps[:, 6, :].rearrange("p (t h c) -> p t h c", t=TT, h=4)
                        V.reciprocal(oinv[:, u % 2, :, :], o4[:, :, :, HD1]).then_inc(o1_inv, 1)
                        dve.wait_ge(o1_inv, kq + u + 1)
                        V.tensor_tensor(otok[:, :, c0:c0 + 4 * HD1].rearrange("p t (h c) -> p t h c", h=4),
                                        o4[:, :, :, 0:HD1], oinv[:, u % 2, :, :].unsqueeze(3).to_broadcast((P, TT, 4, HD1)),
                                        ALU.mult).then_inc(o1_normed, 1)
                if new and n in (2, 3):
                    for t in (2 * n - 4, 2 * n - 3):
                        dve.wait_ge(v_ready, b * TT + t + 1)
                        V.tensor_tensor(v1[:, t, :], ps[:, t % 2, :], vones[:], ALU.add).then_inc(v_kept, 1)
                if new and n == 4:
                    norm_stats(i_next, (b + 1) % BATCHES)
                if new and n == 6:
                    norm_apply(i_next, (b + 1) % BATCHES)
                if old and n == 5:
                    for half in range(2):
                        xs = x_res[:, bass.ds((b - 1) * TT + 2 * half, 2), :]
                        dve.wait_ge(out1_ready, 2 * b - 1 + half)
                        V.tensor_tensor(xs, ps[:, 7 - half, :].rearrange("p (t d) -> p t d", t=2), xs, ALU.add
                                        ).then_inc(out1_summed, 1)
                        dve.wait_ge(out1_summed, 2 * b - 1 + half)
                        V.tensor_tensor(xs, xs, bo1[:].unsqueeze(1).to_broadcast((P, 2, D)), ALU.add
                                        ).then_inc(out1_added, 1)
                if new and n == PAIRS - 1:
                    split_xnT(i_next)

            for n in range(PAIRS):
                pair_step(0, n, True, False)
            with dve.Fori(1, BATCHES) as b:
                for n in range(PAIRS):
                    pair_step(b, n, True, True)
            for n in range(6):
                pair_step(BATCHES, n, False, True)
            dve.wait_ge(out1_added, 2 * BATCHES)

            V.memset(ones[:], 1.0).then_inc(quant_step, 1)
            dve.wait_ge(wd_loaded, 4 * 16)
            flat = [wm1[:].rearrange("p a f -> p (a f)"), wm2[:].rearrange("p a f -> p (a f)")]
            tern = [wt1[:].rearrange("p a f -> p (a f)"), wt2[:].rearrange("p a f -> p (a f)")]
            for i in range(2):
                V.tensor_reduce(wabs[:, i:i + 1], flat[i], AX.X, ALU.add, apply_absolute_value=True
                                ).then_inc(quant_step, 1)
            dve.wait_ge(wabs_summed, 1)
            V.tensor_scalar(wscl[:], ps[:, 6, 0:2], 1.0 / (DFF * D), QUANT_EPS, ALU.mult, ALU.max
                            ).then_inc(quant_step, 1)
            dve.wait_ge(quant_step, 4)
            V.tensor_scalar(whalf[:], wscl[:], 0.5, None, ALU.mult).then_inc(quant_step, 1)
            V.tensor_scalar(wmhalf[:], wscl[:], -0.5, None, ALU.mult).then_inc(quant_step, 1)
            dve.wait_ge(quant_step, 6)
            for i in range(2):
                V.tensor_scalar(wneg[:, i, :], flat[i], wmhalf[:, i:i + 1], None, ALU.is_lt).then_inc(quant_step, 1)
                dve.wait_ge(quant_step, 7 + i)
                V.scalar_tensor_tensor(tern[i], flat[i], whalf[:, i:i + 1], wneg[:, i, :], ALU.is_gt, ALU.subtract
                                       ).then_inc(quantized, 1)
            with dve.Fori(0, BATCHES) as b:
                with_next = (b + 1) % BATCHES
                norm_stats(b + 3 * BATCHES + 1, with_next)
                norm_apply(b + 3 * BATCHES + 1, with_next)
                for f in range(HT):
                    k, s = b * HT + f, f % 2
                    dve.wait_ge(h_act, k + 1)
                    if f >= 2:
                        dve.wait_ge(h_used, k - 1)
                    V.tensor_copy(hact2[0][:, s, :], hact[:, s, :]).then_inc(h_high, 1)
                    dve.wait_ge(h_high, k + 1)
                    V.tensor_tensor(hact2[1][:, s, :], hact[:, s, :], hact2[0][:, s, :], ALU.subtract
                                    ).then_inc(h_split, 1)
                split_xnT(b + 3 * BATCHES + 1)
                add_turned(b + BATCHES, b)

        @block.scalar
        def _(act):
            A = nc.scalar.activation

            def keep_xnT(i):
                for c in range(KT):
                    act.wait_ge(xn_turned, i * KT + c + 2)
                    A(xnT[0][:, c, :], ps[:, c, :], ACT.Copy).then_inc(xnT_high, 1)

            keep_xnT(0)
            for i in range(GROUPS // 2):
                act.wait_ge(wqkv_loaded[i], 16)
                A(*(w[:, 2 * i:2 * i + 2].rearrange("p g c f -> p (g c f)") for w in (wqkv[0], wqkv_in)), ACT.Copy
                  ).then_inc(wqkv_high, 1)
            act.wait_ge(wqkv_split, GROUPS // 2)
            with act.Fori(0, BATCHES) as b:
                k0 = b * STEPS
                for n in range(STEPS + LAST_LAG):
                    if n < STEPS:
                        k, s = k0 + n, n % 2
                        act.wait_ge(projected, k + 1)
                        A(raw[:, n % RAW_RING, :], ps[:, s, :], ACT.Copy).then_inc(raw_kept, 1)
                        if n >= 2:
                            act.wait_ge(rotated, k - 1)
                        A(sq[:, s, :], ps[:, s, 0:3 * P], ACT.Square).then_inc(squared, 1)
                    if n == STEPS + 2:
                        keep_xnT(b + 1)
                    if n >= 8:
                        m = n - 8
                        g, t = m // TT, m % TT
                        act.wait_ge(attended, k0 + m + 1)
                        A(encT[:, 2 * g:2 * g + 2, t * P:(t + 1) * P],
                          ps[:, 6, 0:2 * P].rearrange("p (h f) -> p h f", h=2), ACT.Copy).then_inc(enc_ready, 1)
                    if 4 <= n < STEPS + 4:
                        m = n - 4
                        k, s, w = k0 + m, m % 2, (P if m % TT == 0 else 2 * P)
                        act.wait_ge(max_ready, k + 1)
                        if m >= 2:
                            act.wait_ge(probn_ready, k - 1)
                        for h in range(2):
                            ins = A(prob[:, s, h, 0:w], ps[:, 3 + s, h * 2 * P:h * 2 * P + w], ACT.Exp,
                                    bias=nmax[:, s, h:h + 1], accum_out=psums[:, s, h:h + 1])
                        ins.then_inc(prob_ready, 1)
                    if 2 <= n < STEPS + 2:
                        m = n - 2
                        act.wait_ge(qk_turned, k0 + m + 1)
                        A(qkT[:, m % QK_RING, :, :], ps[:, 2, 0:3 * P].rearrange("p (h f) -> p h f", h=3), ACT.Copy
                          ).then_inc(qkT_ready, 1)

            def split_moe(j):
                act.wait_ge(moe_loaded[j % 2], 32 * (j // 2 + 1))
                A(w1moe[0][:, j], w1_in[:, j % 2], ACT.Copy)
                A(w2moe[0][:, j, :], w2_in[:, j % 2, :], ACT.Copy).then_inc(moe_high, 1)

            def experts(b):
                act.wait_ge(route_step, b * ROUTE + 4 + 2)
                A(gexp[:], lg[:], ACT.Exp).then_inc(gate_exp, 1)
                for j in range(FT + 1):
                    k = b * FT + j
                    if isinstance(b, int) and j + 2 < FT:
                        split_moe(j + 2)
                    if j < FT:
                        act.wait_ge(gu_ready, k + 1)
                        if j >= 2:
                            act.wait_ge(act_ready, k - 1)
                        A(sg[:, j % 2, :], ps[:, j % 2, :], ACT.Silu).then_inc(silu_ready, 1)
                    if j >= 1:
                        m = j - 1
                        act.wait_ge(weighted, k)
                        if m >= 2:
                            act.wait_ge(y_used, k - 2)
                        A(moe_act[0][:, m % 2, :], sg[:, m % 2, :], ACT.Copy).then_inc(act_high, 1)
                keep_xnT(b + BATCHES + 1)
                act.wait_ge(y_used, b * FT + FT)
                for c in range(KT):
                    A(yT[:, c, :], ps[:, 4 + c, :], ACT.Copy).then_inc(yT_ready, 1)

            act.wait_ge(wb_loaded, 16)
            A(gate[0][:], gate_in[:], ACT.Copy).then_inc(gate_high, 1)
            split_moe(0)
            split_moe(1)
            experts(0)
            with act.Fori(1, BATCHES) as b:
                experts(b)

            act.wait_ge(wc_loaded, 5 * 16)
            A(wc[0][:], wc_in, ACT.Copy).then_inc(wc_high, 1)
            act.wait_ge(wc_split, 1)
            def pair_step(b, n, new, old):
                kb, kq = b * PAIRS, b * (PAIRS // 2)
                valid = lambda m: new if m >= 0 else old
                for i in range(2 * TT):
                    if valid(n - 2):
                        m = n - 2
                        h, c, u = i // TT, i % TT, m // 2
                        if i == 0 and (old or m >= 4):
                            act.wait_ge(o1_ready, kq + u - 1)
                        act.wait_ge(st_ready, (kb + m) * 2 * TT + i + 1)
                        A(pT1[:, u % 2, 2 * (m % 2) + h, c, :], ps[:, 4 + i % 2, :], ACT.Exp, scale=SCALE1
                          ).then_inc(p1_ready, 1)
                    if new and i == 3:
                        k = kb + n
                        act.wait_ge(qk1_ready, k + 1)
                        if old or n >= 2:
                            act.wait_ge(qk1_stacked, 2 * (k - 1))
                        A(qhi[:, n % 2, :], ps[:, 0, :], ACT.Copy).then_inc(qk1_hi, 1)
                        A(khi[:, n % 2, :], ps[:, 1, :], ACT.Identity, bias=stack[:, 2:3]).then_inc(qk1_hi, 1)
                    if old and n == 4 and i in (1, 7):
                        c = i // 7
                        act.wait_ge(on_turned, KT * b - 1 + c)
                        A(oTn[:, c, :], ps[:, 6 + c, :], ACT.Copy).then_inc(oTn_ready, 1)
                if n % 2 == 0 and valid((n - 4) // 2):
                    u = (n - 4) // 2
                    act.wait_ge(o1_ready, kq + u + 1)
                    if old or u >= 2:
                        act.wait_ge(o1_turned, kq + u - 1)
                    A(oT1[:, u % 2, :], ps[:, 6, :], ACT.Copy).then_inc(oT1_kept, 1)
                if new and n == PAIRS - 1:
                    keep_xnT(b + 2 * BATCHES + 1)

            for n in range(PAIRS):
                pair_step(0, n, True, False)
            with act.Fori(1, BATCHES) as b:
                for n in range(PAIRS):
                    pair_step(b, n, True, True)
            for n in range(5):
                pair_step(BATCHES, n, False, True)

            act.wait_ge(wd_loaded, 4 * 16)
            with act.Fori(0, BATCHES) as b:
                for f in range(HT):
                    k = b * HT + f
                    act.wait_ge(h_ready, k + 1)
                    if f >= 2:
                        act.wait_ge(h_split, k - 1)
                    A(hact[:, f % 2, :], ps[:, 2 + f % 2, :], ACT.Gelu, bias=b1m[:, f:f + 1]).then_inc(h_act, 1)
                keep_xnT(b + 3 * BATCHES + 1)
                act.wait_ge(h_used, b * HT + HT)
                for c in range(KT):
                    A(yT[:, c, :], ps[:, 6 + c, :], ACT.Identity, bias=b2m[:, c:c + 1]).then_inc(yT_ready, 1)

        @block.tensor
        def _(pe):
            MM, T = nc.tensor.matmul, nc.tensor.transpose

            def split_product(out, left, right, first, last):
                MM(out, left[0], right[1], start=first, stop=False)
                MM(out, left[1], right[0], start=False, stop=False)
                return MM(out, left[0], right[0], start=False, stop=last)

            def turn_xn(i):
                pe.wait_ge(xn_ready, i * TT + TT)
                for c in range(KT):
                    for t in range(TT):
                        ins = T(ps[:, c, t * P:(t + 1) * P], xn[:, t, c * P:(c + 1) * P], ident[:])
                    ins.then_inc(xn_turned, 1)

            def turn_y(i):
                pe.wait_ge(yT_ready, i * KT + KT)
                for t in range(TT):
                    for c in range(KT):
                        ins = T(ps[:, 4 + t // 2, (t % 2) * D + c * P:(t % 2) * D + (c + 1) * P],
                                yT[:, c, t * P:(t + 1) * P], ident[:])
                    if t % 2 == 1:
                        ins.then_inc(y_turned, 1)

            pe.wait_ge(consts_loaded, 16)
            pe.wait_ge(masks_loaded, 32)
            turn_xn(0)
            with pe.Fori(0, BATCHES) as b:
                pe.wait_ge(xnT_ready, b * KT + KT)
                k0 = b * STEPS
                for n in range(STEPS + LAST_LAG):
                    if n >= 8:
                        m = n - 8
                        k, s, t = k0 + m, m % 2, m % TT
                        pe.wait_ge(probT_ready, k + 1)
                        if m >= 1:
                            pe.wait_ge(enc_ready, k)
                        parts = (1,) if t == 0 else (0, 1)
                        for part in parts:
                            ins = MM(ps[:, 6, 0:2 * P], raw[:, (m - 1 + part) % RAW_RING, 3 * P:4 * P],
                                     probT[:, s, part::2, :], start=part == parts[0], stop=part == 1)
                        ins.then_inc(attended, 1)
                    if n < STEPS:
                        k, g, t = k0 + n, n // TT, n % TT
                        if n % (2 * TT) == 0:
                            pe.wait_ge(wqkv_split, n // (2 * TT) + 1)
                        if n >= 2:
                            pe.wait_ge(squared, k - 1)
                        for c in range(KT):
                            ins = split_product(ps[:, n % 2, :], [x[:, c, t * P:(t + 1) * P] for x in xnT],
                                                [w[:, g, c, :] for w in wqkv], c == 0, c == KT - 1)
                        ins.then_inc(projected, 1)
                    if n == STEPS:
                        pe.wait_ge(squared, k0 + STEPS)
                        turn_xn(b + 1)
                    if 2 <= n < STEPS + 2:
                        m = n - 2
                        k = k0 + m
                        pe.wait_ge(qk_normed, k + 1)
                        if m >= 1:
                            pe.wait_ge(qkT_ready, k)
                        for h in range(3):
                            ins = T(ps[:, 2, h * P:(h + 1) * P], qkn[:, m % 2, h * P:(h + 1) * P], ident[:])
                        ins.then_inc(qk_turned, 1)
                    if 3 <= n < STEPS + 3:
                        m = n - 3
                        k, s, t = k0 + m, m % 2, m % TT
                        pe.wait_ge(qkT_ready, k + 1)
                        if m >= 2:
                            pe.wait_ge(prob_ready, k - 1)
                        bank = ps[:, 3 + s, :].rearrange("p (h f) -> p h f", h=2)
                        if t == 0:
                            MM(bank[:, :, 0:P], ident_b[:], window[:, :, 1, :], start=True, stop=False,
                               skip_group_check=True)
                        else:
                            MM(ps[:, 3 + s, :], ident_b[:], window[:].rearrange("p h a f -> p (h a f)"),
                               start=True, stop=False, skip_group_check=True)
                        for h in range(2):
                            for part in ((1,) if t == 0 else (0, 1)):
                                at = 0 if t == 0 else part * P
                                ins = MM(bank[:, h, at:at + P], qkT[:, m % QK_RING, h, :],
                                         qkT[:, (m - 1 + part) % QK_RING, 2, :], start=False,
                                         stop=h == 1 and part == 1, skip_group_check=True)
                        ins.then_inc(scored, 1)
                    if 6 <= n < STEPS + 6:
                        m = n - 6
                        k, s, t = k0 + m, m % 2, m % TT
                        pe.wait_ge(probn_ready, k + 1)
                        if m >= 1:
                            pe.wait_ge(probT_ready, k)
                        for h in range(2):
                            for part in ((1,) if t == 0 else (0, 1)):
                                at = 0 if t == 0 else part * P
                                ins = T(ps[:, 5, (2 * h + part) * P:(2 * h + part + 1) * P],
                                        probn[:, s, h, at:at + P], ident[:])
                        ins.then_inc(prob_turned, 1)
                pe.wait_ge(wo0_loaded, 16)
                pe.wait_ge(enc_ready, k0 + STEPS)
                for t in range(TT):
                    if t >= 2:
                        pe.wait_ge(out0_added, b * TT + t - 1)
                    for h in range(HEADS0):
                        ins = MM(ps[:, 5 + t % 2 * 2, 0:D], encT[:, h, t * P:(t + 1) * P], wo0[:, h, :],
                                 start=h == 0, stop=h == HEADS0 - 1)
                    ins.then_inc(out0_ready, 1)
                pe.wait_ge(out0_added, b * TT + TT)

            def experts(b):
                pe.wait_ge(xnT_ready, (b + BATCHES) * KT + KT)
                for t in range(TT):
                    for c in range(KT):
                        ins = split_product(ps[:, 7, t * EXPERTS:(t + 1) * EXPERTS],
                                            [x[:, c, t * P:(t + 1) * P] for x in xnT],
                                            [w[:, c, :] for w in gate], c == 0, c == KT - 1)
                ins.then_inc(logits_ready, 1)
                for j in range(FT + 2):
                    k = b * FT + j
                    if j < FT:
                        if isinstance(b, int):
                            pe.wait_ge(moe_split, j + 1)
                        if j >= 2:
                            pe.wait_ge(gated_ready, k - 1)
                        for half in range(2):
                            for c in range(KT):
                                ins = split_product(ps[:, 2 * half + j % 2, :], [w[:, j, c, half, :] for w in w1moe],
                                                    [x[:, c, :] for x in xnT], c == 0, c == KT - 1)
                        ins.then_inc(gu_ready, 1)
                    if j == FT:
                        pe.wait_ge(gated_ready, b * FT + FT)
                        turn_xn(b + BATCHES + 1)
                    if j == 1:
                        pe.wait_ge(route_step, b * ROUTE + 4 + 16)
                        for t in range(TT):
                            ins = T(ps[0:PIECE, 6, t * P:(t + 1) * P], comb[:, t, :], ident[:])
                        ins.then_inc(comb_turned, 1)
                        pe.wait_ge(route_step, b * ROUTE + 4 + ROUTE)
                        pe.wait_ge(sel_loaded, 16)
                    if 1 <= j <= FT:
                        if j >= 2:
                            pe.wait_ge(weighted, k - 1)
                        MM(ps[:, 6, :], sel[:, j - 1, :], cpieces[:], start=True, stop=True).then_inc(c_ready, 1)
                    if j >= 2:
                        m = j - 2
                        pe.wait_ge(act_ready, k - 1)
                        for c in range(KT):
                            ins = split_product(ps[:, 4 + c, :], [w[:, m, c * P:(c + 1) * P] for w in w2moe],
                                                [a[:, m % 2, :] for a in moe_act], m == 0, m == FT - 1)
                        ins.then_inc(y_used, 1)
                turn_y(b)
                pe.wait_ge(y_added, b * TT + TT)

            pe.wait_ge(gate_split, 1)
            experts(0)
            with pe.Fori(1, BATCHES) as b:
                experts(b)

            pe.wait_ge(wc_loaded, 5 * 16)
            pe.wait_ge(wc_split, 1)
            pe.wait_ge(c_consts_ready, 1)
            def pair_step(b, n, new, old):
                kb, kq = b * PAIRS, b * (PAIRS // 2)
                valid = lambda m: new if m >= 0 else old
                if new and n == 0:
                    pe.wait_ge(xnT_ready, (b + 2 * BATCHES) * KT + KT)
                for i in range(2 * TT + 2):
                    if valid(n - 1) and i < 2 * TT:
                        m = n - 1
                        k = kb + m
                        h, t = i // TT, i % TT
                        rows = slice(64 * h, 64 * h + 64)
                        if i == 0:
                            pe.wait_ge(qk1_stacked, 2 * (k + 1))
                        if old or m >= 1 or i >= 2:
                            pe.wait_ge(s1_max, k * 2 * TT + i - 1)
                        MM(ps[:, 2 + i % 2, :], qst[rows, m % 2, t * P:(t + 1) * P], kst[rows, m % 4, :],
                           start=True, stop=True).then_inc(s1_ready, 1)
                    if old and n == 4 and i in (0, 5):
                        c = i // 5
                        pe.wait_ge(o1_normed, kq)
                        if c == 1 and new:
                            pe.wait_ge(qsm_ready, kb + 3)
                        for t in range(TT):
                            ins = T(ps[:, 6 + c, t * P:(t + 1) * P], otok[:, t, c * P:(c + 1) * P], ident[:])
                        ins.then_inc(on_turned, 1)
                    if i == 0 and valid(n - 2):
                        m = n - 2
                        k = kb + m
                        pe.wait_ge(s1_max, (k + 1) * 2 * TT)
                        if old or m >= 1:
                            pe.wait_ge(qsm_ready, k)
                        if old and n == 5:
                            pe.wait_ge(oTn_ready, KT * b)
                        if old and n == 6:
                            pe.wait_ge(out1_summed, 2 * b - 1)
                        for t in range(TT):
                            ins = T(ps[:, 7, t * P:(t + 1) * P], nm1[:, m % 2, t, :], ident[:])
                        ins.then_inc(m_turned, 1)
                    if new and i < 2 * KT:
                        k = kb + n
                        if i == 0:
                            if old or n >= 1:
                                pe.wait_ge(qk1_stacked, 2 * k)
                            if n in (3, 4):
                                pe.wait_ge(v_kept, b * TT + 2 * n - 4)
                        bank, c = i // KT, i % KT
                        ins = split_product(ps[:, bank, :], [w[:, c, n, :] for w in (wq1, wk1)[bank]],
                                            [x[:, c, :] for x in xnT], c == 0, c == KT - 1)
                        if i == 2 * KT - 1:
                            ins.then_inc(qk1_ready, 1)
                    if valid(n - 2) and i >= 2:
                        m, e = n - 2, i - 2
                        k = kb + m
                        h, t = e // TT, e % TT
                        rows = slice(64 * h, 64 * h + 64)
                        if e == 0:
                            pe.wait_ge(qsm_ready, k + 1)
                        if old or m >= 1 or e >= 2:
                            pe.wait_ge(p1_ready, k * 2 * TT + e - 1)
                        MM(ps[:, 4 + e % 2, :], kst[rows, m % 4, t * P:(t + 1) * P], qsm[rows, m % 2, :],
                           start=True, stop=True).then_inc(st_ready, 1)
                    if n % 2 == 0 and valid((n - 4) // 2) and 4 <= i < 4 + TT:
                        u, c = (n - 4) // 2, i - 4
                        if c == 0:
                            pe.wait_ge(p1_ready, (kb + 2 * u + 2) * 2 * TT)
                            if old or u >= 1:
                                pe.wait_ge(o1_normed, kq + u)
                            if old and n == 4:
                                pe.wait_ge(oTn_ready, KT * b - 1)
                            if old and n == 6:
                                pe.wait_ge(out1_summed, 2 * b)
                        for h in range(4):
                            col = (4 * (u % (PAIRS // 2)) + h) * VW
                            ins = MM(ps[VW * h:VW * (h + 1), 6, :], v1[:, c, col:col + VW],
                                     pT1[:, u % 2, h, c, :], start=c == 0, stop=c == TT - 1,
                                     tile_position=(0, VW * h), skip_group_check=True)
                        if c == TT - 1:
                            ins.then_inc(o1_ready, 1)
                    if n % 2 == 1 and valid((n - 5) // 2) and i == 3:
                        u = (n - 5) // 2
                        pe.wait_ge(oT1_kept, kq + u + 1)
                        for t in range(TT):
                            ins = T(ps[:, 6, t * P:(t + 1) * P], oT1[:, u % 2, t * P:(t + 1) * P], ident[:])
                        ins.then_inc(o1_turned, 1)
                    if old and n == 5 and i in (5, 8):
                        half = i // 8
                        pe.wait_ge(oTn_ready, KT * b)
                        if new:
                            if half == 0:
                                pe.wait_ge(qsm_ready, kb + 4)
                            else:
                                pe.wait_ge(o1_normed, kq + 1)
                        for t in (2 * half, 2 * half + 1):
                            for c in range(KT):
                                ins = MM(ps[:, 7 - half, (t % 2) * D:(t % 2 + 1) * D],
                                         oTn[:, c, t * P:(t + 1) * P], wo1[:, c, :], start=c == 0, stop=c == KT - 1)
                        ins.then_inc(out1_ready, 1)
                if new and n in (2, 3):
                    pe.wait_ge(qk1_stacked, 2 * (kb + n + 1))
                    for t in (2 * n - 4, 2 * n - 3):
                        for c in range(KT):
                            ins = split_product(ps[:, t % 2, :], [x[:, c, t * P:(t + 1) * P] for x in xnT],
                                                [w[:, c, :] for w in wv1], c == 0, c == KT - 1)
                        ins.then_inc(v_ready, 1)
                if new and n == PAIRS - 1:
                    pe.wait_ge(qk1_stacked, 2 * (kb + PAIRS))
                    turn_xn(b + 2 * BATCHES + 1)

            for n in range(PAIRS):
                pair_step(0, n, True, False)
            with pe.Fori(1, BATCHES) as b:
                for n in range(PAIRS):
                    pair_step(b, n, True, True)
            for n in range(6):
                pair_step(BATCHES, n, False, True)
            pe.wait_ge(out1_added, 2 * BATCHES)

            pe.wait_ge(quant_step, 3)
            MM(ps[:, 6, 0:2], ones[:], wabs[:], start=True, stop=True).then_inc(wabs_summed, 1)
            pe.wait_ge(quantized, 2)
            with pe.Fori(0, BATCHES) as b:
                pe.wait_ge(xnT_ready, (b + 3 * BATCHES) * KT + KT)
                for f in range(HT + 1):
                    k = b * HT + f
                    if f < HT:
                        if f >= 2:
                            pe.wait_ge(h_act, k - 1)
                        for c in range(KT):
                            for part in (1, 0):
                                ins = MM(ps[:, 2 + f % 2, :], wt1[:, c, f * P:(f + 1) * P], xnT[part][:, c, :],
                                         start=c == 0 and part == 1, stop=c == KT - 1 and part == 0)
                        ins.then_inc(h_ready, 1)
                    if f == HT:
                        turn_xn(b + 3 * BATCHES + 1)
                    if f >= 1:
                        m = f - 1
                        pe.wait_ge(h_split, k)
                        for c in range(KT):
                            for part in (1, 0):
                                ins = MM(ps[:, 6 + c, :], wt2[:, m, c * P:(c + 1) * P], hact2[part][:, m % 2, :],
                                         start=m == 0 and part == 1, stop=m == HT - 1 and part == 0)
                        ins.then_inc(h_used, 1)
                turn_y(b + BATCHES)
                pe.wait_ge(y_added, (b + BATCHES) * TT + TT)


def kernel(**inputs):
    import numpy as np
    import concourse.bacc as bacc
    from concourse.bass_utils import run_bass_kernel_spmd as run

    def tiles(a, k):
        return np.ascontiguousarray(a.reshape(k, P, -1).transpose(1, 0, 2))

    g = {k: np.asarray(v) for k, v in inputs.items()}
    arrays = {"x": g["L0_attn_x"], "qs": g["L0_attn_q_norm_scale"], "ks": g["L0_attn_k_norm_scale"]}

    q, kv = g["L0_attn_q_kernel"], g["L0_attn_kv_kernel"]
    w = np.zeros((P, GROUPS, KT, 4, P), np.float32)
    for grp in range(GROUPS):
        for i, head in enumerate((q[2 * grp], q[2 * grp + 1], kv[0, grp], kv[1, grp])):
            w[:, grp, :, i, :] = tiles(head, KT)
    arrays["wqkv"] = w.reshape(P, GROUPS, KT, 4 * P)
    arrays["wo0"] = np.ascontiguousarray(g["L0_attn_out_kernel"].transpose(1, 0, 2))

    w1, w2 = g["L0_ffn_w1"], g["L0_ffn_w2"]
    s1, s2 = g["L0_ffn_shared_w1"], g["L0_ffn_shared_w2"]
    up = np.zeros((2, FT * P, D), np.float32)
    down = np.zeros((FT * P, D), np.float32)
    for half in range(2):
        up[half, 0:EXPERTS * INTER] = w1[:, half * INTER:(half + 1) * INTER, :].reshape(-1, D)
        up[half, EXPERTS * INTER:FEATS] = s1[half * SHARED:(half + 1) * SHARED]
    down[0:EXPERTS * INTER] = w2.transpose(0, 2, 1).reshape(-1, D)
    down[EXPERTS * INTER:FEATS] = s2.T
    arrays["w1moe"] = np.ascontiguousarray(up.reshape(2, FT, P, KT, P).transpose(4, 1, 3, 0, 2))
    arrays["w2moe"] = tiles(down, FT)
    arrays["gate"] = tiles(g["L0_ffn_gate_w"].T, KT)

    thirds = []
    for src in (g["L1_attn_Wq"], g["L1_attn_Wk"]):
        w = np.zeros((D, HEADS1, 4, HD1), np.float32)
        w[:, :, 0:3, :] = src.reshape(D, HEADS1, 1, HD1)
        thirds.append(tiles(w.reshape(D, -1), KT).reshape(P, -1))
    w = np.zeros((D, HEADS1, VW), np.float32)
    w[:, :, 0:HD1] = g["L1_attn_Wv"].reshape(D, HEADS1, HD1)
    thirds.append(tiles(w.reshape(D, -1), KT).reshape(P, -1))
    arrays["wc"] = np.concatenate(thirds, 1)
    arrays["wo1"] = tiles(g["L1_attn_Wo"], KT)
    arrays["bo1"] = g["L1_attn_bo"]
    arrays["wm1"] = tiles(g["L1_ffn_w1"].T, KT)
    arrays["wm2"] = tiles(g["L1_ffn_w2"].T, HT)
    arrays["b1m"] = np.ascontiguousarray(g["L1_ffn_b1"].reshape(HT, P).T)
    arrays["b2m"] = np.ascontiguousarray(g["L1_ffn_b2"].reshape(KT, P).T)

    arrays["c_ident"] = np.eye(P, dtype=np.float32)
    frac = np.arange(0, HD0, 2, dtype=np.float32) / np.float32(HD0)
    angle = np.arange(SEQ, dtype=np.float32)[:, None] / np.float32(10000.0) ** frac
    cos, sin = np.cos(angle), np.sin(angle)
    arrays["c_cos"] = tiles(np.concatenate([cos, cos], 1), TT)
    arrays["c_sin"] = tiles(np.concatenate([-sin, sin], 1), TT)
    qi, kj = np.arange(P)[:, None], np.arange(P)[None, :]
    masks = np.where(np.stack([kj > qi, kj <= qi], 1), np.float32(0), np.float32(-1e30))
    arrays["c_window"] = np.ascontiguousarray(np.broadcast_to(masks[:, None], (P, 2, 2, P)))
    feat = np.arange(FT * P)
    owner = np.where(feat < EXPERTS * INTER, feat // INTER, EXPERTS)
    sel = np.zeros((3, PIECE, FT * P), np.float32)
    sel[:, owner[feat < FEATS], feat[feat < FEATS]] = 1.0
    arrays["c_sel"] = sel.reshape(3 * PIECE, FT, P)
    vones = np.zeros((P, HEADS1, VW), np.float32)
    vones[:, :, HD1] = 1.0
    arrays["c_vones"] = vones.reshape(P, -1)
    stack = np.zeros((2, 64, 4), np.float32)
    stack[:, 2 * HD1:3 * HD1, 0] = -1.0
    stack[:, HD1:2 * HD1, 1] = -1.0
    stack[:, MAX_ROW, 1:3] = 1.0
    arrays["c_stack"] = stack.reshape(P, 4)

    nc = bacc.Bacc("TRN2", target_bir_lowering=False, num_devices=1)
    feeds, dram = {}, {}
    for name, a in arrays.items():
        a = np.ascontiguousarray(a)
        feeds[f"in_{name}"] = a
        dram[name] = nc.dram_tensor(f"in_{name}", a.shape, mybir.dt.from_np(a.dtype), kind="ExternalInput").ap()
    out = nc.dram_tensor("out_x", (BATCHES, SEQ, D), F32, kind="ExternalOutput").ap()
    build(nc, dram, out)
    result = run(nc, [feeds], core_ids=[0])
    return result.results[0]["out_x"]
```

```python
from contextlib import ExitStack

import concourse.bass as bass
from concourse import mybir

F32 = mybir.dt.float32
F32R = mybir.dt.float32r
BF16 = mybir.dt.bfloat16
ALU = mybir.AluOpType
ACT = mybir.ActivationFunctionType
AX = mybir.AxisListType

P = 128
BATCHES, SEQ, D = 4, 512, 256
TT = SEQ // P
KT = D // P
NTILES = BATCHES * TT
LN_EPS = 1e-5

HEADS0, KV0, HD0 = 16, 8, 128
RMS_EPS = 1e-6
ATTN_SCALE0 = 0.08838834764831845
GROUPS = KV0
STEPS = GROUPS * TT
RAW_RING, QK_RING, PROB_RING = 9, 4, 3
LAST_LAG = 8

EXPERTS, INTER, TOP_K, SHARED = 16, 176, 6, 352
FEATS = EXPERTS * INTER + SHARED
FT = -(-FEATS // P)
ROUTE, ROUTED = 22, 16
SG_RING = 3
PIECE = 32

HEADS1, HD1 = 16, 16
PAIRS = HEADS1 // 2
HEADS_T = P // HD1
PAIRS_T = HEADS_T // 2
VW = 32
MAX_ROW = 48
SCALE1 = 0.25

DFF = 1024
HT = DFF // P
H_RING = 3
QUANT_EPS = 1e-8


def build(nc, dram, out):
    with ExitStack() as ctx:
        def sem(name):
            return ctx.enter_context(nc.semaphore(name))

        def sb(name, shape, dt=F32, where=None):
            return (where or ctx).enter_context(nc.sbuf_tensor(name, shape, dt))

        ps = ctx.enter_context(nc.psum_tensor("ps", [P, 8, 512], F32))

        x_res = sb("x_res", [P, NTILES, D])
        turned_only = ExitStack()
        xn = sb("xn", [P, TT, D], where=turned_only)
        turned_only.close()
        wo_parts = [sb(f"wo0_{part}", [P, 2, D], F32R) for part in ("hi", "lo")]
        xnT = [sb(f"xnT_{part}", [P, KT, SEQ], F32R) for part in ("hi", "lo")]
        even_head_only = ExitStack()
        even_head = [sb(f"even_head_{part}", [P, SEQ], F32R, even_head_only) for part in ("hi", "lo")]
        even_head_only.close()
        yT = sb("yT", [P, KT, SEQ])
        ident = sb("ident", [P, P])
        bn_st = sb("bn_st", [P, TT, 6])
        bn_mv = sb("bn_mv", [P, TT, 2])
        ln_ve = sb("ln_ve", [P, TT])
        ln_rs = sb("ln_rs", [P, TT])
        minus_half = sb("minus_half", [P, 16])
        eps_sum = sb("eps_sum", [P, 3])
        spare = sb("spare", [P, 2])

        part_a = ExitStack()
        wqkv = [sb(f"wqkv_{part}", [P, GROUPS, KT, 4 * P], F32R, part_a) for part in ("hi", "lo")]
        wo0 = sb("wo0", [P, HEADS0, D], where=part_a)
        ident_b = sb("ident_b", [P, P], BF16, part_a)
        window = sb("window", [P, 2, 2, P], BF16, part_a)
        qks = sb("qks", [P, 3, P], where=part_a)
        cos3 = sb("cos3", [P, TT, 3, P], where=part_a)
        sin3 = sb("sin3", [P, TT, 3, P], where=part_a)
        raw = sb("raw", [P, RAW_RING, 4 * P], where=part_a)
        ssum = sb("ssum", [P, 2, 3], where=part_a)
        msq = sb("msq", [P, 2, 3], where=part_a)
        rms = sb("rms", [P, 2, 3], where=part_a)
        qkT = sb("qkT", [P, QK_RING, 3, P], where=part_a)
        nmax = sb("nmax", [P, 2, 2], where=part_a)
        psums = sb("psums", [P, 2, 2], where=part_a)
        rsums = sb("rsums", [P, 2, 2], where=part_a)
        prob = sb("prob", [P, PROB_RING, 2, 2 * P], where=part_a)
        probT = sb("probT", [P, 2, 4, P], where=part_a)
        encT = sb("encT", [P, HEADS0, SEQ], where=part_a)
        rope1 = sb("rope1", [P, 2, 3 * P], where=part_a)
        rope2 = sb("rope2", [P, 2, 3 * P], where=part_a)
        qkn = sb("qkn", [P, 2, 3 * P], where=part_a)
        odd_head = [sb(f"odd_head_{part}", [P, SEQ], F32R, part_a) for part in ("hi", "lo")]
        enc_parts = list(zip(even_head, odd_head))
        wqkv_in = encT[:].rearrange("p (g c) f -> p g c f", g=GROUPS)
        cos_in, sin_in = (yT[:, i, :].rearrange("p (t f) -> p t f", t=TT) for i in range(2))
        sq = rope2
        part_a.close()

        part_b = ExitStack()
        w1moe = [sb(f"w1moe_{part}", [P, FT, KT, 2, P], F32R, part_b) for part in ("hi", "lo")]
        w2moe = [sb(f"w2moe_{part}", [P, FT, D], F32R, part_b) for part in ("hi", "lo")]
        gate = [sb(f"gate_{part}", [P, KT, EXPERTS], F32R, part_b) for part in ("hi", "lo")]
        w2_in = sb("w2_in", [P, 2, D], where=part_b)
        w1_in = yT[:].rearrange("p s (c h f) -> p s c h f", c=KT, h=2)
        sel = sb("sel", [3 * PIECE, FT, P], BF16, part_b)
        lg = sb("lg", [P, TT, EXPERTS], where=part_b)
        gmax = sb("gmax", [P, TT], where=part_b)
        gate_in = lg[:, 0:KT, :]
        gsum = sb("gsum", [P, TT], where=part_b)
        ginv = sb("ginv", [P, TT], where=part_b)
        gprob = sb("gprob", [P, TT, EXPERTS + 2], where=part_b)
        gtop = sb("gtop", [P, TT, 8], where=part_b)
        gmark = sb("gmark", [P, TT, EXPERTS + 2], where=part_b)
        gexp = gmark[:, :, 0:EXPERTS]
        gmask = lg
        comb = sb("comb", [P, TT, PIECE], where=part_b)
        cT, cTr = (xn[0:PIECE, 2 * i:2 * i + 2, :].rearrange("p a d -> p (a d)") for i in range(2))
        cpieces = sb("cpieces", [3 * PIECE, SEQ], BF16, part_b)
        sg = sb("sg", [P, SG_RING, SEQ], where=part_b)
        moe_act = [sb(f"moe_act_{part}", [P, 2, SEQ], F32R, part_b) for part in ("hi", "lo")]
        part_b.close()

        part_c = ExitStack()
        wqk1 = [sb(f"wqk1_{part}", [P, KT, 2 * D], F32R, part_c) for part in ("hi", "lo")]
        wv1 = [sb(f"wv1_{part}", [P, KT, HEADS1 * VW], F32R, part_c) for part in ("hi", "lo")]
        pick = sb("pick", [P, PAIRS_T, 2, 2, P], F32R, part_c)
        pT1 = sb("pT1", [P, 2, 4, TT, SEQ], where=part_c)
        wo1 = sb("wo1", [P, KT, D], where=part_c)
        bo1 = sb("bo1", [P, D], where=part_c)
        vones = sb("vones", [P, HEADS1 * VW], where=part_c)
        stack = sb("stack", [P, 4], where=part_c)
        v1 = sb("v1", [P, TT, HEADS1 * VW], where=part_c)
        qk1 = [sb(f"qk1_{part}", [P, 2, 2, SEQ], F32R, part_c) for part in ("hi", "lo")]
        qst = sb("qst", [P, 2, SEQ], F32R, part_c)
        kst = sb("kst", [P, 4, SEQ], F32R, part_c)
        qsm = sb("qsm", [P, 2, SEQ], F32R, part_c)
        nm1 = sb("nm1", [P, 2, TT, P], where=part_c)
        early = pT1[:, 1].rearrange("p h c f -> p h (c f)")
        wqk1_in, wv1_in, pick_in = early[:, 0, 0:KT * 2 * D], early[:, 1, 0:KT * HEADS1 * VW], early[:, 2, 0:4 * PAIRS_T * P]
        oT1 = sb("oT1", [P, 2, SEQ], where=part_c)
        oinv = sb("oinv", [P, 2, TT, 4], where=part_c)
        otok = sb("otok", [P, TT, D], where=part_c)
        oTn = sb("oTn", [P, KT, SEQ], where=part_c)
        wm1 = sb("wm1", [P, KT, DFF], where=part_c)
        wm2 = sb("wm2", [P, HT, D], where=part_c)
        ones = sb("ones", [P, P], where=part_c)
        wabs = sb("wabs", [P, 2], where=part_c)
        wscl = sb("wscl", [P, 2], where=part_c)
        whalf = sb("whalf", [P, 2], where=part_c)
        wmhalf = sb("wmhalf", [P, 2], where=part_c)
        b1m = sb("b1m", [P, HT], where=part_c)
        b2m = sb("b2m", [P, KT], where=part_c)
        part_c.close()
        part_d = ExitStack()
        wt1 = sb("wt1", [P, KT, DFF], F32R, part_d)
        wt2 = sb("wt2", [P, HT, D], F32R, part_d)
        wneg = sb("wneg", [P, 2, KT * DFF], where=part_d)
        hact = sb("hact", [P, H_RING, SEQ], where=part_d)
        hact2 = [sb(f"hact_{part}", [P, H_RING, SEQ], F32R, part_d) for part in ("hi", "lo")]
        part_d.close()

        x_loaded, x_rest_loaded = sem("x_loaded"), sem("x_rest_loaded")
        consts_loaded = sem("consts_loaded")
        tables_loaded = sem("tables_loaded")
        wqkv_loaded = [sem(f"wqkv_loaded{i}") for i in range(GROUPS)]
        wo0_loaded = sem("wo0_loaded")
        gate_loaded = sem("gate_loaded")
        sel_loaded = sem("sel_loaded")
        moe_loaded = [sem(f"moe_loaded{i}") for i in range(2)]
        moe_high, moe_split = sem("moe_high"), sem("moe_split")
        gate_high, gate_split = sem("gate_high"), sem("gate_split")
        wqkv_high, wqkv_split = sem("wqkv_high"), sem("wqkv_split")
        wc_high, wc_split = sem("wc_high"), sem("wc_split")
        wqk1_loaded, wv1_loaded, pick_loaded = sem("wqk1_loaded"), sem("wv1_loaded"), sem("pick_loaded")
        pick_ready = sem("pick_ready")
        c_rest_loaded = sem("c_rest_loaded")
        wd_loaded = sem("wd_loaded")
        masks_loaded = sem("masks_loaded")
        out_stored = sem("out_stored")
        half_set = sem("half_set")
        ln_stats, ln_aggr, ln_var = sem("ln_stats"), sem("ln_aggr"), sem("ln_var")
        ln_rstd, xn_ready = sem("ln_rstd"), sem("xn_ready")
        xn_turned, xnT_high, xnT_ready = sem("xn_turned"), sem("xnT_high"), sem("xnT_ready")
        tables_scaled = sem("tables_scaled")
        projected, raw_kept, squared = sem("projected"), sem("raw_kept"), sem("squared")
        summed, meaned, rms_ready = sem("summed"), sem("meaned"), sem("rms_ready")
        roped, rotated, qk_normed = sem("roped"), sem("rotated"), sem("qk_normed")
        qk_turned, qkT_ready = sem("qk_turned"), sem("qkT_ready")
        scored, max_ready, prob_ready = sem("scored"), sem("max_ready"), sem("prob_ready")
        inv_ready, probn_ready = sem("inv_ready"), sem("probn_ready")
        prob_turned, probT_ready = sem("prob_turned"), sem("probT_ready")
        attended, enc_ready = sem("attended"), sem("enc_ready")
        enc_high, enc_split = sem("enc_high"), sem("enc_split")
        wo0_high, wo0_split, head_used = sem("wo0_high"), sem("wo0_split"), sem("head_used")
        out0_summed, out0_kept = sem("out0_summed"), sem("out0_kept")
        out0_ready, out0_added = sem("out0_ready"), sem("out0_added")
        logits_ready, route_step = sem("logits_ready"), sem("route_step")
        comb_turned, comb_step = sem("comb_turned"), sem("comb_step")
        gate_exp = sem("gate_exp")
        gu_ready, silu_ready, gated_ready = sem("gu_ready"), sem("silu_ready"), sem("gated_ready")
        c_ready, weighted = sem("c_ready"), sem("weighted")
        act_high, act_ready, y_used = sem("act_high"), sem("act_ready"), sem("y_used")
        yT_ready, y_turned, y_added = sem("yT_ready"), sem("y_turned"), sem("y_added")
        c_consts_ready = sem("c_consts_ready")
        v_ready, v_kept = sem("v_ready"), sem("v_kept")
        qk1_ready, qk1_high, qk1_split = sem("qk1_ready"), sem("qk1_high"), sem("qk1_split")
        picked = [sem(f"picked_{name}") for name in ("queries", "keys")]
        q_stacked, k_stacked = sem("q_stacked"), sem("k_stacked")
        s1_ready, s1_max = sem("s1_ready"), sem("s1_max")
        m_turned, qsm_ready = sem("m_turned"), sem("qsm_ready")
        st_ready, p1_ready = sem("st_ready"), sem("p1_ready")
        o1_ready, oT1_kept, o1_turned = sem("o1_ready"), sem("oT1_kept"), sem("o1_turned")
        o1_inv, o1_normed = sem("o1_inv"), sem("o1_normed")
        on_turned, oTn_ready, out1_ready = sem("on_turned"), sem("oTn_ready"), sem("out1_ready")
        out1_summed, out1_added = sem("out1_summed"), sem("out1_added")
        quant_step, wabs_summed, quantized = sem("quant_step"), sem("wabs_summed"), sem("quantized")
        h_ready, h_act, h_high, h_split, h_used = (
            sem("h_ready"), sem("h_act"), sem("h_high"), sem("h_split"), sem("h_used"))

        block = ctx.enter_context(nc.Block())

        def wait(eng, s, value):
            if not (isinstance(value, int) and value <= 0):
                eng.wait_ge(s, value)

        HEADS_AT = {34: (0, 1), 35: (2, 3), 36: (4,), 37: (5, 6), 38: (7,), 39: (8, 9)}
        OLD_HEADS_AT = {0: (10,), 1: (11, 12), 2: (13,), 3: (14,), 4: (15,)}
        EARLY_TURNS = 3
        OLD_STEPS = 8

        def heads_next(n, new, old):
            if n == STEPS + LAST_LAG - 1:
                return (OLD_HEADS_AT[0], 0) if new else ((), 0)
            if n + 1 in HEADS_AT:
                return (HEADS_AT[n + 1], 0) if new else ((), 0)
            return (OLD_HEADS_AT.get(n + 1, ()), -1) if old else ((), 0)

        weighted_tile = lambda j: -1 if j == 0 else j - 2 if j >= 2 else None
        summed_tile = lambda j: j - 2 if j < 2 else j - 3 if j >= 3 else None
        sg_slot = lambda j: 1 if j % FT == FT - 1 else j % FT % SG_RING

        def slot_age(j):
            age = 1
            while sg_slot(j - age) != sg_slot(j):
                age += 1
            return age

        MLP_AFTER = {3: (0, 1), 4: (2,), 5: (3, 4), 6: (5,), 7: (6, 7, 8)}
        hidden_used = lambda f: -1 if f == 0 else f - 2 if f >= 2 else None
        hidden_split = lambda f: f if f < HT else None
        hidden_age = lambda f: 2 if f < 2 else 3

        @block.sync
        def _(sp):
            sp.dma_start(ident[:], dram["c_ident"]).then_inc(consts_loaded, 16)
            sp.dma_start(x_res[:, 0:TT, :], dram["x"][0].rearrange("(t p) d -> p t d", p=P)).then_inc(x_loaded, 16)
            for i in range(GROUPS):
                sp.dma_start(wqkv_in[:, i], dram["wqkv"][:, i]).then_inc(wqkv_loaded[i], 16)
                if i == 0:
                    sp.dma_start(qks[:, 0:2, :], dram["qs"].unsqueeze(0).unsqueeze(0).to_broadcast((P, 2, P))
                                 ).then_inc(tables_loaded, 16)
                    sp.dma_start(qks[:, 2, :], dram["ks"].unsqueeze(0).to_broadcast((P, P))
                                 ).then_inc(tables_loaded, 16)
                    sp.dma_start(cos_in, dram["c_cos"]).then_inc(tables_loaded, 16)
                    sp.dma_start(sin_in, dram["c_sin"]).then_inc(tables_loaded, 16)
            sp.dma_start(x_res[:, TT:NTILES, :], dram["x"][1:BATCHES].rearrange("b (t p) d -> p (b t) d", p=P)
                         ).then_inc(x_rest_loaded, 16)
            sp.dma_start(wo0[:], dram["wo0"]).then_inc(wo0_loaded, 16)
            wait(sp, out0_added, BATCHES * TT)
            sp.dma_start(gate_in, dram["gate"]).then_inc(gate_loaded, 16)
            for j in range(FT):
                if j >= 2:
                    sp.wait_ge(moe_split, j - 1)
                sp.dma_start(w1_in[:, j % 2], dram["w1moe"][:, j]).then_inc(moe_loaded[j % 2], 16)
                sp.dma_start(w2_in[:, j % 2, :], dram["w2moe"][:, j]).then_inc(moe_loaded[j % 2], 16)
            wait(sp, y_added, BATCHES * TT)
            sp.dma_start(wqk1_in, dram["wqk1"]).then_inc(wqk1_loaded, 16)
            sp.dma_start(pick_in, dram["c_pick"]).then_inc(pick_loaded, 16)
            sp.dma_start(stack[:], dram["c_stack"]).then_inc(c_rest_loaded, 16)
            sp.dma_start(wv1_in, dram["wv1"]).then_inc(wv1_loaded, 16)
            for name, dst in (("wo1", wo1), ("c_vones", vones)):
                sp.dma_start(dst[:], dram[name]).then_inc(c_rest_loaded, 16)
            sp.dma_start(bo1[:], dram["bo1"].unsqueeze(0).to_broadcast((P, D))).then_inc(c_rest_loaded, 16)
            for name, dst in (("wm1", wm1), ("wm2", wm2), ("b1m", b1m), ("b2m", b2m)):
                sp.dma_start(dst[:], dram[name]).then_inc(wd_loaded, 16)
            for b in range(BATCHES):
                sp.wait_ge(y_added, (BATCHES + b + 1) * TT)
                sp.dma_start(out[b].rearrange("(t p) d -> p t d", p=P),
                             x_res[:, b * TT:(b + 1) * TT, :]).then_inc(out_stored, 16)
            sp.wait_ge(out_stored, 16 * BATCHES)

        @block.gpsimd
        def _(pool):
            nc.gpsimd.memset(minus_half[:], -0.5).then_inc(half_set, 1)
            nc.gpsimd.memset(eps_sum[:], HD0 * RMS_EPS).then_inc(half_set, 1)
            pool.dma_start(ident_b[:], dram["c_ident"]).then_inc(masks_loaded, 16)
            pool.dma_start(window[:], dram["c_window"]).then_inc(masks_loaded, 16)
            pool.wait_ge(half_set, 2)

            def rstd(i):
                pool.wait_ge(ln_var, i + 1)
                nc.gpsimd.tensor_tensor(ln_rs[:], ln_ve[:], minus_half[:, 0:TT], ALU.pow).then_inc(ln_rstd, 1)

            rstd(0)
            def attention_step(b, n, new, old):
                heads, back = heads_next(n, new, old)

                def split_weights(h):
                    pool.wait_ge(wo0_high, (b + back) * HEADS0 + h + 1)
                    nc.gpsimd.tensor_tensor(wo_parts[1][:, h % 2, :], wo0[:, h, :], wo_parts[0][:, h % 2, :],
                                            ALU.subtract).then_inc(wo0_split, 1)

                if new and n == STEPS // 2 + 1:
                    rstd(b + 1)
                for h in heads[0:1]:
                    split_weights(h)
                if new and n < STEPS:
                    k, s = b * STEPS + n, n % 2
                    pool.wait_ge(summed, k + 1)
                    if n >= 2:
                        pool.wait_ge(qk_normed, k - 1)
                    nc.gpsimd.tensor_tensor(msq[:, s, :], ssum[:, s, :], eps_sum[:], ALU.add).then_inc(meaned, 1)
                    pool.wait_ge(meaned, k + 1)
                    nc.gpsimd.tensor_tensor(rms[:, s, :], msq[:, s, :], minus_half[:, 0:3],
                                            ALU.pow).then_inc(rms_ready, 1)
                    pool.wait_ge(roped, k + 1)
                    nc.gpsimd.tensor_tensor(rope1[:, s, :], rope1[:, s, :], rope2[:, s, :],
                                            ALU.add).then_inc(rotated, 1)
                for h in heads[1:2]:
                    split_weights(h)

            for n in range(STEPS + LAST_LAG):
                attention_step(0, n, True, False)
            with pool.Fori(1, BATCHES) as b:
                for n in range(STEPS + LAST_LAG):
                    attention_step(b, n, True, True)
            for n in range(OLD_STEPS):
                attention_step(BATCHES, n, False, True)
            pool.wait_ge(out0_added, BATCHES * TT)
            pool.dma_start(sel[:], dram["c_sel"]).then_inc(sel_loaded, 16)
            with pool.Fori(BATCHES + 1, 4 * BATCHES) as i:
                rstd(i)

        @block.vector
        def _(dve):
            V = nc.vector

            def x_tile(b, t):
                return x_res[:, bass.ds(b * TT + t, 1), :].rearrange("p a d -> p (a d)")

            def norm_stats(i, b, tiles=range(TT)):
                for t in tiles:
                    V.bn_stats(bn_st[:, t, :], x_tile(b, t)).then_inc(ln_stats, 1)
                if TT - 1 in tiles:
                    dve.wait_ge(ln_stats, i * TT + TT)
                    V.memset(spare[:, 0:1], 0.0)
                    for t in range(TT):
                        V.bn_aggr(bn_mv[:, t, :], bn_st[:, t, :]).then_inc(ln_aggr, 1)
                    dve.wait_ge(ln_aggr, i * TT + TT)
                    V.tensor_scalar(ln_ve[:], bn_mv[:, :, 1], LN_EPS, None, ALU.add).then_inc(ln_var, 1)

            def norm_apply(i, b, tiles=range(TT)):
                if 0 in tiles:
                    dve.wait_ge(ln_rstd, i + 1)
                    dve.wait_ge(xn_turned, i * KT + 1)
                for t in tiles:
                    V.tensor_scalar(xn[:, t, :], x_tile(b, t), bn_mv[:, t, 0:1], ln_rs[:, t:t + 1],
                                    ALU.subtract, ALU.mult).then_inc(xn_ready, 1)

            def split_xnT(i):
                for c in range(KT):
                    dve.wait_ge(xnT_high, i * KT + c + 1)
                    V.tensor_tensor(xnT[1][:, c, :], ps[:, c, :], xnT[0][:, c, :], ALU.subtract
                                    ).then_inc(xnT_ready, 1)

            V.memset(spare[:, 0:1], 0.0).then_inc(xn_turned, 1)
            dve.wait_ge(x_loaded, 16)
            norm_stats(0, 0)
            norm_apply(0, 0)
            split_xnT(0)

            def split_wqkv(g):
                dve.wait_ge(wqkv_high, g + 1)
                V.tensor_tensor(*(w[:, g].rearrange("p c f -> p (c f)") for w in (wqkv[1], wqkv_in, wqkv[0])),
                                ALU.subtract).then_inc(wqkv_split, 1)

            split_wqkv(0)
            dve.wait_ge(tables_loaded, 4 * 16)
            V.tensor_scalar(qks[:, 0:2, :], qks[:, 0:2, :], ATTN_SCALE0 * HD0 ** 0.5, None, ALU.mult
                            ).then_inc(tables_scaled, 1)
            V.tensor_scalar(qks[:, 2, :], qks[:, 2, :], HD0 ** 0.5, None, ALU.mult).then_inc(tables_scaled, 1)
            dve.wait_ge(tables_scaled, 2)
            H2 = HD0 // 2
            for h in range(3):
                sc = qks[:, h:h + 1, :].to_broadcast((P, TT, P))
                lo, hi = sc[:, :, 0:H2], sc[:, :, H2:HD0]
                V.tensor_tensor(cos3[:, :, h, :], cos_in, sc, ALU.mult).then_inc(tables_scaled, 1)
                V.tensor_tensor(sin3[:, :, h, 0:H2], sin_in[:, :, 0:H2], hi, ALU.mult).then_inc(tables_scaled, 1)
                V.tensor_tensor(sin3[:, :, h, H2:HD0], sin_in[:, :, H2:HD0], lo, ALU.mult).then_inc(tables_scaled, 1)
            dve.wait_ge(tables_scaled, 11)

            def attention_step(b, n, new, old):
                heads, back = heads_next(n, new, old)

                def split_head(h):
                    dve.wait_ge(enc_high, (b + back) * HEADS0 + h + 1)
                    V.tensor_tensor(enc_parts[1][h % 2][:], encT[:, h, :], enc_parts[0][h % 2][:],
                                    ALU.subtract).then_inc(enc_split, 1)

                k0 = b * STEPS
                if new and n == STEPS // 2:
                    norm_stats(b + 1, (b + 1) % BATCHES)
                if new and n == STEPS // 2 + 2:
                    norm_apply(b + 1, (b + 1) % BATCHES)
                if new and 6 <= n < STEPS + 6:
                    m = n - 6
                    k, s, w = k0 + m, m % 2, (P if m % TT == 0 else 2 * P)
                    dve.wait_ge(prob_ready, k + 1)
                    V.reciprocal(rsums[:, s, :], psums[:, s, :]).then_inc(inv_ready, 1)
                    dve.wait_ge(inv_ready, k + 1)
                    for h in range(2):
                        ins = V.tensor_scalar(prob[:, m % PROB_RING, h, 0:w], prob[:, m % PROB_RING, h, 0:w], rsums[:, s, h:h + 1],
                                              None, ALU.mult)
                    ins.then_inc(probn_ready, 1)
                if new and 4 <= n < STEPS + 4:
                    m = n - 4
                    k, s, w = k0 + m, m % 2, (P if m % TT == 0 else 2 * P)
                    dve.wait_ge(scored, k + 1)
                    V.tensor_reduce(nmax[:, s, :], ps[:, 3 + s, :].rearrange("p (h f) -> p h f", h=2)[:, :, 0:w],
                                    AX.X, ALU.max, negate=True).then_inc(max_ready, 1)
                if new and n == STEPS + 2:
                    split_xnT(b + 1)
                for h in heads[0:1]:
                    split_head(h)
                if new and 1 <= n <= STEPS:
                    m = n - 1
                    k, s = k0 + m, m % 2
                    dve.wait_ge(rotated, k + 1)
                    dve.wait_ge(rms_ready, k + 1)
                    if m >= 2:
                        dve.wait_ge(qk_turned, k - 1)
                    V.tensor_tensor(qkn[:, s, :].rearrange("p (h f) -> p h f", h=3),
                                    rope1[:, s, :].rearrange("p (h f) -> p h f", h=3),
                                    rms[:, s, :].unsqueeze(2).to_broadcast((P, 3, P)), ALU.mult
                                    ).then_inc(qk_normed, 1)
                if new and n < STEPS:
                    k, s, t = k0 + n, n % 2, n % TT
                    dve.wait_ge(squared, k + 1)
                    if n >= 2:
                        dve.wait_ge(rotated, k - 1)
                        dve.wait_ge(qk_normed, k - 1)
                    V.reduce_sum(ssum[:, s, :], sq[:, s, :].rearrange("p (h f) -> p h f", h=3), AX.X
                                 ).then_inc(summed, 1)
                    r3 = raw[:, n % RAW_RING, 0:3 * P]
                    dve.wait_ge(summed, k + 1)
                    V.tensor_tensor(rope1[:, s, :], r3, cos3[:, t, :, :].rearrange("p h f -> p (h f)"), ALU.mult)
                    rh = r3.rearrange("p (h f) -> p h f", h=3)
                    o2 = rope2[:, s, :].rearrange("p (h f) -> p h f", h=3)
                    V.tensor_tensor(o2[:, :, 0:H2], rh[:, :, H2:HD0], sin3[:, t, :, 0:H2], ALU.mult)
                    V.tensor_tensor(o2[:, :, H2:HD0], rh[:, :, 0:H2], sin3[:, t, :, H2:HD0], ALU.mult
                                    ).then_inc(roped, 1)
                for h in heads[1:2]:
                    split_head(h)
                if old and n in (6, 7):
                    half = n - 6
                    dve.wait_ge(out0_ready, b * 2 - 1 + half)
                    for t in (2 * half, 2 * half + 1):
                        V.tensor_tensor(x_tile(b - 1, t), ps[:, 6 + half, (t % 2) * D:(t % 2 + 1) * D],
                                        x_tile(b - 1, t), ALU.add).then_inc(out0_added, 1)
                    if n == 7:
                        dve.wait_ge(out0_added, b * TT)

            for n in range(STEPS + LAST_LAG):
                if n == STEPS // 2:
                    dve.wait_ge(x_rest_loaded, 16)
                attention_step(0, n, True, False)
                if n + 1 < GROUPS:
                    split_wqkv(n + 1)
            with dve.Fori(1, BATCHES) as b:
                for n in range(STEPS + LAST_LAG):
                    attention_step(b, n, True, True)
            for n in range(OLD_STEPS):
                attention_step(BATCHES, n, False, True)

            V.memset(cpieces[:], 0.0).then_inc(route_step, 1)
            V.memset(comb[:], 0.0).then_inc(route_step, 1)
            V.memset(gprob[:], -1.0).then_inc(route_step, 1)
            dve.wait_ge(route_step, 3)
            V.memset(comb[:, :, EXPERTS:EXPERTS + 1], 1.0).then_inc(route_step, 1)
            dve.wait_ge(route_step, 4)
            def route(b, ahead):
                links = [0 if ahead else ROUTED]

                def link(ins, wait_now=True):
                    links[0] += 1
                    ins.then_inc(route_step, 1)
                    if wait_now:
                        dve.wait_ge(route_step, b * ROUTE + (4 + links[0]))

                if not ahead:
                    dve.wait_ge(comb_turned, b + 1)
                    link(V.tensor_copy(cT, ps[0:PIECE, 7, :]))
                    link(V.tensor_copy(cpieces[0:PIECE, :], cT))
                    link(V.tensor_tensor(cTr, cT, cpieces[0:PIECE, :], ALU.subtract))
                    link(V.tensor_copy(cpieces[PIECE:2 * PIECE, :], cTr))
                    link(V.tensor_tensor(cT, cTr, cpieces[PIECE:2 * PIECE, :], ALU.subtract))
                    link(V.tensor_copy(cpieces[2 * PIECE:3 * PIECE, :], cT))
                    assert links[0] == ROUTE, links
                    return
                dve.wait_ge(logits_ready, b + 1)
                lps = ps[:, 7, 0:TT * EXPERTS].rearrange("p (t e) -> p t e", t=TT)
                link(V.reduce_max(gmax[:], lps, AX.X))
                link(V.tensor_tensor(lg[:], lps, gmax[:].unsqueeze(2).to_broadcast((P, TT, EXPERTS)), ALU.subtract))
                dve.wait_ge(gate_exp, b + 1)
                link(V.reduce_sum(gsum[:], gexp, AX.X))
                link(V.reciprocal(ginv[:], gsum[:]))
                link(V.tensor_tensor(gprob[:, :, 0:EXPERTS], gexp,
                                     ginv[:].unsqueeze(2).to_broadcast((P, TT, EXPERTS)), ALU.mult))
                V.memset(spare[:, 1:2], 0.0)
                for t in range(TT):
                    link(V.max(gtop[:, t, :], gprob[:, t, 0:EXPERTS]), t == TT - 1)
                link(V.memset(gtop[:, :, TOP_K:8], -1.0))
                V.memset(spare[:, 1:2], 0.0)
                for t in range(TT):
                    link(V.match_replace(gmark[:, t, :], gtop[:, t, :], gprob[:, t, :], -2.0), t == TT - 1)
                link(V.tensor_scalar(gmask[:], gmark[:, :, 0:EXPERTS], -2.0, None, ALU.is_equal))
                link(V.tensor_tensor(comb[:, :, 0:EXPERTS], gmask[:], gprob[:, :, 0:EXPERTS], ALU.mult))
                assert links[0] == ROUTED, links

            def add_half(b, half):
                dve.wait_ge(y_turned, b * 2 + half + 1)
                for t in (2 * half, 2 * half + 1):
                    V.tensor_tensor(x_tile(b, t), ps[:, 7, (t % 2) * D:(t % 2 + 1) * D], x_tile(b, t),
                                    ALU.add).then_inc(y_added, 1)

            def expert_step(b, j, new, old):
                if new and isinstance(b, int) and j + 2 < FT:
                    split_moe(j + 2)
                if new and j == FT // 2:
                    norm_stats(b + BATCHES + 1, (b + 1) % BATCHES)
                if new and j == FT // 2 + 2:
                    norm_apply(b + BATCHES + 1, (b + 1) % BATCHES)

                def gated():
                    dve.wait_ge(silu_ready, b * FT + j + 1)
                    s = sg_slot(j)
                    V.tensor_tensor(sg[:, s, :], ps[:, 2 + j % 2, :], sg[:, s, :], ALU.mult).then_inc(gated_ready, 1)

                if new and j in (2, 3):
                    gated()
                m = weighted_tile(j)
                if m is not None and (new if m >= 0 else old):
                    k, s = b * FT + m, sg_slot(m)
                    dve.wait_ge(gated_ready, k + 1)
                    dve.wait_ge(c_ready, k + 1)
                    V.tensor_tensor(sg[:, s, :], ps[:, 6, :], sg[:, s, :], ALU.mult).then_inc(weighted, 1)
                    if old and j == 2:
                        add_half(b - 1, 0)
                    if new and j == FT:
                        split_xnT(b + BATCHES + 1)
                    dve.wait_ge(act_high, k + 1)
                    V.tensor_tensor(moe_act[1][:, m % FT % 2, :], sg[:, s, :], moe_act[0][:, m % FT % 2, :],
                                    ALU.subtract).then_inc(act_ready, 1)
                elif old and j == 2:
                    add_half(b - 1, 0)
                if new and j == 0:
                    route(b, True)
                if new and j < FT and j not in (2, 3):
                    gated()
                if new and j == 1:
                    route(b, False)
                if old and j == 3:
                    add_half(b - 1, 1)

            def split_moe(j):
                dve.wait_ge(moe_high, j + 1)
                V.tensor_tensor(w1moe[1][:, j], w1_in[:, j % 2], w1moe[0][:, j], ALU.subtract)
                V.tensor_tensor(w2moe[1][:, j, :], w2_in[:, j % 2, :], w2moe[0][:, j, :], ALU.subtract
                                ).then_inc(moe_split, 1)

            dve.wait_ge(gate_high, 1)
            V.tensor_tensor(gate[1][:], gate_in, gate[0][:], ALU.subtract).then_inc(gate_split, 1)
            split_moe(0)
            split_moe(1)
            for j in range(FT + 1):
                expert_step(0, j, True, False)
            with dve.Fori(1, BATCHES) as b:
                for j in range(FT + 1):
                    expert_step(b, j, True, True)
            for j in range(4):
                expert_step(BATCHES, j, False, True)
            dve.wait_ge(y_added, BATCHES * TT)

            V.memset(nm1[:], 0.0).then_inc(c_consts_ready, 1)
            dve.wait_ge(c_consts_ready, 1)

            def split_weights(count, w, w_in):
                dve.wait_ge(wc_high, count)
                V.tensor_tensor(w[1][:].rearrange("p c f -> p (c f)"), w_in, w[0][:].rearrange("p c f -> p (c f)"),
                                ALU.subtract).then_inc(wc_split, 1)

            def split_tile(b, tile, which):
                dve.wait_ge(qk1_high, b * 4 + (2 * tile + which + 1))
                V.tensor_tensor(qk1[1][:, tile, which, :], ps[:, which, :], qk1[0][:, tile, which, :], ALU.subtract
                                ).then_inc(qk1_split, 1)

            split_weights(1, wqk1, wqk1_in)

            def stack_queries(b, n, old):
                k = b * PAIRS + n
                dve.wait_ge(picked[0], k + 1)
                if old or n >= 2:
                    dve.wait_ge(qsm_ready, k - 1)
                V.tensor_copy(qst[:, n % 2, :], ps[:, 0, :]).then_inc(q_stacked, 1)

            def pair_step(b, n, new, old):
                kb, kq, i_next = b * PAIRS, b * (PAIRS // 2), b + 2 * BATCHES + 1
                valid = lambda m: new if m >= 0 else old
                for i in range(2 * TT):
                    if valid(n - 1):
                        m = n - 1
                        h, t = i // TT, i % TT
                        dve.wait_ge(s1_ready, (kb + m) * 2 * TT + i + 1)
                        col = 64 * h + MAX_ROW
                        V.tensor_reduce(nm1[:, m % 2, t, col:col + 1], ps[:, 2 + i % 2, :], AX.X, ALU.max,
                                        negate=True).then_inc(s1_max, 1)
                    if i == 0 and valid(n - 2):
                        m = n - 2
                        k = kb + m
                        dve.wait_ge(m_turned, k + 1)
                        if old or m >= 2:
                            dve.wait_ge(st_ready, (k - 1) * 2 * TT)
                        V.tensor_tensor(qsm[:, m % 2, :], ps[:, 7, :], qst[:, m % 2, :], ALU.add
                                        ).then_inc(qsm_ready, 1)
                    if new and n in (4, 6) and i % 2 == 1:
                        (norm_stats if n == 4 else norm_apply)(i_next, (b + 1) % BATCHES, (i // 2,))
                    if n == 0 and new and i in (3, 5):
                        split_tile(b, 0, i // 5)
                    if n >= 1 and i == 3 and new:
                        stack_queries(b, n, old)
                    if i == 5 and n % 2 == 0 and valid((n - 6) // 2):
                        u = (n - 6) // 2
                        c0 = (u % (PAIRS // 2)) * 4 * HD1
                        if u == 0 and old:
                            dve.wait_ge(on_turned, KT * b)
                        dve.wait_ge(o1_turned, kq + u + 1)
                        o4 = ps[:, 7, :].rearrange("p (t h c) -> p t h c", t=TT, h=4)
                        V.reciprocal(oinv[:, u % 2, :, :], o4[:, :, :, HD1]).then_inc(o1_inv, 1)
                        dve.wait_ge(o1_inv, kq + u + 1)
                        V.tensor_tensor(otok[:, :, c0:c0 + 4 * HD1].rearrange("p t (h c) -> p t h c", h=4),
                                        o4[:, :, :, 0:HD1], oinv[:, u % 2, :, :].unsqueeze(3).to_broadcast((P, TT, 4, HD1)),
                                        ALU.mult).then_inc(o1_normed, 1)
                    if old and n == 7 and i in (3, 5):
                        half = i // 5
                        xs = x_res[:, bass.ds((b - 1) * TT + 2 * half, 2), :]
                        dve.wait_ge(out1_ready, 2 * b - 1 + half)
                        V.tensor_tensor(xs, ps[:, 7, :].rearrange("p (t d) -> p t d", t=2), xs, ALU.add
                                        ).then_inc(out1_summed, 1)
                        dve.wait_ge(out1_summed, 2 * b - 1 + half)
                        V.tensor_tensor(xs, xs, bo1[:].unsqueeze(1).to_broadcast((P, 2, D)), ALU.add
                                        ).then_inc(out1_added, 1)
                if n == 0 and new:
                    stack_queries(b, n, old)
                if n == 1 and new:
                    split_tile(b, 1, 0)
                    split_tile(b, 1, 1)
                if new and n in (2, 3):
                    for t in (2 * n - 4, 2 * n - 3):
                        dve.wait_ge(v_ready, b * TT + t + 1)
                        V.tensor_tensor(v1[:, t, :], ps[:, t % 2, :], vones[:], ALU.add).then_inc(v_kept, 1)
                if new and n == PAIRS - 1:
                    split_xnT(i_next)

            flat = [w[:].rearrange("p a f -> p (a f)") for w in (wm1, wm2)]
            tern = [w[:].rearrange("p a f -> p (a f)") for w in (wt1, wt2)]

            def ternary_scales():
                dve.wait_ge(wabs_summed, 1)
                V.tensor_scalar(wscl[:], ps[:, 0, 0:2], 1.0 / (DFF * D), QUANT_EPS, ALU.mult, ALU.max
                                ).then_inc(quant_step, 1)
                dve.wait_ge(quant_step, 4)
                V.tensor_scalar(whalf[:], wscl[:], 0.5, None, ALU.mult).then_inc(quant_step, 1)
                V.tensor_scalar(wmhalf[:], wscl[:], -0.5, None, ALU.mult).then_inc(quant_step, 1)
                dve.wait_ge(quant_step, 6)

            def ternary_weights(i):
                V.tensor_scalar(wneg[:, i, :], flat[i], wmhalf[:, i:i + 1], None, ALU.is_lt).then_inc(quant_step, 1)
                dve.wait_ge(quant_step, 7 + i)
                V.scalar_tensor_tensor(tern[i], flat[i], whalf[:, i:i + 1], wneg[:, i, :], ALU.is_gt, ALU.subtract
                                       ).then_inc(quantized, 1)

            V.memset(ones[:], 1.0).then_inc(quant_step, 1)
            for n in range(PAIRS):
                if n == 0:
                    dve.wait_ge(c_rest_loaded, 4 * 16)
                pair_step(0, n, True, False)
                if n == 0:
                    split_weights(2, wv1, wv1_in)
                if n >= PAIRS - 2:
                    i = n - (PAIRS - 2)
                    dve.wait_ge(wd_loaded, 4 * 16)
                    V.tensor_reduce(wabs[:, i:i + 1], flat[i], AX.X, ALU.add, apply_absolute_value=True
                                    ).then_inc(quant_step, 1)
            with dve.Fori(1, BATCHES) as b:
                for n in range(PAIRS):
                    pair_step(b, n, True, True)
            def mlp_step(b, f, new, old, following):
                i_next = b + 3 * BATCHES + 1
                if following and f == 2:
                    norm_stats(i_next, b + 1)
                if following and f == 4:
                    norm_apply(i_next, b + 1)
                m = hidden_split(f)
                if m is not None and (new if m >= 0 else old):
                    k, s = b * HT + m, m % HT % H_RING
                    dve.wait_ge(h_high, k + 1)
                    V.tensor_tensor(hact2[1][:, s, :], hact[:, s, :], hact2[0][:, s, :], ALU.subtract
                                    ).then_inc(h_split, 1)
                if following and f == HT:
                    split_xnT(i_next)
                if old and f in (2, 3):
                    half, i = f - 2, b + BATCHES - 1
                    dve.wait_ge(y_turned, i * 2 + half + 1)
                    for t in (2 * half, 2 * half + 1):
                        V.tensor_tensor(x_tile(b - 1, t), ps[:, 6 + half, (t % 2) * D:(t % 2 + 1) * D],
                                        x_tile(b - 1, t), ALU.add).then_inc(y_added, 1)

            for n in range(PAIRS):
                pair_step(BATCHES, n, False, True)
                if n == 0:
                    ternary_scales()
                if n in (1, 2):
                    ternary_weights(n - 1)
                for f in MLP_AFTER.get(n, ()):
                    mlp_step(0, f, True, False, True)
            dve.wait_ge(out1_added, 2 * BATCHES)
            with dve.Fori(1, BATCHES - 1) as b:
                for f in range(HT + 1):
                    mlp_step(b, f, True, True, True)
            for f in range(HT + 1):
                mlp_step(BATCHES - 1, f, True, True, False)
            for f in range(4):
                mlp_step(BATCHES, f, False, True, False)

        @block.scalar
        def _(act):
            A = nc.scalar.activation

            def keep_xnT(i):
                for c in range(KT):
                    act.wait_ge(xn_turned, i * KT + c + 2)
                    A(xnT[0][:, c, :], ps[:, c, :], ACT.Copy).then_inc(xnT_high, 1)

            keep_xnT(0)

            def split_wqkv(g):
                act.wait_ge(wqkv_loaded[g], 16)
                A(*(w[:, g].rearrange("p c f -> p (c f)") for w in (wqkv[0], wqkv_in)), ACT.Copy
                  ).then_inc(wqkv_high, 1)

            split_wqkv(0)

            def attention_step(b, n, new, old):
                k0 = b * STEPS
                heads, back = heads_next(n, new, old)

                def split_head(h):
                    act.wait_ge(enc_ready, (b + back) * STEPS + (h // 2 + 1) * TT)
                    if h >= 2:
                        act.wait_ge(head_used, (b + back) * HEADS0 + h - 1)
                    A(enc_parts[0][h % 2][:], encT[:, h, :], ACT.Copy).then_inc(enc_high, 1)
                    A(wo_parts[0][:, h % 2, :], wo0[:, h, :], ACT.Copy).then_inc(wo0_high, 1)

                if new and 7 <= n < STEPS + 7:
                    m = n - 7
                    k, s = k0 + m, m % 2
                    act.wait_ge(prob_turned, k + 1)
                    if m >= 2:
                        act.wait_ge(attended, k - 1)
                    kt = slice(1, 4, 2) if m % TT == 0 else slice(0, 4)
                    A(probT[:, s, kt, :], ps[:, 5, :].rearrange("p (a f) -> p a f", a=4)[:, kt, :], ACT.Copy
                      ).then_inc(probT_ready, 1)
                if new and n == STEPS + 1:
                    keep_xnT(b + 1)
                for h in heads[0:1]:
                    split_head(h)
                if new and n >= 8:
                    m = n - 8
                    g, t = m // TT, m % TT
                    act.wait_ge(attended, k0 + m + 1)
                    A(encT[:, 2 * g:2 * g + 2, t * P:(t + 1) * P],
                      ps[:, 6, 0:2 * P].rearrange("p (h f) -> p h f", h=2), ACT.Copy).then_inc(enc_ready, 1)
                if new and n < STEPS:
                    k, s = k0 + n, n % 2
                    act.wait_ge(projected, k + 1)
                    A(raw[:, n % RAW_RING, :], ps[:, s, :], ACT.Copy).then_inc(raw_kept, 1)
                    if n >= 2:
                        act.wait_ge(rotated, k - 1)
                    A(sq[:, s, :], ps[:, s, 0:3 * P], ACT.Square).then_inc(squared, 1)
                if new and 2 <= n < STEPS + 2:
                    m = n - 2
                    act.wait_ge(qk_turned, k0 + m + 1)
                    A(qkT[:, m % QK_RING, :, :], ps[:, 5 if m < EARLY_TURNS else 2, 0:3 * P].rearrange("p (h f) -> p h f", h=3), ACT.Copy
                      ).then_inc(qkT_ready, 1)
                if new and 4 <= n < STEPS + 4:
                    m = n - 4
                    k, s, w = k0 + m, m % 2, (P if m % TT == 0 else 2 * P)
                    act.wait_ge(max_ready, k + 1)
                    if m >= 2:
                        act.wait_ge(probn_ready, k - 1)
                    if m >= PROB_RING:
                        act.wait_ge(prob_turned, k - PROB_RING + 1)
                    for h in range(2):
                        ins = A(prob[:, m % PROB_RING, h, 0:w], ps[:, 3 + s, h * 2 * P:h * 2 * P + w], ACT.Exp,
                                bias=nmax[:, s, h:h + 1], accum_out=psums[:, s, h:h + 1])
                    ins.then_inc(prob_ready, 1)
                for h in heads[1:2]:
                    split_head(h)
                if old and n == 4:
                    act.wait_ge(out0_summed, b)
                    A(yT[:, 0, :], ps[:, 2, :], ACT.Copy).then_inc(out0_kept, 1)
                    act.wait_ge(head_used, b * HEADS0)
                    A(yT[:, 1, :], ps[:, 7, :], ACT.Copy).then_inc(out0_kept, 1)

            for n in range(STEPS + LAST_LAG):
                if n == LAST_LAG:
                    act.wait_ge(wqkv_split, GROUPS)
                if n == STEPS:
                    act.wait_ge(wo0_loaded, 16)
                attention_step(0, n, True, False)
                if n + 1 < GROUPS:
                    split_wqkv(n + 1)
            with act.Fori(1, BATCHES) as b:
                for n in range(STEPS + LAST_LAG):
                    attention_step(b, n, True, True)
            for n in range(OLD_STEPS):
                attention_step(BATCHES, n, False, True)

            def split_moe(j):
                act.wait_ge(moe_loaded[j % 2], 32 * (j // 2 + 1))
                A(w1moe[0][:, j], w1_in[:, j % 2], ACT.Copy)
                A(w2moe[0][:, j, :], w2_in[:, j % 2, :], ACT.Copy).then_inc(moe_high, 1)

            def expert_step(b, j, new, old):
                if new and isinstance(b, int) and j + 2 < FT:
                    split_moe(j + 2)
                if new and j in (2, 3):
                    silu(b, j, old)
                m = weighted_tile(j)
                if m is not None and (new if m >= 0 else old):
                    k = b * FT + m
                    act.wait_ge(weighted, k + 1)
                    age = 1 if m == 0 else 3 if m == 1 else 2
                    if old or m >= 2:
                        act.wait_ge(y_used, k - age + 1)
                    A(moe_act[0][:, m % FT % 2, :], sg[:, sg_slot(m), :], ACT.Copy).then_inc(act_high, 1)
                if new and j == FT:
                    keep_xnT(b + BATCHES + 1)
                if new and j == 0:
                    act.wait_ge(route_step, b * ROUTE + 4 + 2)
                    A(gexp, lg[:], ACT.Exp).then_inc(gate_exp, 1)
                if new and j < FT and j not in (2, 3):
                    silu(b, j, old)
                if old and j == 1:
                    act.wait_ge(y_used, b * FT)
                    for c in range(KT):
                        A(yT[:, c, :], ps[:, 4 + c, :], ACT.Copy).then_inc(yT_ready, 1)

            def silu(b, j, old):
                k, age = b * FT + j, slot_age(j)
                act.wait_ge(gu_ready, k + 1)
                if old or j >= age:
                    act.wait_ge(act_ready, k - age + 1)
                A(sg[:, sg_slot(j), :], ps[:, j % 2, :], ACT.Silu).then_inc(silu_ready, 1)

            act.wait_ge(gate_loaded, 16)
            A(gate[0][:], gate_in, ACT.Copy).then_inc(gate_high, 1)
            split_moe(0)
            split_moe(1)
            for j in range(FT + 1):
                expert_step(0, j, True, False)
            with act.Fori(1, BATCHES) as b:
                for j in range(FT + 1):
                    expert_step(b, j, True, True)
            expert_step(BATCHES, 0, False, True)
            expert_step(BATCHES, 1, False, True)


            def split_weights(loaded, w, w_in):
                act.wait_ge(loaded, 16)
                A(w[0][:].rearrange("p c f -> p (c f)"), w_in, ACT.Copy).then_inc(wc_high, 1)

            def split_tile(b, tile, which):
                act.wait_ge(qk1_ready, b * 4 + (2 * tile + which + 1))
                A(qk1[0][:, tile, which, :], ps[:, which, :], ACT.Copy).then_inc(qk1_high, 1)

            def stack_keys(b, n, old):
                k = b * PAIRS + n
                act.wait_ge(picked[1], k + 1)
                if old or n >= 4:
                    act.wait_ge(st_ready, (k - 3) * 2 * TT)
                A(kst[:, n % 4, :], ps[:, 1, :], ACT.Identity, bias=stack[:, 0:1]).then_inc(k_stacked, 1)

            split_weights(wqk1_loaded, wqk1, wqk1_in)
            act.wait_ge(pick_loaded, 16)
            A(pick[:].rearrange("p t w r f -> p (t w r f)"), pick_in, ACT.Copy).then_inc(pick_ready, 1)

            def pair_step(b, n, new, old):
                kb, kq = b * PAIRS, b * (PAIRS // 2)
                valid = lambda m: new if m >= 0 else old
                for i in range(2 * TT):
                    if valid(n - 2):
                        m = n - 2
                        h, c, u = i // TT, i % TT, m // 2
                        if i == 0 and (old or m >= 4):
                            act.wait_ge(o1_ready, kq + u - 1)
                        act.wait_ge(st_ready, (kb + m) * 2 * TT + i + 1)
                        A(pT1[:, u % 2, 2 * (m % 2) + h, c, :], ps[:, 4 + i % 2, :], ACT.Exp, scale=SCALE1
                          ).then_inc(p1_ready, 1)
                    if new and n == PAIRS - 1 and i == 2 * TT - 2:
                        keep_xnT(b + 2 * BATCHES + 1)
                    if n == 0 and new and i in (1, 3):
                        split_tile(b, 0, i // 3)
                    if n >= 1 and i == 2 and new:
                        stack_keys(b, n, old)
                    if old and n == 5 and i in (3, 6):
                        c = i // 6
                        act.wait_ge(on_turned, KT * b - 1 + c)
                        A(oTn[:, c, :], ps[:, 7, :], ACT.Copy).then_inc(oTn_ready, 1)
                if n == 0 and new:
                    stack_keys(b, n, old)
                if n == 1 and new:
                    split_tile(b, 1, 0)
                    split_tile(b, 1, 1)
                if n % 2 == 1 and valid((n - 5) // 2):
                    u = (n - 5) // 2
                    act.wait_ge(o1_ready, kq + u + 1)
                    if old or u >= 2:
                        act.wait_ge(o1_turned, kq + u - 1)
                    A(oT1[:, u % 2, :], ps[:, 6, :], ACT.Copy).then_inc(oT1_kept, 1)

            act.wait_ge(c_rest_loaded, 4 * 16)
            for n in range(PAIRS):
                if n == 4:
                    act.wait_ge(wc_split, 2)
                pair_step(0, n, True, False)
                if n == 0:
                    split_weights(wv1_loaded, wv1, wv1_in)
            with act.Fori(1, BATCHES) as b:
                for n in range(PAIRS):
                    pair_step(b, n, True, True)
            act.wait_ge(wd_loaded, 4 * 16)

            def mlp_step(b, f, new, old, following):
                if new and f < HT:
                    k, s, age = b * HT + f, f % H_RING, hidden_age(f)
                    act.wait_ge(h_ready, k + 1)
                    if old or f >= age:
                        act.wait_ge(h_split, k - age + 1)
                    A(hact[:, s, :], ps[:, 2 + f % 2, :], ACT.Gelu, bias=b1m[:, f:f + 1]).then_inc(h_act, 1)
                    act.wait_ge(h_act, k + 1)
                    if old or f >= age:
                        act.wait_ge(h_used, k - age + 1)
                    A(hact2[0][:, s, :], hact[:, s, :], ACT.Copy).then_inc(h_high, 1)
                if following and f == HT:
                    keep_xnT(b + 3 * BATCHES + 1)
                if old and f == 0:
                    act.wait_ge(h_used, b * HT)
                    for c in range(KT):
                        A(yT[:, c, :], ps[:, 4 + c, :], ACT.Identity, bias=b2m[:, c:c + 1]).then_inc(yT_ready, 1)

            for n in range(PAIRS):
                if n < 6:
                    pair_step(BATCHES, n, False, True)
                for f in MLP_AFTER.get(n, ()):
                    mlp_step(0, f, True, False, True)
            with act.Fori(1, BATCHES - 1) as b:
                for f in range(HT + 1):
                    mlp_step(b, f, True, True, True)
            for f in range(HT + 1):
                mlp_step(BATCHES - 1, f, True, True, False)
            mlp_step(BATCHES, 0, False, True, False)

        @block.tensor
        def _(pe):
            MM, T = nc.tensor.matmul, nc.tensor.transpose

            def split_product(out, left, right, first, last):
                MM(out, left[0], right[1], start=first, stop=False)
                MM(out, left[1], right[0], start=False, stop=False)
                return MM(out, left[0], right[0], start=False, stop=last)

            def turn_xn(i):
                pe.wait_ge(xn_ready, i * TT + TT)
                for c in range(KT):
                    for t in range(TT):
                        ins = T(ps[:, c, t * P:(t + 1) * P], xn[:, t, c * P:(c + 1) * P], ident[:])
                    ins.then_inc(xn_turned, 1)

            pe.wait_ge(consts_loaded, 16)
            pe.wait_ge(masks_loaded, 32)
            turn_xn(0)

            def attention_step(b, n, new, old):
                k0 = b * STEPS
                heads, back = (OLD_HEADS_AT.get(n, ()), -1) if old else ((), 0)
                if new and n in HEADS_AT:
                    heads, back = HEADS_AT[n], 0

                def project_head(h):
                    u, s = (b + back) * HEADS0 + h, h % 2
                    pe.wait_ge(enc_split, u + 1)
                    pe.wait_ge(wo0_split, u + 1)
                    if h == 0:
                        pe.wait_ge(qkT_ready, k0 + STEPS)
                        if old:
                            pe.wait_ge(out0_added, b * TT)
                    for c in range(KT):
                        ins = split_product(ps[:, (2, 7)[c], :], [w[:, s, c * P:(c + 1) * P] for w in wo_parts],
                                            [e[s][:] for e in enc_parts], h == 0, h == HEADS0 - 1)
                        if c == 0 and h == HEADS0 - 1:
                            ins.then_inc(out0_summed, 1)
                    ins.then_inc(head_used, 1)

                if new and n == 0:
                    pe.wait_ge(xnT_ready, b * KT + KT)
                if new and n >= 8:
                    m = n - 8
                    k, s, t = k0 + m, m % 2, m % TT
                    pe.wait_ge(probT_ready, k + 1)
                    if m >= 1:
                        pe.wait_ge(enc_ready, k)
                    elif old:
                        pe.wait_ge(out0_added, b * TT - 2)
                    parts = (1,) if t == 0 else (0, 1)
                    for part in parts:
                        ins = MM(ps[:, 6, 0:2 * P], raw[:, (m - 1 + part) % RAW_RING, 3 * P:4 * P],
                                 probT[:, s, part::2, :], start=part == parts[0], stop=part == 1)
                    ins.then_inc(attended, 1)
                if new and n < STEPS:
                    k, g, t = k0 + n, n // TT, n % TT
                    if not old and n % TT == 0:
                        pe.wait_ge(wqkv_split, g + 1)
                    if n >= 2:
                        pe.wait_ge(squared, k - 1)
                    for c in range(KT):
                        ins = split_product(ps[:, n % 2, :], [x[:, c, t * P:(t + 1) * P] for x in xnT],
                                            [w[:, g, c, :] for w in wqkv], c == 0, c == KT - 1)
                    ins.then_inc(projected, 1)
                if new and n == STEPS:
                    pe.wait_ge(squared, k0 + STEPS)
                    turn_xn(b + 1)
                if new and 2 <= n < STEPS + 2:
                    m = n - 2
                    k = k0 + m
                    pe.wait_ge(qk_normed, k + 1)
                    if m >= 1:
                        pe.wait_ge(qkT_ready, k)
                    if m == EARLY_TURNS and old:
                        pe.wait_ge(out0_kept, b * KT - 1)
                    for h in range(3):
                        ins = T(ps[:, 5 if m < EARLY_TURNS else 2, h * P:(h + 1) * P], qkn[:, m % 2, h * P:(h + 1) * P], ident[:])
                    ins.then_inc(qk_turned, 1)
                if new and 3 <= n < STEPS + 3:
                    m = n - 3
                    k, s, t = k0 + m, m % 2, m % TT
                    pe.wait_ge(qkT_ready, k + 1)
                    if m >= 2:
                        pe.wait_ge(prob_ready, k - 1)
                    bank = ps[:, 3 + s, :].rearrange("p (h f) -> p h f", h=2)
                    if t == 0:
                        MM(bank[:, :, 0:P], ident_b[:], window[:, :, 1, :], start=True, stop=False,
                           skip_group_check=True)
                    else:
                        MM(ps[:, 3 + s, :], ident_b[:], window[:].rearrange("p h a f -> p (h a f)"),
                           start=True, stop=False, skip_group_check=True)
                    for h in range(2):
                        for part in ((1,) if t == 0 else (0, 1)):
                            at = 0 if t == 0 else part * P
                            ins = MM(bank[:, h, at:at + P], qkT[:, m % QK_RING, h, :],
                                     qkT[:, (m - 1 + part) % QK_RING, 2, :], start=False,
                                     stop=h == 1 and part == 1, skip_group_check=True)
                    ins.then_inc(scored, 1)
                for h in heads[0:1]:
                    project_head(h)
                if new and 6 <= n < STEPS + 6:
                    m = n - 6
                    k, s, t = k0 + m, m % 2, m % TT
                    pe.wait_ge(probn_ready, k + 1)
                    if m >= 1:
                        pe.wait_ge(probT_ready, k)
                    for h in range(2):
                        for part in ((1,) if t == 0 else (0, 1)):
                            at = 0 if t == 0 else part * P
                            ins = T(ps[:, 5, (2 * h + part) * P:(2 * h + part + 1) * P],
                                    prob[:, m % PROB_RING, h, at:at + P], ident[:])
                    ins.then_inc(prob_turned, 1)
                for h in heads[1:2]:
                    project_head(h)
                if old and n in (6, 7):
                    half = n - 6
                    pe.wait_ge(out0_kept, b * KT)
                    for t in (2 * half, 2 * half + 1):
                        for c in range(KT):
                            ins = T(ps[:, 6 + half, (t % 2) * D + c * P:(t % 2) * D + (c + 1) * P],
                                    yT[:, c, t * P:(t + 1) * P], ident[:])
                    ins.then_inc(out0_ready, 1)

            for n in range(STEPS + LAST_LAG):
                attention_step(0, n, True, False)
            with pe.Fori(1, BATCHES) as b:
                for n in range(STEPS + LAST_LAG):
                    attention_step(b, n, True, True)
            for n in range(OLD_STEPS):
                attention_step(BATCHES, n, False, True)
            pe.wait_ge(out0_added, BATCHES * TT)

            def turn_half(b, half):
                for t in (2 * half, 2 * half + 1):
                    for c in range(KT):
                        ins = T(ps[:, 7, (t % 2) * D + c * P:(t % 2) * D + (c + 1) * P],
                                yT[:, c, t * P:(t + 1) * P], ident[:])
                ins.then_inc(y_turned, 1)

            def expert_step(b, j, new, old):
                k = b * FT + j

                def combine(m):
                    if old or m >= 1:
                        pe.wait_ge(weighted, b * FT + m)
                    MM(ps[:, 6, :], sel[:, m % FT, :], cpieces[:], start=True, stop=True).then_inc(c_ready, 1)

                def down(m):
                    pe.wait_ge(act_ready, b * FT + m + 1)
                    if old and m == 0:
                        pe.wait_ge(yT_ready, b * KT)
                    for c in range(KT):
                        ins = split_product(ps[:, 4 + c, :], [w[:, m % FT, c * P:(c + 1) * P] for w in w2moe],
                                            [a[:, m % FT % 2, :] for a in moe_act], m % FT == 0, m % FT == FT - 1)
                    ins.then_inc(y_used, 1)

                mc, my = weighted_tile(j), summed_tile(j)
                if mc is not None and (j not in (2, 3) or not new) and (new if mc >= 0 else old):
                    combine(mc)
                if new and j == FT:
                    pe.wait_ge(gated_ready, b * FT + FT)
                    turn_xn(b + BATCHES + 1)
                if my is not None and j in (0, FT) and (new if my >= 0 else old):
                    down(my)
                if new and j == 0:
                    pe.wait_ge(xnT_ready, (b + BATCHES) * KT + KT)
                    for t in range(TT):
                        for c in range(KT):
                            ins = split_product(ps[:, 7, t * EXPERTS:(t + 1) * EXPERTS],
                                                [x[:, c, t * P:(t + 1) * P] for x in xnT],
                                                [w[:, c, :] for w in gate], c == 0, c == KT - 1)
                    ins.then_inc(logits_ready, 1)
                if new and j < FT:
                    if isinstance(b, int):
                        pe.wait_ge(moe_split, j + 1)
                    if j >= 2:
                        pe.wait_ge(gated_ready, k - 1)
                    for half in range(2):
                        for c in range(KT):
                            ins = split_product(ps[:, 2 * half + j % 2, :], [w[:, j, c, half, :] for w in w1moe],
                                                [x[:, c, :] for x in xnT], c == 0, c == KT - 1)
                    ins.then_inc(gu_ready, 1)
                if new and j == 1:
                    pe.wait_ge(route_step, b * ROUTE + (4 + ROUTED))
                    for t in range(TT):
                        ins = T(ps[0:PIECE, 7, t * P:(t + 1) * P], comb[:, t, :], ident[:])
                    ins.then_inc(comb_turned, 1)
                if new and j == 2:
                    pe.wait_ge(route_step, b * ROUTE + (4 + ROUTE))
                    pe.wait_ge(sel_loaded, 16)
                    combine(0)
                if new and j == 3:
                    combine(1)
                if my is not None and 0 < j < FT and (new if my >= 0 else old):
                    down(my)
                if old and j == 2:
                    pe.wait_ge(yT_ready, b * KT)
                    turn_half(b - 1, 0)
                if old and j == 3:
                    pe.wait_ge(y_added, (b - 1) * TT + 2)
                    turn_half(b - 1, 1)
                if old and new and j == 5:
                    pe.wait_ge(y_added, b * TT)

            pe.wait_ge(gate_split, 1)
            for j in range(FT + 1):
                expert_step(0, j, True, False)
            with pe.Fori(1, BATCHES) as b:
                for j in range(FT + 1):
                    expert_step(b, j, True, True)
            for j in range(4):
                expert_step(BATCHES, j, False, True)
            pe.wait_ge(y_added, BATCHES * TT)

            pe.wait_ge(c_consts_ready, 1)

            def project_tile(b, tile, which, chunks):
                at = which * D + tile * P
                for c in chunks:
                    ins = split_product(ps[:, which, :], [w[:, c, at:at + P] for w in wqk1],
                                        [x[:, c, :] for x in xnT], c == 0, c == KT - 1)
                if KT - 1 in chunks:
                    ins.then_inc(qk1_ready, 1)

            def pair_step(b, n, new, old):
                kb, kq = b * PAIRS, b * (PAIRS // 2)
                valid = lambda m: new if m >= 0 else old
                for i in range(2 * TT + 2):
                    if new and n == PAIRS - 1 and i == 2 * TT:
                        pe.wait_ge(q_stacked, kb + PAIRS)
                        pe.wait_ge(k_stacked, kb + PAIRS)
                        turn_xn(b + 2 * BATCHES + 1)
                    if valid(n - 1) and i < 2 * TT:
                        m = n - 1
                        k = kb + m
                        h, t = i // TT, i % TT
                        rows = slice(64 * h, 64 * h + 64)
                        if i == 0:
                            pe.wait_ge(q_stacked, k + 1)
                            pe.wait_ge(k_stacked, k + 1)
                        if old or m >= 1 or i >= 2:
                            pe.wait_ge(s1_max, k * 2 * TT + i - 1)
                        MM(ps[:, 2 + i % 2, :], qst[rows, m % 2, t * P:(t + 1) * P], kst[rows, m % 4, :],
                           start=True, stop=True).then_inc(s1_ready, 1)
                    if old and n == 5 and i in (3, 7):
                        c = i // 7
                        pe.wait_ge(o1_normed, kq)
                        if new:
                            pe.wait_ge(qsm_ready, kb + n - 1)
                        if c == 1:
                            pe.wait_ge(oTn_ready, KT * b - 1)
                        for t in range(TT):
                            ins = T(ps[:, 7, t * P:(t + 1) * P], otok[:, t, c * P:(c + 1) * P], ident[:])
                        ins.then_inc(on_turned, 1)
                    if i == 0 and valid(n - 2):
                        m = n - 2
                        k = kb + m
                        pe.wait_ge(s1_max, (k + 1) * 2 * TT)
                        if old or m >= 1:
                            pe.wait_ge(qsm_ready, k)
                        if n % 2 == 1 and valid((n - 7) // 2):
                            pe.wait_ge(o1_normed, kq + (n - 7) // 2 + 1)
                        if old and n == 6:
                            pe.wait_ge(oTn_ready, KT * b)
                        for t in range(TT):
                            ins = T(ps[:, 7, t * P:(t + 1) * P], nm1[:, m % 2, t, :], ident[:])
                        ins.then_inc(m_turned, 1)
                    if new and n == 0 and 1 <= i <= 2 * KT:
                        if i == 1:
                            pe.wait_ge(xnT_ready, (b + 2 * BATCHES) * KT + KT)
                            if not old:
                                pe.wait_ge(wc_split, 1)
                        project_tile(b, 0, (i - 1) // KT, ((i - 1) % KT,))
                    if new and (i < 2 if n else i == 2 * TT + 1):
                        k = kb + n
                        for which in ((i,) if n else (0, 1)):
                            if which == 0 and n in (0, 2):
                                pe.wait_ge(qk1_split, b * 4 + n + 2)
                            if n == 0 and not old:
                                pe.wait_ge(pick_ready, 1)
                            if n >= 1:
                                pe.wait_ge((q_stacked, k_stacked)[which], k)
                            if n in (3, 4):
                                pe.wait_ge(v_kept, b * TT + 2 * n - 5 + which)
                            for part in range(2):
                                ins = MM(ps[:, which, :], pick[:, n % PAIRS_T, which, part, :],
                                         qk1[part][:, n // PAIRS_T, which, :], start=part == 0, stop=part == 1)
                            ins.then_inc(picked[which], 1)
                    if valid(n - 2) and i >= 2:
                        m, e = n - 2, i - 2
                        k = kb + m
                        h, t = e // TT, e % TT
                        rows = slice(64 * h, 64 * h + 64)
                        if e == 0:
                            pe.wait_ge(qsm_ready, k + 1)
                        if old or m >= 1 or e >= 2:
                            pe.wait_ge(p1_ready, k * 2 * TT + e - 1)
                        MM(ps[:, 4 + e % 2, :], kst[rows, m % 4, t * P:(t + 1) * P], qsm[rows, m % 2, :],
                           start=True, stop=True).then_inc(st_ready, 1)
                    if valid(n // 2 - 2) and i in (5, 7):
                        u, c = n // 2 - 2, n % 2 * 2 + i // 7
                        if c == 0:
                            pe.wait_ge(p1_ready, (kb + 2 * u + 2) * 2 * TT)
                            if old or u >= 1:
                                pe.wait_ge(oT1_kept, kq + u)
                        for h in range(4):
                            col = (4 * (u % (PAIRS // 2)) + h) * VW
                            ins = MM(ps[VW * h:VW * (h + 1), 6, :], v1[:, c, col:col + VW],
                                     pT1[:, u % 2, h, c, :], start=c == 0, stop=c == TT - 1,
                                     tile_position=(0, VW * h), skip_group_check=True)
                        if c == TT - 1:
                            ins.then_inc(o1_ready, 1)
                    if n % 2 == 0 and valid((n - 6) // 2) and i == 3:
                        u = (n - 6) // 2
                        pe.wait_ge(oT1_kept, kq + u + 1)
                        if valid(n - 2):
                            pe.wait_ge(qsm_ready, kb + n - 1)
                        else:
                            pe.wait_ge(o1_normed, kq + u)
                        for t in range(TT):
                            ins = T(ps[:, 7, t * P:(t + 1) * P], oT1[:, u % 2, t * P:(t + 1) * P], ident[:])
                        ins.then_inc(o1_turned, 1)
                    if old and n == 7 and i in (2, 5):
                        half = i // 5
                        pe.wait_ge(oTn_ready, KT * b)
                        if half == 1:
                            pe.wait_ge(out1_summed, 2 * b - 1)
                        elif new:
                            pe.wait_ge(qsm_ready, kb + n - 1)
                        for t in (2 * half, 2 * half + 1):
                            for c in range(KT):
                                ins = MM(ps[:, 7, (t % 2) * D:(t % 2 + 1) * D],
                                         oTn[:, c, t * P:(t + 1) * P], wo1[:, c, :], start=c == 0, stop=c == KT - 1)
                        ins.then_inc(out1_ready, 1)
                if new and n in (1, 2, 3):
                    pe.wait_ge(q_stacked, kb + n + 1)
                    pe.wait_ge(k_stacked, kb + n + 1)
                if new and n == 1:
                    for which in range(2):
                        project_tile(b, 1, which, range(KT))
                if new and n in (2, 3):
                    if n == 2:
                        pe.wait_ge(c_rest_loaded, 4 * 16)
                        pe.wait_ge(wc_split, 2)
                    for t in (2 * n - 4, 2 * n - 3):
                        for c in range(KT):
                            ins = split_product(ps[:, t % 2, :], [x[:, c, t * P:(t + 1) * P] for x in xnT],
                                                [w[:, c, :] for w in wv1], c == 0, c == KT - 1)
                        ins.then_inc(v_ready, 1)
                if old and n == PAIRS - 1:
                    pe.wait_ge(out1_summed, 2 * b)

            for n in range(PAIRS):
                pair_step(0, n, True, False)
            with pe.Fori(1, BATCHES) as b:
                for n in range(PAIRS):
                    pair_step(b, n, True, True)
            def mlp_step(b, f, new, old, following):
                def down(m):
                    pe.wait_ge(h_split, b * HT + m + 1)
                    if old and m == 0:
                        pe.wait_ge(yT_ready, (b + BATCHES) * KT)
                    for c in range(KT):
                        for part in (1, 0):
                            ins = MM(ps[:, 4 + c, :], wt2[:, m % HT, c * P:(c + 1) * P],
                                     hact2[part][:, m % HT % H_RING, :], start=m % HT == 0 and part == 1,
                                     stop=m % HT == HT - 1 and part == 0)
                    ins.then_inc(h_used, 1)

                m = hidden_used(f)
                if following and f == HT:
                    turn_xn(b + 3 * BATCHES + 1)
                if f in (0, HT) and (new if m >= 0 else old):
                    down(m)
                if new and f < HT:
                    k = b * HT + f
                    if f == 0:
                        pe.wait_ge(xnT_ready, (b + 3 * BATCHES) * KT + KT)
                    if old or f >= 2:
                        pe.wait_ge(h_act, k - 1)
                    for c in range(KT):
                        for part in (1, 0):
                            ins = MM(ps[:, 2 + f % 2, :], wt1[:, c, f * P:(f + 1) * P], xnT[part][:, c, :],
                                     start=c == 0 and part == 1, stop=c == KT - 1 and part == 0)
                    ins.then_inc(h_ready, 1)
                if new and m is not None and 0 < f < HT:
                    down(m)
                if old and f in (2, 3):
                    half, i = f - 2, b + BATCHES - 1
                    pe.wait_ge(yT_ready, i * KT + KT)
                    for t in (2 * half, 2 * half + 1):
                        for c in range(KT):
                            ins = T(ps[:, 6 + half, (t % 2) * D + c * P:(t % 2) * D + (c + 1) * P],
                                    yT[:, c, t * P:(t + 1) * P], ident[:])
                    ins.then_inc(y_turned, 1)

            for n in range(PAIRS):
                pair_step(BATCHES, n, False, True)
                if n == 0:
                    pe.wait_ge(quant_step, 3)
                    pe.wait_ge(xnT_ready, 3 * BATCHES * KT + KT)
                    MM(ps[:, 0, 0:2], ones[:], wabs[:], start=True, stop=True).then_inc(wabs_summed, 1)
                for f in MLP_AFTER.get(n, ()):
                    if f == 0:
                        pe.wait_ge(quantized, 2)
                    mlp_step(0, f, True, False, True)
            with pe.Fori(1, BATCHES - 1) as b:
                for f in range(HT + 1):
                    mlp_step(b, f, True, True, True)
            for f in range(HT + 1):
                mlp_step(BATCHES - 1, f, True, True, False)
            for f in (0, 2, 3):
                mlp_step(BATCHES, f, False, True, False)


def kernel(**inputs):
    import numpy as np
    import concourse.bacc as bacc
    from concourse.bass_utils import run_bass_kernel_spmd as run

    def tiles(a, k):
        return np.ascontiguousarray(a.reshape(k, P, -1).transpose(1, 0, 2))

    g = {k: np.asarray(v) for k, v in inputs.items()}
    arrays = {"x": g["L0_attn_x"], "qs": g["L0_attn_q_norm_scale"], "ks": g["L0_attn_k_norm_scale"]}

    q, kv = g["L0_attn_q_kernel"], g["L0_attn_kv_kernel"]
    w = np.zeros((P, GROUPS, KT, 4, P), np.float32)
    for grp in range(GROUPS):
        for i, head in enumerate((q[2 * grp], q[2 * grp + 1], kv[0, grp], kv[1, grp])):
            w[:, grp, :, i, :] = tiles(head, KT)
    arrays["wqkv"] = w.reshape(P, GROUPS, KT, 4 * P)
    arrays["wo0"] = np.ascontiguousarray(g["L0_attn_out_kernel"].transpose(1, 0, 2))

    w1, w2 = g["L0_ffn_w1"], g["L0_ffn_w2"]
    s1, s2 = g["L0_ffn_shared_w1"], g["L0_ffn_shared_w2"]
    up = np.zeros((2, FT * P, D), np.float32)
    down = np.zeros((FT * P, D), np.float32)
    for half in range(2):
        up[half, 0:EXPERTS * INTER] = w1[:, half * INTER:(half + 1) * INTER, :].reshape(-1, D)
        up[half, EXPERTS * INTER:FEATS] = s1[half * SHARED:(half + 1) * SHARED]
    down[0:EXPERTS * INTER] = w2.transpose(0, 2, 1).reshape(-1, D)
    down[EXPERTS * INTER:FEATS] = s2.T
    arrays["w1moe"] = np.ascontiguousarray(up.reshape(2, FT, P, KT, P).transpose(4, 1, 3, 0, 2))
    arrays["w2moe"] = tiles(down, FT)
    arrays["gate"] = tiles(g["L0_ffn_gate_w"].T, KT)

    arrays["wqk1"] = tiles(np.concatenate([g["L1_attn_Wq"], g["L1_attn_Wk"]], 1), KT).reshape(P, -1)
    w = np.zeros((D, HEADS1, VW), np.float32)
    w[:, :, 0:HD1] = g["L1_attn_Wv"].reshape(D, HEADS1, HD1)
    arrays["wv1"] = tiles(w.reshape(D, -1), KT).reshape(P, -1)
    arrays["wo1"] = tiles(g["L1_attn_Wo"], KT)
    arrays["bo1"] = g["L1_attn_bo"]
    arrays["wm1"] = tiles(g["L1_ffn_w1"].T, KT)
    arrays["wm2"] = tiles(g["L1_ffn_w2"].T, HT)
    arrays["b1m"] = np.ascontiguousarray(g["L1_ffn_b1"].reshape(HT, P).T)
    arrays["b2m"] = np.ascontiguousarray(g["L1_ffn_b2"].reshape(KT, P).T)

    arrays["c_ident"] = np.eye(P, dtype=np.float32)
    frac = np.arange(0, HD0, 2, dtype=np.float32) / np.float32(HD0)
    angle = np.arange(SEQ, dtype=np.float32)[:, None] / np.float32(10000.0) ** frac
    cos, sin = np.cos(angle), np.sin(angle)
    arrays["c_cos"] = tiles(np.concatenate([cos, cos], 1), TT)
    arrays["c_sin"] = tiles(np.concatenate([-sin, sin], 1), TT)
    qi, kj = np.arange(P)[:, None], np.arange(P)[None, :]
    masks = np.where(np.stack([kj > qi, kj <= qi], 1), np.float32(0), np.float32(-1e30))
    arrays["c_window"] = np.ascontiguousarray(np.broadcast_to(masks[:, None], (P, 2, 2, P)))
    feat = np.arange(FT * P)
    owner = np.where(feat < EXPERTS * INTER, feat // INTER, EXPERTS)
    sel = np.zeros((3, PIECE, FT * P), np.float32)
    sel[:, owner[feat < FEATS], feat[feat < FEATS]] = 1.0
    arrays["c_sel"] = sel.reshape(3 * PIECE, FT, P)
    vones = np.zeros((P, HEADS1, VW), np.float32)
    vones[:, :, HD1] = 1.0
    arrays["c_vones"] = vones.reshape(P, -1)
    stack = np.zeros((2, 64, 4), np.float32)
    stack[:, MAX_ROW, 0] = 1.0
    arrays["c_stack"] = stack.reshape(P, 4)
    pick = np.zeros((PAIRS_T, 2, HD1, PAIRS_T, 2, 2, 2, 4, HD1), np.float32)
    for pair in range(PAIRS_T):
        for head in range(2):
            for which, parts in enumerate(((0, 0, 1), (0, 1, 0))):
                for copy, part in enumerate(parts):
                    pick[pair, head, :, pair, which, part, head, copy, :] = np.eye(HD1, dtype=np.float32)
    arrays["c_pick"] = pick.reshape(P, -1)

    nc = bacc.Bacc("TRN2", target_bir_lowering=False, num_devices=1)
    feeds, dram = {}, {}
    for name, a in arrays.items():
        a = np.ascontiguousarray(a)
        feeds[f"in_{name}"] = a
        dram[name] = nc.dram_tensor(f"in_{name}", a.shape, mybir.dt.from_np(a.dtype), kind="ExternalInput").ap()
    out = nc.dram_tensor("out_x", (BATCHES, SEQ, D), F32, kind="ExternalOutput").ap()
    build(nc, dram, out)
    result = run(nc, [feeds], core_ids=[0])
    return result.results[0]["out_x"]
```
